# Optimizing a Trainium2 kernel written in Bass

```python
import numpy as np
import jax
import jax.numpy as jnp

def _softmax(x, axis=-1):
    return jax.nn.softmax(x, axis=axis)

def _gelu(x):
    return jax.nn.gelu(x, approximate=True)

def _silu(x):
    return jax.nn.silu(x)

def _sigmoid(x):
    return jax.nn.sigmoid(x)

def _layernorm(x, axis=-1, eps=1e-05):
    m = jnp.mean(x, axis=axis, keepdims=True)
    v = jnp.var(x, axis=axis, keepdims=True)
    return (x - m) / jnp.sqrt(v + eps)

def _scatter_add(tgt, idx, src, axis=0):
    return tgt.at[idx].add(src)

def _segment_sum(src, seg, n):
    return jax.ops.segment_sum(src, seg, n)
kernel_name = 'mk_flamingo_gated_d4_seqx_r4_5fc337'

def setup_inputs(seed: int=0):
    np.random.seed(seed)
    _w = jnp.asarray

    def _rec_inputs():
        import jax
        import jax.numpy as jnp
        _rk = jax.random.key(seed)
        x = -7.109e-05 + 0.9999 * jax.random.normal(jax.random.fold_in(_rk, 1), (4, 512, 512), jnp.float32)
        _lenS = 512 - jax.random.randint(jax.random.fold_in(_rk, 7), (4,), 0, max(1, 512 // 4) + 1, jnp.int32)
        _lenS2 = 512 - jax.random.randint(jax.random.fold_in(_rk, 8), (4,), 0, max(1, 512 // 4) + 1, jnp.int32)
        _ctx_512P = jax.random.normal(jax.random.fold_in(_rk, 11), (4, 16, 128), jnp.float32)
        _ctx_512c = jax.random.dirichlet(jax.random.fold_in(_rk, 511), 0.3 * jnp.ones((16,), jnp.float32), (4, 512))
        _ctx_512t = jnp.einsum('bsk,bkd->bsd', _ctx_512c, _ctx_512P)
        _ctx_512t = _ctx_512t * jax.lax.rsqrt(jnp.mean(jnp.square(_ctx_512t)) + 1e-12) * 0.953939
        ctx_512 = 2.81802e-05 + 1.00001 * (_ctx_512t + 0.3 * jax.random.normal(jax.random.fold_in(_rk, 611), (4, 512, 128), jnp.float32))
        _g = jax.random.normal(jax.random.fold_in(_rk, 9001), (2, 4), jnp.float32)
        _g = jnp.sign(_g) * jnp.maximum(jnp.abs(_g), 1.0) + (_g == 0) * 1.0
        g_xattn = _g[0]
        g_ffn = _g[1]
        return (x, ctx_512, g_xattn, g_ffn)
    x, ctx_512, g_xattn, g_ffn = _rec_inputs()

    def _L0_xattn_setup():
        import jax, jax.numpy as jnp
        import numpy as np
        EPS = 1e-06
        IMAGE_DIMS = 512
        key = jax.random.key(seed)
        k1, k2, k3 = jax.random.split(key, 3)
        B, I, J, D = (16, 512, 512, 128)
        p = jax.random.normal(k1, (B, I, J), dtype=jnp.float32)
        k_v = jax.random.normal(k2, (B, J, D), dtype=jnp.float32)
        W_k = jax.random.normal(k3, (D, D), dtype=jnp.float32) * (1.0 / np.sqrt(D))
        b_k = jnp.zeros((D,), dtype=jnp.float32)
        ln_gamma = jnp.ones((J,), dtype=jnp.float32)
        ln_beta = jnp.zeros((J,), dtype=jnp.float32)
        return {'p': p, 'k_v': k_v, 'W_k': W_k, 'b_k': b_k, 'ln_gamma': ln_gamma, 'ln_beta': ln_beta}
    _L0_xattn_all = _L0_xattn_setup()
    _L0_xattn_in = {k: v for k, v in _L0_xattn_all.items() if k in ('W_k', 'b_k', 'ln_gamma', 'ln_beta')}
    del _L0_xattn_all

    def _L0_ffn_setup():
        import jax, jax.numpy as jnp
        import numpy as np
        TARGET_SPARSITY = 0.9
        LN_EPS = 1e-05

        def ternary_quant(W):
            scale = jnp.mean(jnp.abs(W))
            q = jnp.clip(jnp.round(W / (scale + 1e-08)), -1.0, 1.0) * scale
            return W + jax.lax.stop_gradient(q - W)

        def layernorm(x, gamma, beta):
            mu = jnp.mean(x, axis=-1, keepdims=True)
            var = jnp.var(x, axis=-1, keepdims=True)
            return (x - mu) * jax.lax.rsqrt(var + LN_EPS) * gamma + beta
        key = jax.random.key(seed)
        ks = jax.random.split(key, 3)
        B, S, D, N = (4, 512, 512, 2048)
        x = jax.random.normal(ks[0], (B, S, D), dtype=jnp.float32)
        W_syn = jax.random.normal(ks[1], (N, D), dtype=jnp.float32) * (1.0 / np.sqrt(D))
        b_syn = jnp.zeros((N,), dtype=jnp.float32)
        W_out = jax.random.normal(ks[2], (D, N), dtype=jnp.float32) * (1.0 / np.sqrt(N))
        b_out = jnp.zeros((D,), dtype=jnp.float32)
        gamma = jnp.ones((D,), dtype=jnp.float32)
        beta = jnp.zeros((D,), dtype=jnp.float32)
        return {'x': x, 'W_syn': W_syn, 'b_syn': b_syn, 'W_out': W_out, 'b_out': b_out, 'gamma': gamma, 'beta': beta}
    _L0_ffn_all = _L0_ffn_setup()
    _L0_ffn_in = {k: v for k, v in _L0_ffn_all.items() if k in ('W_syn', 'b_syn', 'W_out', 'b_out', 'gamma', 'beta')}
    del _L0_ffn_all

    def _L1_xattn_setup():
        import jax, jax.numpy as jnp
        import numpy as np
        B, N, D = (16, 512, 128)
        H = 4
        TOP_K_RATIO = 0.3
        key = jax.random.key(seed)
        k1, k2, k3, k4 = jax.random.split(key, 4)
        h = jax.random.normal(k1, (B, N, D), dtype=jnp.float32)
        adj_raw = jax.random.uniform(k2, (B, N, N), dtype=jnp.float32)
        lim = 1.0 / np.sqrt(D)
        Wq = jax.random.uniform(k3, (D, D), minval=-lim, maxval=lim, dtype=jnp.float32)
        Wk = jax.random.uniform(k4, (D, D), minval=-lim, maxval=lim, dtype=jnp.float32)
        gamma_raw = jnp.float32(-0.85)
        return {'h': h, 'adj_raw': adj_raw, 'Wq': Wq, 'Wk': Wk, 'gamma_raw': gamma_raw}
    _L1_xattn_all = _L1_xattn_setup()
    _L1_xattn_in = {k: v for k, v in _L1_xattn_all.items() if k in ('Wq', 'Wk', 'gamma_raw')}
    del _L1_xattn_all

    def _L1_ffn_setup():
        import jax, jax.numpy as jnp
        import numpy as np
        key = jax.random.key(seed)
        k1, k2, k3, k4 = jax.random.split(key, 4)
        B, S, D_IN, D_OUT = (4, 1024, 512, 512)
        x = jax.random.normal(k1, (B, S, D_IN), dtype=jnp.float32)
        weight = jax.random.normal(k2, (D_OUT, D_IN), dtype=jnp.float32) * 0.02
        scale_weight = jax.random.uniform(k3, (D_OUT,), dtype=jnp.float32, minval=0.5, maxval=1.5)
        bias = jax.random.normal(k4, (D_OUT,), dtype=jnp.float32) * 0.02
        return {'x': x, 'weight': weight, 'scale_weight': scale_weight, 'bias': bias}
    _L1_ffn_all = _L1_ffn_setup()
    _L1_ffn_in = {k: v for k, v in _L1_ffn_all.items() if k in ('weight', 'scale_weight', 'bias')}
    del _L1_ffn_all

    def _L2_xattn_setup():
        import jax, jax.numpy as jnp
        import numpy as np
        B, S, L = (2, 256, 256)
        DIM_Q, H, K, D_C, D_CQ, R = (512, 16, 128, 128, 384, 64)

        def _rope_tables(seq_len, dim, dtype):
            inv_freq = 1.0 / 10000.0 ** (jnp.arange(0, dim, 2, dtype=dtype) / dim)
            t = jnp.arange(seq_len, dtype=dtype)
            freqs = t[:, None] * inv_freq[None, :]
            sin = jnp.repeat(jnp.sin(freqs), 2, axis=-1)
            cos = jnp.repeat(jnp.cos(freqs), 2, axis=-1)
            return (sin, cos)

        def _rotate_half(x):
            h = x.shape[-1] // 2
            return jnp.concatenate([-x[..., h:], x[..., :h]], axis=-1)
        key = jax.random.key(seed)
        ks = jax.random.split(key, 8)
        s_in = 1.0 / np.sqrt(DIM_Q)
        s_k = 1.0 / np.sqrt(K)
        s_cq = 1.0 / np.sqrt(D_CQ)
        s_c = 1.0 / np.sqrt(D_C)
        return {'hidden_q': jax.random.normal(ks[0], (B, S, DIM_Q), jnp.float32), 'kv_c': jax.random.normal(ks[1], (B, L, D_C), jnp.float32), 'Wq': jax.random.normal(ks[2], (H * K, DIM_Q), jnp.float32) * s_in, 'w_kc_q': jax.random.normal(ks[3], (H, K, D_CQ), jnp.float32) * s_k, 'w_kc_kv': jax.random.normal(ks[4], (H, K, D_C), jnp.float32) * s_k, 'W_qr': jax.random.normal(ks[5], (H, D_CQ, R), jnp.float32) * s_cq / np.sqrt(R), 'W_kr': jax.random.normal(ks[6], (H, D_C, R), jnp.float32) * s_c, 'Wo': jax.random.normal(ks[7], (DIM_Q, H * K), jnp.float32) * s_k}
    _L2_xattn_all = _L2_xattn_setup()
    _L2_xattn_in = {k: v for k, v in _L2_xattn_all.items() if k in ('Wq', 'w_kc_q', 'w_kc_kv', 'W_qr', 'W_kr', 'Wo')}
    del _L2_xattn_all

    def _L2_ffn_setup():
        import jax, jax.numpy as jnp
        import numpy as np
        B, T, D = (4, 256, 512)
        N, S, H = (8, 8, 8)
        ETA = 1.0
        key = jax.random.key(seed)
        ks = jax.random.split(key, 9)
        return {'x': jax.random.normal(ks[0], (B, T, D), jnp.float32), 'select_weight': jax.random.normal(ks[1], (N, D, S), jnp.float32) / D, 'select_mean_diff': jax.random.normal(ks[2], (N, D), jnp.float32) / D, 'imp_center': jax.random.normal(ks[3], (N,), jnp.float32), 'imp_slope': jax.random.normal(ks[4], (N,), jnp.float32) * 5.0, 'lora_update': jax.random.normal(ks[5], (N, D, H), jnp.float32) * 0.02, 'lora_degen': jax.random.normal(ks[6], (N, D, H), jnp.float32) * 0.02, 'bias_w': jax.random.normal(ks[7], (N, D), jnp.float32) * 0.02, 'debias_w': jax.random.normal(ks[8], (N, D), jnp.float32) * 0.02}
    _L2_ffn_all = _L2_ffn_setup()
    _L2_ffn_in = {k: v for k, v in _L2_ffn_all.items() if k in ('select_weight', 'select_mean_diff', 'imp_center', 'imp_slope', 'lora_update', 'lora_degen', 'bias_w', 'debias_w')}
    del _L2_ffn_all

    def _L3_xattn_setup():
        import jax, jax.numpy as jnp
        import numpy as np
        B, S, H, NH, L = (2, 512, 512, 16, 128)
        HD = H // NH
        key = jax.random.key(seed)
        k1, k2, k3, k4, k5 = jax.random.split(key, 5)
        scale = 0.02
        return {'q': jax.random.normal(k1, (B, S, H), dtype=jnp.float32), 'latent_kv': jax.random.normal(k2, (B, S, L), dtype=jnp.float32), 'Wq': jax.random.normal(k3, (H, H), dtype=jnp.float32) * scale, 'Wkv_expand': jax.random.normal(k4, (2 * H, L), dtype=jnp.float32) * scale, 'Wout': jax.random.normal(k5, (H, H), dtype=jnp.float32) * scale}
    _L3_xattn_all = _L3_xattn_setup()
    _L3_xattn_in = {k: v for k, v in _L3_xattn_all.items() if k in ('Wq', 'Wkv_expand', 'Wout')}
    del _L3_xattn_all

    def _L3_ffn_setup():
        import jax, jax.numpy as jnp
        import numpy as np
        B, S, D, FF, E = (4, 512, 512, 2048, 2)
        key = jax.random.key(seed)
        k0, k1, k2, k3, k4 = jax.random.split(key, 5)
        s = 0.02
        return {'hidden_states': jax.random.normal(k0, (B, S, D), jnp.float32), 'gate_w': jax.random.normal(k1, (E, D), jnp.float32) * s, 'w_gate': jax.random.normal(k2, (E, FF, D), jnp.float32) * s, 'w_up': jax.random.normal(k3, (E, FF, D), jnp.float32) * s, 'w_down': jax.random.normal(k4, (E, D, FF), jnp.float32) * s}
    _L3_ffn_all = _L3_ffn_setup()
    _L3_ffn_in = {k: v for k, v in _L3_ffn_all.items() if k in ('gate_w', 'w_gate', 'w_up', 'w_down')}
    del _L3_ffn_all
    return {'x': x, 'ctx_512': ctx_512, 'g_xattn': g_xattn, 'g_ffn': g_ffn, 'L0_xattn_W_k': _L0_xattn_in['W_k'], 'L0_xattn_b_k': _L0_xattn_in['b_k'], 'L0_xattn_ln_gamma': _L0_xattn_in['ln_gamma'], 'L0_xattn_ln_beta': _L0_xattn_in['ln_beta'], 'L0_ffn_W_syn': _L0_ffn_in['W_syn'], 'L0_ffn_b_syn': _L0_ffn_in['b_syn'], 'L0_ffn_W_out': _L0_ffn_in['W_out'], 'L0_ffn_b_out': _L0_ffn_in['b_out'], 'L0_ffn_gamma': _L0_ffn_in['gamma'], 'L0_ffn_beta': _L0_ffn_in['beta'], 'L1_xattn_Wq': _L1_xattn_in['Wq'], 'L1_xattn_Wk': _L1_xattn_in['Wk'], 'L1_xattn_gamma_raw': _L1_xattn_in['gamma_raw'], 'L1_ffn_weight': _L1_ffn_in['weight'], 'L1_ffn_scale_weight': _L1_ffn_in['scale_weight'], 'L1_ffn_bias': _L1_ffn_in['bias'], 'L2_xattn_Wq': _L2_xattn_in['Wq'], 'L2_xattn_w_kc_q': _L2_xattn_in['w_kc_q'], 'L2_xattn_w_kc_kv': _L2_xattn_in['w_kc_kv'], 'L2_xattn_W_qr': _L2_xattn_in['W_qr'], 'L2_xattn_W_kr': _L2_xattn_in['W_kr'], 'L2_xattn_Wo': _L2_xattn_in['Wo'], 'L2_ffn_select_weight': _L2_ffn_in['select_weight'], 'L2_ffn_select_mean_diff': _L2_ffn_in['select_mean_diff'], 'L2_ffn_imp_center': _L2_ffn_in['imp_center'], 'L2_ffn_imp_slope': _L2_ffn_in['imp_slope'], 'L2_ffn_lora_update': _L2_ffn_in['lora_update'], 'L2_ffn_lora_degen': _L2_ffn_in['lora_degen'], 'L2_ffn_bias_w': _L2_ffn_in['bias_w'], 'L2_ffn_debias_w': _L2_ffn_in['debias_w'], 'L3_xattn_Wq': _L3_xattn_in['Wq'], 'L3_xattn_Wkv_expand': _L3_xattn_in['Wkv_expand'], 'L3_xattn_Wout': _L3_xattn_in['Wout'], 'L3_ffn_gate_w': _L3_ffn_in['gate_w'], 'L3_ffn_w_gate': _L3_ffn_in['w_gate'], 'L3_ffn_w_up': _L3_ffn_in['w_up'], 'L3_ffn_w_down': _L3_ffn_in['w_down']}

def reference(x, ctx_512, g_xattn, g_ffn, L0_xattn_W_k, L0_xattn_b_k, L0_xattn_ln_gamma, L0_xattn_ln_beta, L0_ffn_W_syn, L0_ffn_b_syn, L0_ffn_W_out, L0_ffn_b_out, L0_ffn_gamma, L0_ffn_beta, L1_xattn_Wq, L1_xattn_Wk, L1_xattn_gamma_raw, L1_ffn_weight, L1_ffn_scale_weight, L1_ffn_bias, L2_xattn_Wq, L2_xattn_w_kc_q, L2_xattn_w_kc_kv, L2_xattn_W_qr, L2_xattn_W_kr, L2_xattn_Wo, L2_ffn_select_weight, L2_ffn_select_mean_diff, L2_ffn_imp_center, L2_ffn_imp_slope, L2_ffn_lora_update, L2_ffn_lora_degen, L2_ffn_bias_w, L2_ffn_debias_w, L3_xattn_Wq, L3_xattn_Wkv_expand, L3_xattn_Wout, L3_ffn_gate_w, L3_ffn_w_gate, L3_ffn_w_up, L3_ffn_w_down):
    import jax
    import jax.numpy as jnp

    def _L0_xattn_ref(p, k_v, W_k, b_k, ln_gamma, ln_beta):
        import jax, jax.numpy as jnp
        import numpy as np
        EPS = 1e-06
        IMAGE_DIMS = 512
        kv = k_v @ W_k.T + b_k
        out = jnp.einsum('bij,bjd->bid', p, kv)
        scale = IMAGE_DIMS ** (-0.5)
        sim = jnp.einsum('bid,bjd->bij', out, kv) * scale
        mu = jnp.mean(sim, axis=-1, keepdims=True)
        var = jnp.var(sim, axis=-1, keepdims=True)
        sim = (sim - mu) * jax.lax.rsqrt(var + EPS) * ln_gamma + ln_beta
        attn = jax.nn.softmax(sim, axis=-1)
        return attn

    def _L0_ffn_ref(x, W_syn, b_syn, W_out, b_out, gamma, beta):
        import jax, jax.numpy as jnp
        import numpy as np
        TARGET_SPARSITY = 0.9
        LN_EPS = 1e-05

        def ternary_quant(W):
            scale = jnp.mean(jnp.abs(W))
            q = jnp.clip(jnp.round(W / (scale + 1e-08)), -1.0, 1.0) * scale
            return W + jax.lax.stop_gradient(q - W)

        def layernorm(x, gamma, beta):
            mu = jnp.mean(x, axis=-1, keepdims=True)
            var = jnp.var(x, axis=-1, keepdims=True)
            return (x - mu) * jax.lax.rsqrt(var + LN_EPS) * gamma + beta
        B, S, D = x.shape
        N = W_syn.shape[0]
        x_flat = x.reshape(-1, D)
        z = x_flat @ ternary_quant(W_syn).T + b_syn
        k = max(1, int(N * (1.0 - TARGET_SPARSITY)))
        topv, _ = jax.lax.top_k(z, k)
        thresh = topv[:, -1:]
        hidden = jnp.where(z >= thresh, jax.nn.relu(z), 0.0)
        out = hidden @ ternary_quant(W_out).T + b_out
        out = out.reshape(B, S, D)
        return layernorm(x + out, gamma, beta)

    def _L1_xattn_ref(h, adj_raw, Wq, Wk, gamma_raw):
        import jax, jax.numpy as jnp
        import numpy as np
        B, N, D = (16, 512, 128)
        H = 4
        TOP_K_RATIO = 0.3
        b, n, dm = h.shape
        d = dm // H
        Q = (h @ Wq.T).reshape(b, n, H, d).transpose(0, 2, 1, 3)
        K = (h @ Wk.T).reshape(b, n, H, d).transpose(0, 2, 1, 3)
        sim = jnp.einsum('bhnd,bhmd->bnm', Q, K) / (jnp.sqrt(jnp.float32(d)) * H)
        k = max(1, int(n * TOP_K_RATIO))
        topk_vals = jax.lax.top_k(sim, k)[0]
        threshold = topk_vals[:, :, -1:]
        sparse_mask = (sim >= threshold).astype(sim.dtype)
        A_learned = jax.nn.sigmoid(sim) * sparse_mask
        A_learned = (A_learned + jnp.swapaxes(A_learned, -1, -2)) * 0.5
        gamma = jax.nn.sigmoid(gamma_raw)
        return (1.0 - gamma) * adj_raw + gamma * A_learned

    def _L1_ffn_ref(x, weight, scale_weight, bias):
        import jax, jax.numpy as jnp
        import numpy as np
        w = weight * scale_weight[:, None]
        out = jnp.einsum('bsi,oi->bso', x, w) + bias
        return out

    def _L2_xattn_ref(hidden_q, kv_c, Wq, w_kc_q, w_kc_kv, W_qr, W_kr, Wo):
        import jax, jax.numpy as jnp
        import numpy as np
        B, S, L = (2, 256, 256)
        DIM_Q, H, K, D_C, D_CQ, R = (512, 16, 128, 128, 384, 64)

        def _rope_tables(seq_len, dim, dtype):
            inv_freq = 1.0 / 10000.0 ** (jnp.arange(0, dim, 2, dtype=dtype) / dim)
            t = jnp.arange(seq_len, dtype=dtype)
            freqs = t[:, None] * inv_freq[None, :]
            sin = jnp.repeat(jnp.sin(freqs), 2, axis=-1)
            cos = jnp.repeat(jnp.cos(freqs), 2, axis=-1)
            return (sin, cos)

        def _rotate_half(x):
            h = x.shape[-1] // 2
            return jnp.concatenate([-x[..., h:], x[..., :h]], axis=-1)
        b, s, _ = hidden_q.shape
        l = kv_c.shape[1]
        q_hk = (hidden_q @ Wq.T).reshape(b, s, H, K)
        q_big = jnp.einsum('bshk,hkq->bshq', q_hk, w_kc_q)
        sin, cos = _rope_tables(l, D_C, kv_c.dtype)
        kv_rope = kv_c * cos[None] + _rotate_half(kv_c) * sin[None]
        q_r = jnp.einsum('bshq,hqr->bhsr', q_big, W_qr)
        k_r = jnp.einsum('bld,hdr->bhlr', kv_rope, W_kr)
        scores = jnp.einsum('bhsr,bhlr->bhsl', q_r, k_r)
        attn = jax.nn.softmax(scores, axis=-1)
        ctx_c = jnp.einsum('bhsl,bld->bhsd', attn, kv_rope)
        ctx_lat = jnp.einsum('bhsd,hkd->bshk', ctx_c, w_kc_kv)
        out = ctx_lat.reshape(b, s, H * K) @ Wo.T
        return out

    def _L2_ffn_ref(x, select_weight, select_mean_diff, imp_center, imp_slope, lora_update, lora_degen, bias_w, debias_w):
        import jax, jax.numpy as jnp
        import numpy as np
        B, T, D = (4, 256, 512)
        N, S, H = (8, 8, 8)
        ETA = 1.0
        x_diff = x[:, None, :, :] - select_mean_diff[None, :, None, :]
        x_diff = x_diff / jnp.linalg.norm(x_diff, axis=3, keepdims=True)
        cont = jnp.einsum('nds,bntd->bnts', select_weight, x_diff) ** 2
        score = cont.sum(axis=-1)
        gate = jax.nn.sigmoid(imp_slope[None, :, None] * (score - imp_center[None, :, None]))
        sel_scale = gate.max(axis=1)[..., None]
        sel_idx = gate.argmax(axis=1)
        debias = jnp.take(debias_w, sel_idx, axis=0)
        bias = jnp.take(bias_w, sel_idx, axis=0)
        upd = jnp.take(lora_update, sel_idx, axis=0)
        dgn = jnp.take(lora_degen, sel_idx, axis=0)
        x_debias = x - debias
        mod_x = jnp.einsum('btdh,btd->bth', upd, x_debias)
        degen_up = jnp.einsum('btdh,bth->btd', dgn, mod_x)
        mod_x_bias = ETA * (bias + degen_up)
        return (1.0 - sel_scale) * x + sel_scale * mod_x_bias

    def _L3_xattn_ref(q, latent_kv, Wq, Wkv_expand, Wout):
        import jax, jax.numpy as jnp
        import numpy as np
        B, S, H, NH, L = (2, 512, 512, 16, 128)
        HD = H // NH
        b, sq, _ = q.shape
        sk = latent_kv.shape[1]
        qp = q @ Wq.T
        kv = latent_kv @ Wkv_expand.T
        k, v = jnp.split(kv, 2, axis=-1)
        qh = qp.reshape(b, sq, NH, HD).transpose(0, 2, 1, 3)
        kh = k.reshape(b, sk, NH, HD).transpose(0, 2, 1, 3)
        vh = v.reshape(b, sk, NH, HD).transpose(0, 2, 1, 3)
        inv_sqrt_d = 1.0 / jnp.sqrt(jnp.float32(HD))
        scores = jnp.einsum('bhqd,bhkd->bhqk', qh, kh) * inv_sqrt_d
        causal = jnp.tril(jnp.ones((sq, sk), dtype=bool))
        scores = jnp.where(causal, scores, jnp.finfo(scores.dtype).min)
        attn = jax.nn.softmax(scores, axis=-1)
        out = jnp.einsum('bhqk,bhkd->bhqd', attn, vh)
        out = out.transpose(0, 2, 1, 3).reshape(b, sq, H)
        return out @ Wout.T

    def _L3_ffn_ref(hidden_states, gate_w, w_gate, w_up, w_down):
        import jax, jax.numpy as jnp
        import numpy as np
        B, S, D, FF, E = (4, 512, 512, 2048, 2)
        b, s, d = hidden_states.shape
        x = hidden_states.reshape(-1, d)
        logits = x @ gate_w.T
        probs = jax.nn.softmax(logits.astype(jnp.float32), axis=-1)
        sel = jnp.argmax(probs, axis=-1)
        top_w = jnp.take_along_axis(probs, sel[:, None], axis=-1)
        onehot = jax.nn.one_hot(sel, gate_w.shape[0], dtype=x.dtype)
        g = jnp.einsum('td,efd->etf', x, w_gate)
        u = jnp.einsum('td,efd->etf', x, w_up)
        h = jax.nn.silu(g) * u
        y = jnp.einsum('etf,edf->etd', h, w_down)
        out = jnp.einsum('etd,te->td', y, onehot * top_w)
        return out.reshape(b, s, d)
    x = x + jnp.tanh(g_xattn[0]) * _L0_xattn_ref(_layernorm(x, axis=-1), ctx_512, L0_xattn_W_k, L0_xattn_b_k, L0_xattn_ln_gamma, L0_xattn_ln_beta)
    x = x + jnp.tanh(g_ffn[0]) * _L0_ffn_ref(_layernorm(x, axis=-1), L0_ffn_W_syn, L0_ffn_b_syn, L0_ffn_W_out, L0_ffn_b_out, L0_ffn_gamma, L0_ffn_beta)
    x = x + jnp.tanh(g_xattn[1]) * _L1_xattn_ref(ctx_512, _layernorm(x, axis=-1), L1_xattn_Wq, L1_xattn_Wk, L1_xattn_gamma_raw)
    x = x + jnp.tanh(g_ffn[1]) * _L1_ffn_ref(_layernorm(x, axis=-1), L1_ffn_weight, L1_ffn_scale_weight, L1_ffn_bias)
    x = x + jnp.tanh(g_xattn[2]) * _L2_xattn_ref(_layernorm(x, axis=-1), ctx_512, L2_xattn_Wq, L2_xattn_w_kc_q, L2_xattn_w_kc_kv, L2_xattn_W_qr, L2_xattn_W_kr, L2_xattn_Wo)
    x = x + jnp.tanh(g_ffn[2]) * _L2_ffn_ref(_layernorm(x, axis=-1), L2_ffn_select_weight, L2_ffn_select_mean_diff, L2_ffn_imp_center, L2_ffn_imp_slope, L2_ffn_lora_update, L2_ffn_lora_degen, L2_ffn_bias_w, L2_ffn_debias_w)
    x = x + jnp.tanh(g_xattn[3]) * _L3_xattn_ref(_layernorm(x, axis=-1), ctx_512, L3_xattn_Wq, L3_xattn_Wkv_expand, L3_xattn_Wout)
    x = x + jnp.tanh(g_ffn[3]) * _L3_ffn_ref(_layernorm(x, axis=-1), L3_ffn_gate_w, L3_ffn_w_gate, L3_ffn_w_up, L3_ffn_w_down)
    return x

_drawn_inputs = setup_inputs


def setup_inputs(seed=0):
    import zlib

    import numpy as np

    out = dict(_drawn_inputs(seed))
    spreads = {'L0_xattn_b_k': (0.0, 2.0),
     'L0_xattn_ln_gamma': (1.0, 0.6),
     'L0_xattn_ln_beta': (0.0, 2.0),
     'L0_ffn_b_syn': (0.0, 0.1),
     'L0_ffn_b_out': (0.0, 0.1),
     'L0_ffn_gamma': (1.0, 0.2),
     'L0_ffn_beta': (0.0, 0.1)}
    factors = {'g_ffn': 25.256,
     'L0_xattn_W_k': 7.099,
     'L1_ffn_bias': 2.67,
     'L2_ffn_lora_update': 3.057,
     'L2_ffn_lora_degen': 3.422,
     'L2_ffn_bias_w': 4.2,
     'L2_ffn_debias_w': 8.0,
     'L3_xattn_Wq': 36.364}
    for name, (base, spread) in spreads.items():
        noise = np.random.default_rng([zlib.crc32(name.encode()), seed]).standard_normal(out[name].shape)
        drawn = base * np.exp(spread * noise) if base else spread * noise
        out[name] = jnp.asarray(drawn.astype(out[name].dtype))
    for name, factor in factors.items():
        out[name] = (out[name] * factor).astype(out[name].dtype)
    return out
```

```python
import math
from contextlib import ExitStack

import numpy as np

import concourse.bass as bass
from concourse import mybir

F32 = mybir.dt.float32
F32R = mybir.dt.float32r
ALU = mybir.AluOpType
ACT = mybir.ActivationFunctionType
AX = mybir.AxisListType

P = 128
B, S, D, DC = 4, 512, 512, 128
TILES = B * S // P
TB = S // P
C = D // P
HID = 2048
HC = HID // P
BANK = 512
LN_EPS = 1e-5


class InOrder:

    def __init__(self, eng, sem):
        self.eng, self.sem, self.base, self.n = eng, sem, 0, 0

    def __call__(self, instruction):
        self.n += 1
        instruction.then_inc(self.sem, 1)
        self.eng.wait_ge(self.sem, self.base + self.n)

    def enter(self, i, per):
        outer = (self.base, self.n)
        self.base, self.n = self.base + self.n + i * per, 0
        return outer

    def leave(self, outer, turns, per):
        assert self.n == per, f"{self.sem}: {self.n} steps a turn, not {per}"
        self.base, self.n = outer[0], outer[1] + turns * per


def program(nc, inp, out, stages=8):
    ctx = ExitStack()
    with ctx:
        sems = {}

        def sem(name):
            if name not in sems:
                sems[name] = ctx.enter_context(nc.semaphore(name))
            return sems[name]

        def sb(name, shape, dt=F32, where=ctx):
            return where.enter_context(nc.sbuf_tensor(name, shape, dt))

        ps = ctx.enter_context(nc.psum_tensor("ps", [P, 8, BANK], F32))

        X = sb("X", [P, TILES, D])
        tg = sb("tg", [P, 8])
        ident = sb("ident", [P, P])
        ones = sb("ones", [P, P])
        minus_half = sb("minus_half", [P, TB])
        xn = sb("xn", [P, TB, D])
        xT_hi = sb("xT_hi", [P, C, S], F32R)
        xT_lo = sb("xT_lo", [P, C, S], F32R)
        ln_stats = sb("ln_stats", [P, TB, 6])
        ln_mv = sb("ln_mv", [P, TB, 2])
        ln_var = sb("ln_var", [P, TB])
        ln_rstd = sb("ln_rstd", [P, TB])
        small = sb("small", [P, 64])

        def mm3(pe, o, l_hi, l_lo, r_hi, r_lo, start, stop):
            pe.matmul(o, l_hi, r_hi, start=start, stop=False)
            pe.matmul(o, l_hi, r_lo, start=False, stop=False)
            return pe.matmul(o, l_lo, r_hi, start=False, stop=stop)

        def plain(eng):
            eng.sem_inc(sem("plain"), 1)

        def end_stage(eng, n):
            eng.drain().then_inc(sem("stage_done"), 1)
            eng.wait_ge(sem("stage_done"), 4 * (n + 1))

        def ln_turn(s, i):
            return B * "abcdefgh".index(s) + i

        def xT_turn(s, i):
            return {"g": 6 * B + 2 * i, "g2": 6 * B + 2 * i + 1, "h": 8 * B + i}.get(s) if s in ("g", "g2", "h") else ln_turn(s, i)

        def norm_vector(dve, k, s, i, X=X):
            for j in range(TB):
                k(dve.bn_stats(ln_stats[:, j, :], X[:, i * TB + j, :]))
            for j in range(TB):
                plain(dve)
                k(dve.bn_aggr(ln_mv[:, j, :], ln_stats[:, j, :]))
            dve.tensor_scalar(ln_var[:, :], ln_mv[:, :, 1], LN_EPS, None, ALU.add).then_inc(sem("ln_var"), 1)
            dve.wait_ge(sem("ln_rstd"), ln_turn(s, i) + 1)
            for j in range(TB):
                dve.tensor_scalar(xn[:, j, :], X[:, i * TB + j, :], ln_mv[:, j, 0:1], ln_rstd[:, j:j + 1],
                                  ALU.subtract, ALU.mult).then_inc(sem("ln_xn"), 1)
            dve.wait_ge(sem("ln_xn"), TB * (xT_turn(s, i) + 1))
            for j in range(TB):
                dve.wait_ge(sem("ln_xT_hi"), TB * xT_turn(s, i) + j + 1)
                q = slice(j * P, (j + 1) * P)
                dve.tensor_tensor(xT_lo[:, :, q], ps[:, j % 2, :].rearrange("p (c t) -> p c t", c=C),
                                  xT_hi[:, :, q].bitcast(F32), ALU.subtract).then_inc(sem("ln_xT"), 1)
            dve.wait_ge(sem("ln_xT"), TB * (xT_turn(s, i) + 1))

        def norm_pool(pool, s, i):
            pool.wait_ge(sem("ln_var"), ln_turn(s, i) + 1)
            pool.tensor_tensor(ln_rstd[:, :], ln_var[:, :], minus_half[:, :], ALU.pow).then_inc(sem("ln_rstd"), 1)

        def norm_tensor(pe, s, i):
            for j in range(TB):
                pe.wait_ge(sem("ln_xn"), TB * xT_turn(s, i) + j + 1)
                if j >= 2:
                    pe.wait_ge(sem("ln_xT"), TB * xT_turn(s, i) + j - 1)
                for c in range(C):
                    t = pe.transpose(ps[:, j % 2, c * P:(c + 1) * P], xn[:, j, c * P:(c + 1) * P], ident[:, :])
                t.then_inc(sem("ln_xT_ps"), 1)
            pe.wait_ge(sem("ln_xT"), TB * (xT_turn(s, i) + 1))

        def norm_scalar(act, s, i):
            for j in range(TB):
                act.wait_ge(sem("ln_xT_ps"), TB * xT_turn(s, i) + j + 1)
                act.activation(xT_hi[:, :, j * P:(j + 1) * P], ps[:, j % 2, :].rearrange("p (c t) -> p c t", c=C),
                               ACT.Copy).then_inc(sem("ln_xT_hi"), 1)

        stack = {}

        def mem(stage):
            stack[stage] = ExitStack()
            return lambda name, shape, dt=F32: sb(name, shape, dt, stack[stage])

        m = mem("A")
        a_ctxT = m("a_ctxT", [P, B * S])
        a_ctx_hi, a_ctx_lo = m("a_ctx_hi", [P, B * S], F32R), m("a_ctx_lo", [P, B * S], F32R)
        a_wk = m("a_wk", [P, DC])
        a_wk_hi, a_wk_lo = m("a_wk_hi", [P, DC], F32R), m("a_wk_lo", [P, DC], F32R)
        a_bk = m("a_bk", [P, 1])
        a_gamma, a_beta = m("a_gamma", [P, S]), m("a_beta", [P, S])
        a_kvT = m("a_kvT", [P, S])
        a_kvT_hi, a_kvT_lo = m("a_kvT_hi", [P, S], F32R), m("a_kvT_lo", [P, S], F32R)
        a_kv_hi, a_kv_lo = m("a_kv_hi", [P, TB, DC], F32R), m("a_kv_lo", [P, TB, DC], F32R)
        a_oT_hi, a_oT_lo = m("a_oT_hi", [P, S], F32R), m("a_oT_lo", [P, S], F32R)
        a_sim = m("a_sim", [P, S])
        a_exp = m("a_exp", [P, S])
        a_st = m("a_st", [P, 16])
        stack["A"].close()
        m = mem("B")
        b_tsyn = m("b_tsyn", [P, C, HID], F32R)
        b_tout = m("b_tout", [P, HC, D], F32R)
        b_z = m("b_z", [P, TB, HID])
        b_bsyn = m("b_bsyn", [P, HID])
        b_hT_hi, b_hT_lo = m("b_hT_hi", [P, HC, P], F32R), m("b_hT_lo", [P, HC, P], F32R)
        b_rows = m("b_rows", [P, 3, D])
        b_y = m("b_y", [P, D])
        b_st = m("b_st", [P, 16])
        b_tk = m("b_tk", [P, 8, TB])
        b_junk = m("b_junk", [P, 2, HID], mybir.dt.bfloat16)
        stack["B"].close()
        b_wraw = b_z[:, :, :].rearrange("p a n -> p (a n)")
        b_tmp = b_junk[:, :, :].rearrange("p a n -> p (a n)")
        m = mem("C")
        c_ctxT = m("c_ctxT", [P, B * S])
        c_ctx_hi, c_ctx_lo = m("c_ctx_hi", [P, B * S], F32R), m("c_ctx_lo", [P, B * S], F32R)
        c_w = m("c_w", [P, 2, DC])
        c_w_hi, c_w_lo = m("c_w_hi", [P, 2, DC], F32R), m("c_w_lo", [P, 2, DC], F32R)
        c_qk_hi, c_qk_lo = m("c_qk_hi", [P, 2, S], F32R), m("c_qk_lo", [P, 2, S], F32R)
        c_sim = m("c_sim", [P, TB, S])
        c_a = m("c_a", [P, TB, S])
        c_tk = m("c_tk", [P, 8, TB])
        c_g = m("c_g", [P, 4])
        c_junk = m("c_junk", [P, 2, S])
        c_t = m("c_t", [P, S])
        stack["C"].close()
        m = mem("D")
        d_w = m("d_w", [P, C, D])
        d_w_hi, d_w_lo = m("d_w_hi", [P, C, D], F32R), m("d_w_lo", [P, C, D], F32R)
        d_rows = m("d_rows", [P, 2, D])
        stack["D"].close()

        m = mem("E")
        e_blob = m("e_blob", [P, 2, E_RAW])
        e_wkr = m("e_wkr", [P, P])
        e_u = m("e_u", [P, 2, E_R])
        e_qkw = m("e_qkw", [P, 2, 2, E_QKW], F32R)
        e_g = m("e_g", [P, 2, 2, 2 * D], F32R)
        e_ctx = m("e_ctx", [P, TB, DC])
        e_cos, e_sin = m("e_cos", [P, TB, DC]), m("e_sin", [P, TB, DC])
        e_rot = m("e_rot", [P, TB, DC])
        e_kvr = m("e_kvr", [P, TB, DC])
        e_kvr_hi, e_kvr_lo = m("e_kvr_hi", [P, TB, DC], F32R), m("e_kvr_lo", [P, TB, DC], F32R)
        e_kT_hi, e_kT_lo = m("e_kT_hi", [P, S], F32R), m("e_kT_lo", [P, S], F32R)
        e_qk_hi, e_qk_lo = m("e_qk_hi", [P, 2, 2, S], F32R), m("e_qk_lo", [P, 2, 2, S], F32R)
        e_p = m("e_p", [P, 2, TB, S])
        e_pT_hi, e_pT_lo = m("e_pT_hi", [P, TB, S], F32R), m("e_pT_lo", [P, TB, S], F32R)
        e_cT_hi, e_cT_lo = m("e_cT_hi", [P, 2, S], F32R), m("e_cT_lo", [P, 2, S], F32R)
        e_st = m("e_st", [P, 2, 16])
        e_zero = m("e_zero", [P, S], F32R)
        stack["E"].close()
        e_qkw_kept = nc.dram_tensor("e_qkw_kept", (E_HEADS // 2, P, 2, E_QKW), F32, kind="Internal").ap()
        e_g_kept = nc.dram_tensor("e_g_kept", (E_HEADS // 2, P, 2, 2 * D), F32, kind="Internal").ap()
        m = mem("F")
        f_w, f_q = m("f_w", [P, C, F_N]), m("f_q", [P, C, F_N])
        f_w_hi, f_w_lo = m("f_w_hi", [P, C, F_N], F32R), m("f_w_lo", [P, C, F_N], F32R)
        f_d = m("f_d", [F_K, D])
        f_d_hi, f_d_lo = m("f_d_hi", [F_K, D], F32R), m("f_d_lo", [F_K, D], F32R)
        f_const = m("f_const", [P, F_N])
        f_rows = m("f_rows", [P, 3, 8])
        f_a = m("f_a", [P, TB, F_N])
        f_sq = m("f_sq", [P, TB, 64])
        f_xx = m("f_xx", [P, TB])
        f_g = m("f_g", [P, 6, TB, 8])
        f_s = m("f_s", [P, 4, TB])
        f_m = m("f_m", [P, TB, F_K])
        f_junk = m("f_junk", [P, D])
        f_mT_hi, f_mT_lo = m("f_mT_hi", [F_K, S], F32R), m("f_mT_lo", [F_K, S], F32R)
        stack["F"].close()
        m = mem("G")
        g_w = m("g_w", [P, C, D])
        g_wq_hi, g_wq_lo = m("g_wq_hi", [P, C, D], F32R), m("g_wq_lo", [P, C, D], F32R)
        g_wo_hi, g_wo_lo = m("g_wo_hi", [P, C, D], F32R), m("g_wo_lo", [P, C, D], F32R)
        g_wkv_hi, g_wkv_lo = m("g_wkv_hi", [P, 2 * D], F32R), m("g_wkv_lo", [P, 2 * D], F32R)
        g_ctxT = m("g_ctxT", [P, S])
        g_ctx_hi, g_ctx_lo = m("g_ctx_hi", [P, S], F32R), m("g_ctx_lo", [P, S], F32R)
        g_qT, g_kT = m("g_qT", [P, C, S]), m("g_kT", [P, C, S])
        g_v_hi, g_v_lo = m("g_v_hi", [P, TB, D], F32R), m("g_v_lo", [P, TB, D], F32R)
        g_qk_hi, g_qk_lo = m("g_qk_hi", [P, 2, S], F32R), m("g_qk_lo", [P, 2, S], F32R)
        g_mask = m("g_mask", [P, P])
        g_p = m("g_p", [P, TB, S])
        g_pT_hi, g_pT_lo = m("g_pT_hi", [P, TB, S], F32R), m("g_pT_lo", [P, TB, S], F32R)
        g_st = m("g_st", [P, 16])
        g_o = xn
        stack["G"].close()
        m = mem("H")
        h_w = m("h_w", [P, 2, H_BLOB])
        h_w_hi, h_w_lo = m("h_w_hi", [P, 2, H_BLOB], F32R), m("h_w_lo", [P, 2, H_BLOB], F32R)
        h_gw = m("h_gw", [P, C, 2])
        h_gw_hi, h_gw_lo = m("h_gw_hi", [P, C, 2], F32R), m("h_gw_lo", [P, C, 2], F32R)
        h_sg = m("h_sg", [P, 2, S])
        h_h = m("h_h", [P, 2, S])
        h_h_hi, h_h_lo = m("h_h_hi", [P, 2, S], F32R), m("h_h_lo", [P, 2, S], F32R)
        h_l = m("h_l", [P, 6, TB, 2])
        h_s = m("h_s", [P, 4, TB])
        h_zero = m("h_zero", [P, S], F32R)
        stack["H"].close()

        block = ctx.enter_context(nc.Block())

        @block.sync
        def _(sp):
            for name in ("e_blob_used", "e_ctx_used", "e_g_used0", "e_g_used1", "g_ctx_used", "h_w_used0", "h_w_used1",
                         "h_down0", "h_down1", "h_h0", "h_h1", "e_mg", "e_pair_kept"):
                sp.sem_inc(sem(name), 1)
            sp.sem_inc(sem("qk_ps"), QK_AHEAD)
            sp.dma_start(X[:, :, :], inp["x"]).then_inc(sem("x_in"), 16)
            sp.dma_start(tg[:, 0:4], inp["g_xattn"].partition_broadcast(P)).then_inc(sem("x_in"), 16)
            sp.dma_start(tg[:, 4:8], inp["g_ffn"].partition_broadcast(P)).then_inc(sem("x_in"), 16)
            for dst, src in ((a_ctxT[:, :], inp["ctxT"]), (a_wk[:, :], inp["l0_wkT"]), (a_bk[:, :], inp["l0_bk"]),
                             (a_gamma[:, :], inp["l0_gamma"].partition_broadcast(P)),
                             (a_beta[:, :], inp["l0_beta"].partition_broadcast(P))):
                sp.dma_start(dst, src).then_inc(sem("a_in"), 16)
            if stages > 1:
                sp.wait_ge(sem("stage_done"), 4)
                sp.dma_start(b_wraw, inp["wsynT"]).then_inc(sem("b_in"), 16)
                for dst, src in ((b_bsyn[:, :], inp["b_syn"]), (b_rows[:, 0, :], inp["b_out"]),
                                 (b_rows[:, 1, :], inp["ffn_gamma"]), (b_rows[:, 2, :], inp["ffn_beta"])):
                    sp.dma_start(dst, src.partition_broadcast(P)).then_inc(sem("b_rows_in"), 16)
                sp.wait_ge(sem("b_raw_used"), 1)
                sp.dma_start(b_wraw, inp["woutT"]).then_inc(sem("b_in"), 16)
            if stages > 2:
                sp.wait_ge(sem("stage_done"), 8)
                for dst, src in ((c_ctxT[:, :], inp["ctxT"]), (c_w[:, :, :], inp["l1_wqkT"]),
                                 (c_g[:, 0:1], inp["l1_gamma_raw"].partition_broadcast(P))):
                    sp.dma_start(dst, src).then_inc(sem("c_in"), 16)
            if stages > 3:
                sp.wait_ge(sem("stage_done"), 12)
                for dst, src in ((d_w[:, :, :], inp["l1_wT"]), (d_rows[:, 0, :], inp["l1_scale"].partition_broadcast(P)),
                                 (d_rows[:, 1, :], inp["l1_bias"].partition_broadcast(P))):
                    sp.dma_start(dst, src).then_inc(sem("d_in"), 16)
            if stages > 4:
                sp.wait_ge(sem("stage_done"), 16)
                sp.dma_start(e_cos[:, :, :], inp["cos"]).then_inc(sem("e_tables"), 16)
                sp.dma_start(e_sin[:, :, :], inp["sin"]).then_inc(sem("e_tables"), 16)
                with sp.Fori(0, E_HEADS // 2) as i:
                    sp.wait_ge(sem("e_blob_used"), i + 1)
                    sp.dma_start(e_blob[:, :, :], inp["l2_heads"][i]).then_inc(sem("e_blob_in"), 16)
                    sp.dma_start(e_wkr[:, :], inp["l2_wkr"][i]).then_inc(sem("e_blob_in"), 16)
                    sp.wait_ge(sem("e_pair_made"), i + 1)
                    sp.dma_start(e_qkw_kept[i], e_qkw[:, 0, :, :].bitcast(F32)).then_inc(sem("e_pair_kept"), 16)
                    sp.dma_start(e_g_kept[i], e_g[:, 0, :, :].bitcast(F32)).then_inc(sem("e_pair_kept"), 16)
                sp.wait_ge(sem("e_pair_kept"), 32 * (E_HEADS // 2) + 1)
                with sp.Fori(0, B) as i:
                    sp.wait_ge(sem("e_ctx_used"), i + 1)
                    sp.dma_start(e_ctx[:, :, :], inp["ctx"][i]).then_inc(sem("e_ctx_in"), 16)
                    with sp.Fori(0, E_HEADS // 4) as g:
                        for u in range(2):
                            n = (i * (E_HEADS // 4) + g)
                            sp.wait_ge(sem("qk_ps"), n * E_BODY + 2 * u - 2 + QK_AHEAD)
                            sp.dma_start(e_qkw[:, u, :, :].bitcast(F32), e_qkw_kept[g * 2 + u]).then_inc(sem(f"e_qkw_in{u}"), 16)
                            sp.wait_ge(sem(f"e_g_used{u}"), n + 1)
                            sp.dma_start(e_g[:, u, :, :].bitcast(F32), e_g_kept[g * 2 + u]).then_inc(sem(f"e_g_in{u}"), 16)
            if stages > 5:
                sp.wait_ge(sem("stage_done"), 20)
                for dst, src in ((f_w[:, :, :], inp["l2_fw"]), (f_q[:, :, :], inp["l2_fq"]), (f_d[:, :], inp["l2_fd"]),
                                 (f_rows[:, 0, :], inp["l2_center"].partition_broadcast(P)),
                                 (f_rows[:, 1, :], inp["l2_slope"].partition_broadcast(P)),
                                 (f_rows[:, 2, :], inp["order"].partition_broadcast(P))):
                    sp.dma_start(dst, src).then_inc(sem("f_in"), 16)
            if stages > 6:
                sp.wait_ge(sem("stage_done"), 24)
                for n, src in enumerate(("l3_wqT", "l3_woT", "l3_wkvT")):
                    sp.wait_ge(sem("g_raw_used"), n)
                    dst = g_w[:, :, :] if n < 2 else g_w[:, 0:2, :].rearrange("p a n -> p (a n)")
                    sp.dma_start(dst, inp[src]).then_inc(sem("g_in"), 16)
                with sp.Fori(0, B) as i:
                    sp.wait_ge(sem("g_ctx_used"), i + 1)
                    sp.dma_start(g_ctxT[:, :], inp["ctxT"][:, bass.ts(i, S)]).then_inc(sem("g_ctx_in"), 16)
            if stages > 7:
                sp.wait_ge(sem("stage_done"), 28)
                sp.dma_start(h_gw[:, :, :], inp["l3_gateT"]).then_inc(sem("h_gw_in"), 16)
                with sp.Fori(0, B) as i:
                    for e in range(2):
                        with sp.Fori(0, HC // 2) as f:
                            for u in range(2):
                                n = (i * 2 + e) * (HC // 2) + f
                                sp.wait_ge(sem(f"h_w_used{u}"), n + 1)
                                sp.dma_start(h_w[:, u, :], inp["l3_blob"][e, f * 2 + u]).then_inc(sem(f"h_w_in{u}"), 16)
            sp.wait_ge(sem("stage_done"), 4 * stages)
            sp.dma_start(out, X[:, :, :]).then_inc(sem("x_out"), 16)
            sp.wait_ge(sem("x_out"), 16)

        @block.gpsimd
        def _(pool):
            k = InOrder(pool, sem("pool_steps"))
            k(pool.memset(ident[:, :], 0.0))
            k(pool.memset(ones[:, :], 1.0))
            k(pool.memset(minus_half[:, :], -0.5))
            pool.affine_select(out=ident[:, :], in_=ident[:, :], compare_op=ALU.not_equal, fill=1.0, base=0,
                               pattern=[[-1, P]], channel_multiplier=1).then_inc(sem("consts"), 1)
            with pool.Fori(0, B) as i:
                norm_pool(pool, "a", i)
                for j in range(TB):
                    pool.wait_ge(sem("a_sim_var"), i * TB + j + 1)
                    pool.tensor_tensor(a_st[:, 8:9], a_st[:, 7:8], minus_half[:, 0:1], ALU.pow).then_inc(sem("a_sim_rstd"), 1)
            end_stage(pool, 0)
            if stages > 1:
                with pool.Fori(0, B) as i:
                    norm_pool(pool, "b", i)
                    for j in range(TB):
                        pool.wait_ge(sem("b_y_var"), i * TB + j + 1)
                        pool.tensor_tensor(b_st[:, 8:9], b_st[:, 7:8], minus_half[:, 0:1], ALU.pow).then_inc(sem("b_y_rstd"), 1)
                end_stage(pool, 1)
            for n, name in enumerate("cdefgh", 2):
                if stages > n:
                    if name == "g":
                        k(pool.memset(g_mask[:, :], 0.0))
                        pool.affine_select(out=g_mask[:, :], in_=g_mask[:, :], compare_op=ALU.is_ge, fill=NEG, base=0,
                                           pattern=[[-1, P]], channel_multiplier=1).then_inc(sem("g_mask"), 1)
                    with pool.Fori(0, B) as i:
                        norm_pool(pool, name, i)
                    end_stage(pool, n)

        @block.scalar
        def _(act):
            act.wait_ge(sem("x_in"), 48)
            act.activation(tg[:, :], tg[:, :], ACT.Tanh).then_inc(sem("tg"), 1)
            act.wait_ge(sem("a_in"), 80)
            act.activation(a_ctx_hi[:, :], a_ctxT[:, :], ACT.Copy).then_inc(sem("weights_hi"), 1)
            act.activation(a_wk_hi[:, :], a_wk[:, :], ACT.Copy).then_inc(sem("weights_hi"), 1)
            with act.Fori(0, B) as i:
                norm_scalar(act, "a", i)
                act.wait_ge(sem("a_kvT_ps"), i + 1)
                act.activation(a_kvT[:, :], ps[:, 2, :], ACT.Identity, bias=a_bk[:, 0:1]).then_inc(sem("a_kvT_f"), 1)
                act.wait_ge(sem("a_kvT_f"), i + 1)
                act.activation(a_kvT_hi[:, :], a_kvT[:, :], ACT.Copy).then_inc(sem("a_kvT_hi"), 1)
                act.wait_ge(sem("a_kv_ps"), i + 1)
                act.activation(a_kv_hi[:, :, :], ps[:, 3, :].rearrange("p (t d) -> p t d", t=TB), ACT.Copy)\
                    .then_inc(sem("a_kv_hi"), 1)
                act.wait_ge(sem("a_oT_ps"), i + 1)
                act.activation(a_oT_hi[:, :], ps[:, 4, :], ACT.Copy).then_inc(sem("a_oT_hi"), 1)
                for j in range(TB):
                    act.wait_ge(sem("a_max"), i * TB + j + 1)
                    act.activation(a_exp[:, :], a_sim[:, :], ACT.Exp, bias=a_st[:, 9:10],
                                   accum_out=a_st[:, 10:11]).then_inc(sem("a_exp"), 1)
            end_stage(act, 0)
            if stages > 1:
                with act.Fori(0, B) as i:
                    norm_scalar(act, "b", i)
                    with act.Fori(0, SYN_STEPS) as r:
                        n = i * SYN_STEPS + r
                        act.wait_ge(sem("b_try"), n + 1)
                        for j in (2, 3):
                            act.activation(b_junk[:, 1, :], b_z[:, j, :], ACT.Sign, bias=b_tk[:, 3, j:j + 1],
                                           accum_out=b_tk[:, 4, j:j + 1]).then_inc(sem("b_act_count"), 1)
                            act.wait_ge(sem("b_act_count"), n * 2 + j - 1)
                    for j in range(TB):
                        for q in range(4):
                            act.wait_ge(sem("b_hT_ps"), (i * TB + j) * 4 + q + 1)
                            act.activation(b_hT_hi[:, 4 * q:4 * q + 4, :], ps[:, q, :].rearrange("p (c t) -> p c t", c=4),
                                           ACT.Copy).then_inc(sem("b_hT_hi"), 1)
                end_stage(act, 1)
            if stages > 2:
                act.wait_ge(sem("c_in"), 48)
                act.activation(c_ctx_hi[:, :], c_ctxT[:, :], ACT.Copy).then_inc(sem("weights_hi"), 1)
                act.activation(c_w_hi[:, :, :], c_w[:, :, :], ACT.Copy).then_inc(sem("weights_hi"), 1)
                act.activation(c_g[:, 1:2], c_g[:, 0:1], ACT.Exp, scale=-1.0).then_inc(sem("c_g"), 1)
                with act.Fori(0, B) as i:
                    norm_scalar(act, "c", i)
                    for w in range(2):
                        act.wait_ge(sem("c_qk_ps"), i * 2 + w + 1)
                        act.activation(c_qk_hi[:, w, :], ps[:, 2 + w, :], ACT.Copy).then_inc(sem("c_qk_hi"), 1)
                    for j in range(TB):
                        act.wait_ge(sem("c_sim_ps"), i * TB + j + 1)
                        act.activation(c_sim[:, j, :], ps[:, 4 + j % 2, :], ACT.Copy, scale=SIM1_SCALE).then_inc(sem("c_sim"), 1)
                    for j in range(TB):
                        act.wait_ge(sem("c_sim"), i * TB + j + 1)
                        act.activation(c_a[:, j, :], c_sim[:, j, :], ACT.Exp, scale=-1.0).then_inc(sem("c_e"), 1)
                end_stage(act, 2)
            if stages > 3:
                act.wait_ge(sem("d_ws"), 4)
                act.activation(d_w_hi[:, :, :], d_w[:, :, :], ACT.Copy).then_inc(sem("weights_hi"), 1)
                with act.Fori(0, B) as i:
                    norm_scalar(act, "d", i)
                end_stage(act, 3)

            if stages > 4:
                def e_qk_scalar(turn, d):
                    u = d % 2
                    for w in range(2):
                        act.wait_ge(sem("qk_ps"), QK_AHEAD + turn * E_BODY + d * 2 + w + 1)
                        act.activation(e_qk_hi[:, u, w, :], ps[:, 2 + w, :], ACT.Copy).then_inc(sem("qk_hi"), 1)

                def e_exp_scalar(h, a):
                    for t in range(TB):
                        act.wait_ge(sem("score_max"), h * TB + t + 1)
                        act.activation(e_p[:, a, t, :], ps[:, t % 2, :], ACT.Exp, bias=e_st[:, a, t:t + 1],
                                       accum_out=e_st[:, a, 4 + t:5 + t]).then_inc(sem("exp"), 1)

                def e_head_scalar(turn, hh, tail):
                    h = turn * E_BODY + hh
                    if not (tail and hh == E_BODY - 1):
                        e_exp_scalar(h + 1, (hh + 1) % 2)
                    for c in range(TB):
                        act.wait_ge(sem("pT_ps"), h * TB + c + 1)
                        act.activation(e_pT_hi[:, c, :], ps[:, 2 + c % 2, :], ACT.Copy).then_inc(sem("pT_hi"), 1)
                    act.wait_ge(sem("head_ps"), h + 1)
                    act.activation(e_cT_hi[:, hh % 2, :], ps[:, 1, :], ACT.Copy).then_inc(sem("head_hi"), 1)
                    if hh % 2 == 0 and not (tail and hh == E_BODY - 2):
                        e_qk_scalar(turn, hh // 2 + 1)

                with act.Fori(0, E_HEADS // 2) as i:
                    for u in range(2):
                        n = i * 2 + u
                        act.wait_ge(sem("e_u_ps"), n + 1)
                        act.activation(e_u[:, u, :], ps[:, 0, 0:E_R], ACT.Copy).then_inc(sem("e_u"), 1)
                        act.wait_ge(sem("e_mg_ps"), n + 1)
                        if u == 0:
                            act.wait_ge(sem("e_pair_kept"), 32 * i + 1)
                        act.activation(e_qkw[:, 0, 0, 0:4 * P].rearrange("p (c n) -> p c n", c=C)[:, :, u * E_R:(u + 1) * E_R],
                                       ps[:, 1, 0:C * E_R].rearrange("p (c n) -> p c n", c=C), ACT.Copy).then_inc(sem("e_mg_hi"), 1)
                        act.activation(e_g[:, 0, 0, u * D:(u + 1) * D], ps[:, 2, :], ACT.Copy).then_inc(sem("e_mg_hi"), 1)
                    act.wait_ge(sem("e_blob_in"), 32 * (i + 1))
                    act.activation(e_qkw[:, 0, 0, 4 * P:5 * P], e_wkr[:, :], ACT.Copy).then_inc(sem("e_wkr_hi"), 1)
                with act.Fori(0, B) as i:
                    norm_scalar(act, "e", i)
                    act.wait_ge(sem("e_kvr"), i + 1)
                    act.activation(e_kvr_hi[:, :, :], e_kvr[:, :, :], ACT.Copy).then_inc(sem("e_kvr_hi"), 1)
                    act.wait_ge(sem("e_kT_ps"), i + 1)
                    act.activation(e_kT_hi[:, :], ps[:, 2, :], ACT.Copy).then_inc(sem("e_kT_hi"), 1)
                    e_qk_scalar(i * E_TURNS, 0)
                    e_exp_scalar(i * E_HEADS, 0)
                    with act.Fori(0, E_TURNS - 1) as g:
                        for hh in range(E_BODY):
                            e_head_scalar(i * E_TURNS + g, hh, False)
                    for hh in range(E_BODY):
                        e_head_scalar((i + 1) * E_TURNS - 1, hh, True)
                end_stage(act, 4)
            if stages > 5:
                act.wait_ge(sem("f_in"), 96)
                act.activation(f_w_hi[:, :, :], f_w[:, :, :], ACT.Copy).then_inc(sem("weights_hi"), 1)
                act.activation(f_d_hi[:, :], f_d[:, :], ACT.Copy).then_inc(sem("weights_hi"), 1)
                with act.Fori(0, B) as i:
                    norm_scalar(act, "f", i)
                    act.wait_ge(sem("ln_xn"), TB * (xT_turn("f", i) + 1))
                    for j in range(TB):
                        act.activation(f_junk[:, :], xn[:, j, :], ACT.Square, accum_out=f_xx[:, j:j + 1]).then_inc(sem("f_xx"), 1)
                        act.wait_ge(sem("f_xx"), i * TB + j + 1)
                    act.wait_ge(sem("f_z"), i + 1)
                    act.activation(f_g[:, 1, :, :], f_g[:, 0, :, :], ACT.Exp, scale=-1.0).then_inc(sem("f_e"), 1)
                    act.wait_ge(sem("f_mT_ps"), i + 1)
                    act.activation(f_mT_hi[:, :], ps[0:F_K, 4, :], ACT.Copy).then_inc(sem("f_mT_hi"), 1)
                end_stage(act, 5)
            if stages > 6:
                for n, dst in enumerate((g_wq_hi, g_wo_hi)):
                    act.wait_ge(sem("g_in"), 16 * (n + 1))
                    act.activation(dst[:, :, :], g_w[:, :, :], ACT.Copy).then_inc(sem("weights_hi"), 1)
                act.wait_ge(sem("g_in"), 48)
                act.activation(g_wkv_hi[:, :], g_w[:, 0:2, :].rearrange("p a n -> p (a n)"), ACT.Copy).then_inc(sem("weights_hi"), 1)
                with act.Fori(0, B) as i:
                    norm_scalar(act, "g", i)
                    act.wait_ge(sem("g_ctx_in"), 16 * (i + 1))
                    act.activation(g_ctx_hi[:, :], g_ctxT[:, :], ACT.Copy).then_inc(sem("g_ctx_hi"), 1)
                    for m_ in range(C):
                        act.wait_ge(sem("g_q_ps"), i * C + m_ + 1)
                        act.activation(g_qT[:, m_, :], ps[:, 2 + m_ % 2, :], ACT.Copy).then_inc(sem("g_q"), 1)
                        act.wait_ge(sem("g_k_ps"), i * C + m_ + 1)
                        act.activation(g_kT[:, m_, :], ps[:, 4 + m_ % 2, :], ACT.Copy).then_inc(sem("g_k"), 1)
                    for t in range(TB):
                        act.wait_ge(sem("g_v_ps"), i * TB + t + 1)
                        act.activation(g_v_hi[:, t, :], ps[:, 6 + t % 2, :], ACT.Copy).then_inc(sem("g_v_hi"), 1)
                    with act.Fori(0, C) as g:
                        n = i * C + g
                        act.wait_ge(sem("head_out"), G_HEADS_BEFORE + n * 4)
                        act.activation(g_qk_hi[:, 0, :], g_qT[:, g, :], ACT.Copy).then_inc(sem("qk_hi"), 1)
                        act.activation(g_qk_hi[:, 1, :], g_kT[:, g, :], ACT.Copy).then_inc(sem("qk_hi"), 1)
                        for hh in range(4):
                            h = G_HEADS_BEFORE + n * 4 + hh
                            for t in range(TB):
                                w = (t + 1) * P
                                act.wait_ge(sem("score_max"), h * TB + t + 1)
                                act.activation(g_p[:, t, 0:w], ps[:, t % 2, 0:w], ACT.Exp, bias=g_st[:, t:t + 1], scale=G_SCALE,
                                               accum_out=g_st[:, 4 + t:5 + t]).then_inc(sem("exp"), 1)
                            for c in range(TB):
                                act.wait_ge(sem("pT_ps"), h * TB + c + 1)
                                act.activation(g_pT_hi[:, c, c * P:], ps[:, 2 + c % 2, c * P:], ACT.Copy).then_inc(sem("pT_hi"), 1)
                    norm_scalar(act, "g2", i)
                end_stage(act, 6)
            if stages > 7:
                act.wait_ge(sem("h_gw_in"), 16)
                act.activation(h_gw_hi[:, :, :], h_gw[:, :, :], ACT.Copy).then_inc(sem("weights_hi"), 1)

                def h_split_scalar(n, u):
                    act.wait_ge(sem(f"h_w_in{u}"), 16 * (n + 1))
                    act.wait_ge(sem(f"h_down{u}"), n + 1)
                    act.activation(h_w_hi[:, u, :], h_w[:, u, :], ACT.Copy).then_inc(sem(f"h_w_hi{u}"), 1)

                def h_hidden_scalar(n, u):
                    act.wait_ge(sem(f"h_gu_ps{u}"), n + 1)
                    act.activation(h_sg[:, u, :], ps[:, u, :], ACT.Silu).then_inc(sem(f"h_sg{u}"), 1)
                    act.wait_ge(sem(f"h_h{u}"), n + 2)
                    act.activation(h_h_hi[:, u, :], h_h[:, u, :], ACT.Copy).then_inc(sem(f"h_h_hi{u}"), 1)

                with act.Fori(0, B) as i:
                    norm_scalar(act, "h", i)
                    act.wait_ge(sem("h_logit"), i + 1)
                    act.activation(h_l[:, 2, :, :], h_l[:, 1, :, :], ACT.Exp).then_inc(sem("h_le"), 1)
                    for e in range(2):
                        first = (i * 2 + e) * (HC // 2)
                        h_split_scalar(first, 0)
                        with act.Fori(0, HC // 2 - 1) as f:
                            n = first + f
                            h_split_scalar(n, 1)
                            h_hidden_scalar(n, 0)
                            h_split_scalar(n + 1, 0)
                            h_hidden_scalar(n, 1)
                        last = first + HC // 2 - 1
                        h_split_scalar(last, 1)
                        h_hidden_scalar(last, 0)
                        h_hidden_scalar(last, 1)
                end_stage(act, 7)

        @block.vector
        def _(dve):
            k = InOrder(dve, sem("dve_steps"))
            dve.wait_ge(sem("x_in"), 48)
            dve.wait_ge(sem("consts"), 1)
            dve.wait_ge(sem("tg"), 1)
            dve.wait_ge(sem("weights_hi"), HI_BEFORE["a"] + 2)
            k(dve.tensor_tensor(a_ctx_lo[:, :], a_ctxT[:, :], a_ctx_hi[:, :].bitcast(F32), ALU.subtract))
            dve.tensor_tensor(a_wk_lo[:, :], a_wk[:, :], a_wk_hi[:, :].bitcast(F32), ALU.subtract).then_inc(sem("weights"), 1)
            dve.wait_ge(sem("weights"), READY["a"])
            with dve.Fori(0, B) as i:
                per = 2 * TB + TB * 9
                o = k.enter(i, per)
                norm_vector(dve, k, "a", i)
                dve.wait_ge(sem("a_kvT_hi"), i + 1)
                dve.tensor_tensor(a_kvT_lo[:, :], a_kvT[:, :], a_kvT_hi[:, :].bitcast(F32), ALU.subtract).then_inc(sem("a_kvT"), 1)
                dve.wait_ge(sem("a_kv_hi"), i + 1)
                dve.tensor_tensor(a_kv_lo[:, :, :], ps[:, 3, :].rearrange("p (t d) -> p t d", t=TB),
                                  a_kv_hi[:, :, :].bitcast(F32), ALU.subtract).then_inc(sem("a_kv"), 1)
                dve.wait_ge(sem("a_oT_hi"), i + 1)
                dve.tensor_tensor(a_oT_lo[:, :], ps[:, 4, :], a_oT_hi[:, :].bitcast(F32), ALU.subtract).then_inc(sem("a_oT"), 1)
                for j in range(TB):
                    n = i * TB + j
                    sim = ps[:, 5 + j % 2, :]
                    dve.wait_ge(sem("a_sim_ps"), n + 1)
                    k(dve.bn_stats(a_st[:, 0:6], sim))
                    plain(dve)
                    k(dve.bn_aggr(a_st[:, 11:13], a_st[:, 0:6]))
                    dve.tensor_scalar(a_st[:, 7:8], a_st[:, 12:13], float(D) ** -1, 1e-6, ALU.mult, ALU.add).then_inc(sem("a_sim_var"), 1)
                    dve.wait_ge(sem("a_sim_rstd"), n + 1)
                    k(dve.tensor_scalar(a_st[:, 13:14], a_st[:, 8:9], float(D) ** -0.5, None, ALU.mult))
                    dve.tensor_scalar(a_sim[:, :], sim, a_st[:, 11:12], a_st[:, 13:14], ALU.subtract, ALU.mult)\
                        .then_inc(sem("a_sim_used"), 1)
                    dve.wait_ge(sem("a_sim_used"), n + 1)
                    k(dve.tensor_tensor(a_sim[:, :], a_sim[:, :], a_gamma[:, :], ALU.mult))
                    k(dve.tensor_tensor(a_sim[:, :], a_sim[:, :], a_beta[:, :], ALU.add))
                    k(dve.tensor_reduce(a_st[:, 6:7], a_sim[:, :], AX.X, ALU.max))
                    dve.tensor_scalar(a_st[:, 9:10], a_st[:, 6:7], -1.0, None, ALU.mult).then_inc(sem("a_max"), 1)
                    dve.wait_ge(sem("a_exp"), n + 1)
                    k(dve.reciprocal(a_st[:, 14:15], a_st[:, 10:11]))
                    k(dve.tensor_tensor(a_st[:, 15:16], a_st[:, 14:15], tg[:, 0:1], ALU.mult))
                    k(dve.scalar_tensor_tensor(X[:, n, :], a_exp[:, :], a_st[:, 15:16], X[:, n, :], ALU.mult, ALU.add))
                k.leave(o, B, per)
            end_stage(dve, 0)

            if stages > 1:
                for w, dst in enumerate((b_tsyn[:, :, :].rearrange("p c n -> p (c n)"), b_tout[:, :, :].rearrange("p c n -> p (c n)"))):
                    dve.wait_ge(sem("b_in"), 16 * (w + 1))
                    dve.tensor_reduce(b_st[:, w:w + 1], b_wraw, AX.X, ALU.add, apply_absolute_value=True).then_inc(sem("b_abs"), 1)
                    dve.wait_ge(sem("b_abs_ps"), w + 1)
                    k(dve.tensor_scalar(b_st[:, 2 + w:3 + w], ps[:, 2, 0:1], 1.0 / (HID * D), None, ALU.mult))
                    k(dve.tensor_scalar(b_st[:, 4:5], b_st[:, 2 + w:3 + w], 1e-8, 0.5, ALU.add, ALU.mult))
                    k(dve.tensor_scalar(b_st[:, 5:6], b_st[:, 4:5], -1.0, None, ALU.mult))
                    for h in range(2):
                        half = slice(h * 2 * HID, (h + 1) * 2 * HID)
                        k(dve.tensor_scalar(b_tmp, b_wraw[:, half], b_st[:, 5:6], None, ALU.is_lt))
                        k(dve.scalar_tensor_tensor(dst[:, half], b_wraw[:, half], b_st[:, 4:5], b_tmp, ALU.is_gt, ALU.subtract))
                    dve.sem_inc(sem("b_raw_used"), 1)
                dve.wait_ge(sem("b_raw_used"), 2)
                dve.wait_ge(sem("b_rows_in"), 64)
                k(dve.tensor_scalar(b_rows[:, 1:3, :], b_rows[:, 1:3, :], tg[:, 4:5], None, ALU.mult))
                k(dve.memset(b_tk[:, 5, 0:2], float(SYN_K)))
                k(dve.memset(b_tk[:, 5, 2:4], float(2 * SYN_K - HID)))
                dve.sem_inc(sem("weights"), 1)
                with dve.Fori(0, B) as i:
                    per = 2 * TB + TB + 3 + SYN_STEPS * 7 + TB + TB * 7
                    o = k.enter(i, per)
                    norm_vector(dve, k, "b", i)
                    for j in range(TB):
                        for q in range(4):
                            n = (i * TB + j) * 4 + q
                            dve.wait_ge(sem("b_z_ps"), n + 1)
                            dve.scalar_tensor_tensor(b_z[:, j, q * BANK:(q + 1) * BANK], ps[:, 4 + q, :], b_st[:, 2:3],
                                                     b_bsyn[:, q * BANK:(q + 1) * BANK], ALU.mult, ALU.add).then_inc(sem("b_z_used"), 1)
                    low, step, cand, neg, cnt, kk, take = (b_tk[:, r, :] for r in range(7))
                    dve.wait_ge(sem("b_z_used"), 16 * (i + 1))
                    for j in range(TB):
                        k(dve.tensor_reduce(step[:, j:j + 1], b_z[:, j, :], AX.X, ALU.max))
                    k(dve.tensor_scalar(step, step, 0.0, 0.5, ALU.max, ALU.mult))
                    k(dve.memset(low, 0.0))
                    k(dve.tensor_copy(cand, step))
                    plain(dve)
                    with dve.Fori(0, SYN_STEPS) as r:
                        p2 = k.enter(r, 7)
                        n = i * SYN_STEPS + r
                        dve.tensor_scalar(neg, cand, -1.0, None, ALU.mult).then_inc(sem("b_try"), 1)
                        for j in (0, 1):
                            k(dve.tensor_scalar(b_junk[:, 0, :], b_z[:, j, :], cand[:, j:j + 1], 0.0, ALU.is_ge, ALU.add,
                                                accum_out=cnt[:, j:j + 1]))
                        dve.wait_ge(sem("b_act_count"), 2 * (n + 1))
                        k(dve.tensor_tensor(take, cnt, kk, ALU.is_ge))
                        k(dve.tensor_tensor(take, take, step, ALU.mult))
                        k(dve.tensor_tensor(low, low, take, ALU.add))
                        k(dve.tensor_scalar(step, step, 0.5, None, ALU.mult))
                        k(dve.tensor_tensor(cand, low, step, ALU.add))
                        k.leave(p2, SYN_STEPS, 7)
                    for j in range(TB):
                        k(dve.scalar_tensor_tensor(b_z[:, j, :], b_z[:, j, :], low[:, j:j + 1], b_z[:, j, :], ALU.is_ge, ALU.mult))
                        dve.sem_inc(sem("b_h"), 1)
                    for j in range(TB):
                        n = i * TB + j
                        for q in range(4):
                            dve.wait_ge(sem("b_hT_hi"), n * 4 + q + 1)
                            dve.tensor_tensor(b_hT_lo[:, 4 * q:4 * q + 4, :], ps[:, q, :].rearrange("p (c t) -> p c t", c=4),
                                              b_hT_hi[:, 4 * q:4 * q + 4, :].bitcast(F32), ALU.subtract).then_inc(sem("b_hT"), 1)
                        dve.wait_ge(sem("b_y_ps"), n + 1)
                        dve.scalar_tensor_tensor(b_y[:, :], ps[:, 4, :], b_st[:, 3:4], xn[:, j, :], ALU.mult, ALU.add)\
                            .then_inc(sem("b_y_used"), 1)
                        dve.wait_ge(sem("b_y_used"), n + 1)
                        k(dve.tensor_tensor(b_y[:, :], b_y[:, :], b_rows[:, 0, :], ALU.add))
                        k(dve.bn_stats(b_st[:, 9:15], b_y[:, :]))
                        plain(dve)
                        k(dve.bn_aggr(b_st[:, 4:6], b_st[:, 9:15]))
                        dve.tensor_scalar(b_st[:, 7:8], b_st[:, 5:6], LN_EPS, None, ALU.add).then_inc(sem("b_y_var"), 1)
                        dve.wait_ge(sem("b_y_rstd"), n + 1)
                        k(dve.tensor_scalar(b_y[:, :], b_y[:, :], b_st[:, 4:5], b_st[:, 8:9], ALU.subtract, ALU.mult))
                        k(dve.tensor_tensor(b_y[:, :], b_y[:, :], b_rows[:, 1, :], ALU.mult))
                        k(dve.tensor_tensor(b_y[:, :], b_y[:, :], b_rows[:, 2, :], ALU.add))
                        k(dve.tensor_tensor(X[:, n, :], X[:, n, :], b_y[:, :], ALU.add))
                    k.leave(o, B, per)
                end_stage(dve, 1)

            if stages > 2:
                dve.wait_ge(sem("c_in"), 48)
                dve.wait_ge(sem("weights_hi"), HI_BEFORE["c"] + 2)
                k(dve.tensor_tensor(c_ctx_lo[:, :], c_ctxT[:, :], c_ctx_hi[:, :].bitcast(F32), ALU.subtract))
                dve.tensor_tensor(c_w_lo[:, :, :], c_w[:, :, :], c_w_hi[:, :, :].bitcast(F32), ALU.subtract).then_inc(sem("weights"), 1)
                dve.wait_ge(sem("c_g"), 1)
                k(dve.tensor_scalar(c_g[:, 1:2], c_g[:, 1:2], 1.0, None, ALU.add))
                k(dve.reciprocal(c_g[:, 1:2], c_g[:, 1:2]))
                k(dve.tensor_scalar(c_g[:, 2:3], c_g[:, 1:2], -1.0, 1.0, ALU.mult, ALU.add))
                k(dve.tensor_tensor(c_g[:, 2:3], c_g[:, 2:3], tg[:, 1:2], ALU.mult))
                k(dve.tensor_scalar(c_g[:, 3:4], c_g[:, 1:2], 0.5, None, ALU.mult))
                k(dve.tensor_tensor(c_g[:, 3:4], c_g[:, 3:4], tg[:, 1:2], ALU.mult))
                with dve.Fori(0, B) as i:
                    per = 2 * TB + 2 * TB + 3 + SIM_STEPS * 8 + 3 * TB + 2 * TB
                    o = k.enter(i, per)
                    norm_vector(dve, k, "c", i)
                    for w in range(2):
                        dve.wait_ge(sem("c_qk_hi"), i * 2 + w + 1)
                        dve.tensor_tensor(c_qk_lo[:, w, :], ps[:, 2 + w, :], c_qk_hi[:, w, :].bitcast(F32), ALU.subtract)\
                            .then_inc(sem("c_qk"), 1)
                    low, step, cand, cnt, take = (c_tk[:, r, :] for r in range(5))
                    dve.wait_ge(sem("c_sim"), TB * (i + 1))
                    for j in range(TB):
                        k(dve.tensor_reduce(step[:, j:j + 1], c_sim[:, j, :], AX.X, ALU.max))
                        k(dve.tensor_reduce(low[:, j:j + 1], c_sim[:, j, :], AX.X, ALU.min))
                    k(dve.tensor_tensor(step, step, low, ALU.subtract))
                    k(dve.tensor_scalar(step, step, 0.5, None, ALU.mult))
                    k(dve.tensor_tensor(cand, low, step, ALU.add))
                    plain(dve)
                    with dve.Fori(0, SIM_STEPS) as r:
                        p2 = k.enter(r, 8)
                        for j in range(TB):
                            k(dve.tensor_scalar(c_junk[:, 0, :], c_sim[:, j, :], cand[:, j:j + 1], 0.0, ALU.is_ge, ALU.add,
                                                accum_out=cnt[:, j:j + 1]))
                        k(dve.scalar_tensor_tensor(take, cnt, float(SIM_K), step, ALU.is_ge, ALU.mult))
                        k(dve.tensor_tensor(low, low, take, ALU.add))
                        k(dve.tensor_scalar(step, step, 0.5, None, ALU.mult))
                        k(dve.tensor_tensor(cand, low, step, ALU.add))
                        k.leave(p2, SIM_STEPS, 8)
                    dve.wait_ge(sem("c_e"), TB * (i + 1))
                    for j in range(TB):
                        k(dve.tensor_scalar(c_a[:, j, :], c_a[:, j, :], 1.0, None, ALU.add))
                        k(dve.reciprocal(c_a[:, j, :], c_a[:, j, :]))
                        k(dve.scalar_tensor_tensor(c_a[:, j, :], c_sim[:, j, :], low[:, j:j + 1], c_a[:, j, :], ALU.is_ge, ALU.mult))
                    dve.sem_inc(sem("c_A"), 1)
                    for j in range(TB):
                        n = i * TB + j
                        k(dve.scalar_tensor_tensor(X[:, n, :], xn[:, j, :], c_g[:, 2:3], X[:, n, :], ALU.mult, ALU.add))
                        dve.wait_ge(sem("c_AT_ps"), n + 1)
                        dve.tensor_tensor(c_t[:, :], ps[:, 6 + j % 2, :], c_a[:, j, :], ALU.add).then_inc(sem("c_AT_used"), 1)
                        dve.wait_ge(sem("c_AT_used"), n + 1)
                        k(dve.scalar_tensor_tensor(X[:, n, :], c_t[:, :], c_g[:, 3:4], X[:, n, :], ALU.mult, ALU.add))
                    k.leave(o, B, per)
                end_stage(dve, 2)

            if stages > 3:
                dve.wait_ge(sem("d_in"), 48)
                for c in range(C):
                    dve.tensor_tensor(d_w[:, c, :], d_w[:, c, :], d_rows[:, 0, :], ALU.mult).then_inc(sem("d_ws"), 1)
                k(dve.tensor_scalar(d_rows[:, 1, :], d_rows[:, 1, :], tg[:, 5:6], None, ALU.mult))
                dve.wait_ge(sem("weights_hi"), HI_BEFORE["d"] + 1)
                dve.tensor_tensor(d_w_lo[:, :, :], d_w[:, :, :], d_w_hi[:, :, :].bitcast(F32), ALU.subtract).then_inc(sem("weights"), 1)
                with dve.Fori(0, B) as i:
                    per = 2 * TB + TB
                    o = k.enter(i, per)
                    norm_vector(dve, k, "d", i)
                    for j in range(TB):
                        n = i * TB + j
                        k(dve.tensor_tensor(X[:, n, :], X[:, n, :], d_rows[:, 1, :], ALU.add))
                        dve.wait_ge(sem("y_ps"), n + 1)
                        dve.scalar_tensor_tensor(X[:, n, :], ps[:, 2 + j % 2, :], tg[:, 5:6], X[:, n, :], ALU.mult, ALU.add)\
                            .then_inc(sem("y_used"), 1)
                    dve.wait_ge(sem("y_used"), TB * (i + 1))
                    k.leave(o, B, per)
                end_stage(dve, 3)

            if stages > 4:
                dve.wait_ge(sem("e_tables"), 32)
                dve.memset(e_zero[:, :].bitcast(F32), 0.0).then_inc(sem("e_zero"), 1)

                def e_qk_vector(turn, d):
                    u = d % 2
                    for w in range(2):
                        dve.wait_ge(sem("qk_hi"), turn * E_BODY + d * 2 + w + 1)
                        dve.tensor_tensor(e_qk_lo[:, u, w, :], ps[:, 2 + w, :], e_qk_hi[:, u, w, :].bitcast(F32), ALU.subtract)\
                            .then_inc(sem("qk"), 1)

                def e_max_vector(h, a):
                    for t in range(TB):
                        dve.wait_ge(sem("scores_ps"), h * TB + t + 1)
                        dve.tensor_reduce(e_st[:, a, t:t + 1], ps[:, t % 2, :], AX.X, ALU.max, negate=True).then_inc(sem("score_max"), 1)

                def e_scale_vector(h, a):
                    dve.wait_ge(sem("exp"), TB * (h + 1))
                    k(dve.reciprocal(e_st[:, a, 8:12], e_st[:, a, 4:8]))
                    for t in range(TB):
                        dve.tensor_scalar(e_p[:, a, t, :], e_p[:, a, t, :], e_st[:, a, 8 + t:9 + t], None, ALU.mult).then_inc(sem("e_p"), 1)

                def e_head_vector(turn, hh, tail):
                    h = turn * E_BODY + hh
                    more = not (tail and hh == E_BODY - 1)
                    if more:
                        e_max_vector(h + 1, (hh + 1) % 2)
                    for c in range(TB):
                        dve.wait_ge(sem("pT_hi"), h * TB + c + 1)
                        dve.tensor_tensor(e_pT_lo[:, c, :], ps[:, 2 + c % 2, :], e_pT_hi[:, c, :].bitcast(F32), ALU.subtract)\
                            .then_inc(sem("pT"), 1)
                    if more:
                        e_scale_vector(h + 1, (hh + 1) % 2)
                    dve.wait_ge(sem("head_hi"), h + 1)
                    dve.tensor_tensor(e_cT_lo[:, hh % 2, :], ps[:, 1, :], e_cT_hi[:, hh % 2, :].bitcast(F32), ALU.subtract)\
                        .then_inc(sem("head_out"), 1)
                    if hh % 2 == 0 and not (tail and hh == E_BODY - 2):
                        e_qk_vector(turn, hh // 2 + 1)

                with dve.Fori(0, E_HEADS // 2) as i:
                    for u in range(2):
                        n = i * 2 + u
                        dve.wait_ge(sem("e_mg_hi"), 2 * (n + 1))
                        m_ = [e_qkw[:, 0, q, 0:4 * P].rearrange("p (c n) -> p c n", c=C)[:, :, u * E_R:(u + 1) * E_R] for q in range(2)]
                        g_ = [e_g[:, 0, q, u * D:(u + 1) * D] for q in range(2)]
                        dve.tensor_tensor(m_[1], ps[:, 1, 0:C * E_R].rearrange("p (c n) -> p c n", c=C), m_[0].bitcast(F32),
                                          ALU.subtract).then_inc(sem("e_mg"), 1)
                        dve.tensor_tensor(g_[1], ps[:, 2, :], g_[0].bitcast(F32), ALU.subtract).then_inc(sem("e_mg"), 1)
                    dve.wait_ge(sem("e_wkr_hi"), i + 1)
                    dve.wait_ge(sem("e_mg"), 4 * (i + 1) + 1)
                    dve.tensor_tensor(e_qkw[:, 0, 1, 4 * P:5 * P], e_wkr[:, :], e_qkw[:, 0, 0, 4 * P:5 * P].bitcast(F32), ALU.subtract)\
                        .then_inc(sem("e_pair_made"), 1)
                    dve.wait_ge(sem("e_pair_made"), i + 1)
                    dve.sem_inc(sem("e_blob_used"), 1)
                with dve.Fori(0, B) as i:
                    per = 2 * TB + 4 + E_HEADS
                    o = k.enter(i, per)
                    norm_vector(dve, k, "e", i)
                    dve.wait_ge(sem("e_ctx_in"), 16 * (i + 1))
                    hd = DC // 2
                    k(dve.tensor_tensor(e_rot[:, :, 0:hd], e_ctx[:, :, hd:DC], e_sin[:, :, 0:hd], ALU.mult))
                    k(dve.tensor_tensor(e_rot[:, :, hd:DC], e_ctx[:, :, 0:hd], e_sin[:, :, hd:DC], ALU.mult))
                    k(dve.tensor_tensor(e_kvr[:, :, :], e_ctx[:, :, :], e_cos[:, :, :], ALU.mult))
                    dve.tensor_tensor(e_kvr[:, :, :], e_kvr[:, :, :], e_rot[:, :, :], ALU.add).then_inc(sem("e_kvr"), 1)
                    dve.wait_ge(sem("e_kvr"), i + 1)
                    dve.sem_inc(sem("e_ctx_used"), 1)
                    dve.wait_ge(sem("e_kvr_hi"), i + 1)
                    k(dve.tensor_tensor(e_kvr_lo[:, :, :], e_kvr[:, :, :], e_kvr_hi[:, :, :].bitcast(F32), ALU.subtract))
                    dve.wait_ge(sem("e_kT_hi"), i + 1)
                    dve.tensor_tensor(e_kT_lo[:, :], ps[:, 2, :], e_kT_hi[:, :].bitcast(F32), ALU.subtract).then_inc(sem("e_kT"), 1)
                    plain(dve)
                    e_qk_vector(i * E_TURNS, 0)
                    e_max_vector(E_HEADS * i, 0)
                    e_scale_vector(E_HEADS * i, 0)
                    plain(dve)
                    with dve.Fori(0, E_TURNS - 1) as g:
                        p2 = k.enter(g, E_BODY)
                        for hh in range(E_BODY):
                            e_head_vector(i * E_TURNS + g, hh, False)
                        k.leave(p2, E_TURNS - 1, E_BODY)
                    for hh in range(E_BODY):
                        e_head_vector((i + 1) * E_TURNS - 1, hh, True)
                    dve.wait_ge(sem("e_y_ps"), i + 1)
                    for j in range(TB):
                        n = i * TB + j
                        dve.scalar_tensor_tensor(X[:, n, :], ps[:, 4 + j, :], tg[:, 2:3], X[:, n, :], ALU.mult, ALU.add)\
                            .then_inc(sem("e_y_used"), 1)
                    dve.wait_ge(sem("e_y_used"), TB * (i + 1))
                    k.leave(o, B, per)
                end_stage(dve, 4)

            if stages > 5:
                dve.wait_ge(sem("weights_hi"), HI_BEFORE["f"] + 2)
                k(dve.tensor_tensor(f_w_lo[:, :, :], f_w[:, :, :], f_w_hi[:, :, :].bitcast(F32), ALU.subtract))
                k(dve.tensor_tensor(f_d_lo[:, :], f_d[:, :], f_d_hi[:, :].bitcast(F32), ALU.subtract))
                dve.tensor_tensor(f_q[:, :, :], f_q[:, :, :], f_w[:, :, :], ALU.mult).then_inc(sem("weights"), 1)
                dve.wait_ge(sem("f_const_ps"), 1)
                k(dve.tensor_copy(f_const[:, :], ps[:, 2, 0:F_N]))
                with dve.Fori(0, B) as i:
                    per = 2 * TB + 36
                    o = k.enter(i, per)
                    norm_vector(dve, k, "f", i)
                    for j in range(TB):
                        n = i * TB + j
                        dve.wait_ge(sem("f_a_ps"), n + 1)
                        k(dve.tensor_tensor(f_a[:, j, 0:P], ps[:, 2 + j % 2, 0:P], f_const[:, 0:P], ALU.subtract))
                        dve.scalar_tensor_tensor(f_a[:, j, P:F_N], ps[:, 2 + j % 2, P:F_N], -2.0, f_const[:, P:F_N], ALU.mult, ALU.add)\
                            .then_inc(sem("f_a"), 1)
                    dve.wait_ge(sem("f_a"), TB * (i + 1))
                    k(dve.tensor_tensor(f_sq[:, :, :], f_a[:, :, 0:64], f_a[:, :, 0:64], ALU.mult))
                    score, pri = f_g[:, 2, :, :], f_g[:, 3, :, :]
                    k(dve.tensor_reduce(score, f_sq[:, :, :].rearrange("p t (n s) -> p t n s", n=8), AX.X, ALU.add))
                    dve.wait_ge(sem("f_xx"), TB * (i + 1))
                    for j in range(TB):
                        k(dve.tensor_scalar(f_a[:, j, P:F_N], f_a[:, j, P:F_N], f_xx[:, j:j + 1], None, ALU.add))
                    k(dve.reciprocal(f_g[:, 4, :, :], f_a[:, :, P:F_N]))
                    k(dve.tensor_tensor(score, score, f_g[:, 4, :, :], ALU.mult))
                    for j in range(TB):
                        k(dve.tensor_tensor(f_g[:, 4, j, :], score[:, j, :], f_rows[:, 0, :], ALU.subtract))
                    for j in range(TB):
                        k(dve.tensor_tensor(f_g[:, 0, j, :], f_g[:, 4, j, :], f_rows[:, 1, :], ALU.mult))
                    dve.sem_inc(sem("f_z"), 1)
                    dve.wait_ge(sem("f_e"), i + 1)
                    gate = f_g[:, 1, :, :]
                    k(dve.tensor_scalar(gate, gate, 1.0, None, ALU.add))
                    k(dve.reciprocal(gate, gate))
                    top = f_s[:, 0, :]
                    k(dve.tensor_reduce(top, gate, AX.X, ALU.max))
                    k(dve.tensor_tensor(pri, gate, top.unsqueeze(2).broadcast_to([P, TB, 8]), ALU.is_ge))
                    for j in range(TB):
                        k(dve.tensor_tensor(pri[:, j, :], pri[:, j, :], f_rows[:, 2, :], ALU.mult))
                    k(dve.tensor_reduce(f_s[:, 1, :], pri, AX.X, ALU.max))
                    hot = f_m[:, :, 64:72]
                    k(dve.tensor_tensor(hot, pri, f_s[:, 1, :].unsqueeze(2).broadcast_to([P, TB, 8]), ALU.is_equal))
                    for j in range(TB):
                        dve.tensor_tensor(f_m[:, j, 0:64].rearrange("p (n h) -> p n h", n=8),
                                          f_a[:, j, 64:P].rearrange("p (n h) -> p n h", n=8),
                                          hot[:, j, :].unsqueeze(2).broadcast_to([P, 8, 8]), ALU.mult).then_inc(sem("f_m"), 1)
                    k(dve.tensor_scalar(f_s[:, 2, :], top, tg[:, 6:7], None, ALU.mult))
                    k(dve.tensor_scalar(f_s[:, 3, :], f_s[:, 2, :], -1.0, tg[:, 6:7], ALU.mult, ALU.add))
                    dve.wait_ge(sem("f_mT_hi"), i + 1)
                    dve.tensor_tensor(f_mT_lo[:, :], ps[0:F_K, 4, :], f_mT_hi[:, :].bitcast(F32), ALU.subtract).then_inc(sem("f_mT"), 1)
                    for j in range(TB):
                        n = i * TB + j
                        k(dve.scalar_tensor_tensor(X[:, n, :], xn[:, j, :], f_s[:, 3, j:j + 1], X[:, n, :], ALU.mult, ALU.add))
                        dve.wait_ge(sem("y_ps"), 1 * TILES + n + 1)
                        dve.scalar_tensor_tensor(X[:, n, :], ps[:, 6 + j % 2, :], f_s[:, 2, j:j + 1], X[:, n, :], ALU.mult, ALU.add)\
                            .then_inc(sem("y_used"), 1)
                    dve.wait_ge(sem("y_used"), 1 * TILES + TB * (i + 1))
                    k.leave(o, B, per)
                end_stage(dve, 5)

            if stages > 6:
                for n, (dst, hi) in enumerate(((g_wq_lo, g_wq_hi), (g_wo_lo, g_wo_hi))):
                    dve.wait_ge(sem("weights_hi"), HI_BEFORE["g"] + n + 1)
                    dve.tensor_tensor(dst[:, :, :], g_w[:, :, :], hi[:, :, :].bitcast(F32), ALU.subtract).then_inc(sem("g_raw_used"), 1)
                dve.wait_ge(sem("weights_hi"), HI_BEFORE["g"] + 3)
                dve.wait_ge(sem("g_mask"), 1)
                dve.tensor_tensor(g_wkv_lo[:, :], g_w[:, 0:2, :].rearrange("p a n -> p (a n)"), g_wkv_hi[:, :].bitcast(F32), ALU.subtract)\
                    .then_inc(sem("weights"), 1)
                with dve.Fori(0, B) as i:
                    per = 2 * TB + C * 4 * 9
                    o = k.enter(i, per)
                    norm_vector(dve, k, "g", i)
                    dve.wait_ge(sem("g_ctx_hi"), i + 1)
                    dve.tensor_tensor(g_ctx_lo[:, :], g_ctxT[:, :], g_ctx_hi[:, :].bitcast(F32), ALU.subtract).then_inc(sem("g_ctx_used"), 1)
                    for t in range(TB):
                        dve.wait_ge(sem("g_v_hi"), i * TB + t + 1)
                        dve.tensor_tensor(g_v_lo[:, t, :], ps[:, 6 + t % 2, :], g_v_hi[:, t, :].bitcast(F32), ALU.subtract).then_inc(sem("g_v"), 1)
                    plain(dve)
                    with dve.Fori(0, C) as g:
                        p2 = k.enter(g, 4 * 9)
                        n = i * C + g
                        for w, src in enumerate((g_qT, g_kT)):
                            dve.wait_ge(sem("qk_hi"), G_HEADS_BEFORE + n * 2 + w + 1)
                            dve.tensor_tensor(g_qk_lo[:, w, :], src[:, g, :], g_qk_hi[:, w, :].bitcast(F32), ALU.subtract).then_inc(sem("qk"), 1)
                        for hh in range(4):
                            h = G_HEADS_BEFORE + n * 4 + hh
                            for t in range(TB):
                                dve.wait_ge(sem("scores_ps"), h * TB + t + 1)
                                dg = ps[:, t % 2, t * P:(t + 1) * P]
                                k(dve.tensor_tensor(dg, dg, g_mask[:, :], ALU.add))
                                k(dve.tensor_reduce(g_st[:, 12 + t:13 + t], ps[:, t % 2, 0:(t + 1) * P], AX.X, ALU.max, negate=True))
                                dve.tensor_scalar(g_st[:, t:t + 1], g_st[:, 12 + t:13 + t], G_SCALE, None, ALU.mult).then_inc(sem("score_max"), 1)
                            dve.wait_ge(sem("exp"), TB * (h + 1))
                            k(dve.reciprocal(g_st[:, 8:12], g_st[:, 4:8]))
                            for c in range(TB):
                                dve.wait_ge(sem("pT_hi"), h * TB + c + 1)
                                dve.tensor_tensor(g_pT_lo[:, c, c * P:], ps[:, 2 + c % 2, c * P:], g_pT_hi[:, c, c * P:].bitcast(F32), ALU.subtract)\
                                    .then_inc(sem("pT"), 1)
                            dve.wait_ge(sem("head_ps"), h + 1)
                            dve.tensor_tensor(g_o[:, :, bass.ds(g * P + hh * G_HD, G_HD)], ps[:, 4, 0:TB * G_HD].rearrange("p (t d) -> p t d", t=TB),
                                              g_st[:, 8:12].unsqueeze(2).broadcast_to([P, TB, G_HD]), ALU.mult).then_inc(sem("head_out"), 1)
                            dve.wait_ge(sem("head_out"), h + 1)
                        k.leave(p2, C, 4 * 9)
                    for j in range(TB):
                        dve.sem_inc(sem("ln_xn"), 1)
                    for j in range(TB):
                        dve.wait_ge(sem("ln_xT_hi"), TB * xT_turn("g2", i) + j + 1)
                        q = slice(j * P, (j + 1) * P)
                        dve.tensor_tensor(xT_lo[:, :, q], ps[:, j % 2, :].rearrange("p (c t) -> p c t", c=C),
                                          xT_hi[:, :, q].bitcast(F32), ALU.subtract).then_inc(sem("ln_xT"), 1)
                    for j in range(TB):
                        n = i * TB + j
                        dve.wait_ge(sem("y_ps"), 2 * TILES + n + 1)
                        dve.scalar_tensor_tensor(X[:, n, :], ps[:, 2 + j % 2, :], tg[:, 3:4], X[:, n, :], ALU.mult, ALU.add)\
                            .then_inc(sem("y_used"), 1)
                    dve.wait_ge(sem("y_used"), 2 * TILES + TB * (i + 1))
                    k.leave(o, B, per)
                end_stage(dve, 6)

            if stages > 7:
                dve.wait_ge(sem("weights_hi"), HI_BEFORE["h"] + 1)
                dve.memset(h_zero[:, :].bitcast(F32), 0.0).then_inc(sem("h_zero"), 1)
                dve.tensor_tensor(h_gw_lo[:, :, :], h_gw[:, :, :], h_gw_hi[:, :, :].bitcast(F32), ALU.subtract).then_inc(sem("weights"), 1)

                def h_split_vector(n, u):
                    dve.wait_ge(sem(f"h_w_hi{u}"), n + 1)
                    dve.tensor_tensor(h_w_lo[:, u, :], h_w[:, u, :], h_w_hi[:, u, :].bitcast(F32), ALU.subtract).then_inc(sem(f"h_w_used{u}"), 1)

                def h_hidden_vector(n, u):
                    dve.wait_ge(sem(f"h_sg{u}"), n + 1)
                    dve.tensor_tensor(h_h[:, u, :], ps[:, 2 + u, :], h_sg[:, u, :], ALU.mult).then_inc(sem(f"h_h{u}"), 1)
                    dve.wait_ge(sem(f"h_h_hi{u}"), n + 1)
                    dve.tensor_tensor(h_h_lo[:, u, :], h_h[:, u, :], h_h_hi[:, u, :].bitcast(F32), ALU.subtract).then_inc(sem(f"h_h_lo{u}"), 1)

                with dve.Fori(0, B) as i:
                    per = 2 * TB + 9
                    o = k.enter(i, per)
                    norm_vector(dve, k, "h", i)
                    dve.wait_ge(sem("h_l_ps"), i + 1)
                    k(dve.tensor_copy(h_l[:, 0, :, :], ps[:, 0, 0:2 * TB].rearrange("p (t e) -> p t e", t=TB)))
                    k(dve.tensor_reduce(h_s[:, 0, :], h_l[:, 0, :, :], AX.X, ALU.max))
                    dve.tensor_tensor(h_l[:, 1, :, :], h_l[:, 0, :, :], h_s[:, 0, :].unsqueeze(2).broadcast_to([P, TB, 2]), ALU.subtract)\
                        .then_inc(sem("h_logit"), 1)
                    dve.wait_ge(sem("h_le"), i + 1)
                    ee = h_l[:, 2, :, :]
                    k(dve.tensor_reduce(h_s[:, 1, :], ee, AX.X, ALU.add))
                    k(dve.reciprocal(h_s[:, 1, :], h_s[:, 1, :]))
                    k(dve.tensor_tensor(h_l[:, 3, :, :], ee, h_s[:, 1, :].unsqueeze(2).broadcast_to([P, TB, 2]), ALU.mult))
                    p0, p1 = h_l[:, 3, :, 0], h_l[:, 3, :, 1]
                    k(dve.tensor_tensor(h_l[:, 4, :, 1], p1, p0, ALU.is_gt))
                    k(dve.tensor_scalar(h_l[:, 4, :, 0], h_l[:, 4, :, 1], -1.0, 1.0, ALU.mult, ALU.add))
                    k(dve.tensor_tensor(h_l[:, 5, :, :], h_l[:, 4, :, :], h_l[:, 3, :, :], ALU.mult))
                    k(dve.tensor_scalar(h_l[:, 5, :, :], h_l[:, 5, :, :], tg[:, 7:8], None, ALU.mult))
                    for e in range(2):
                        first = (i * 2 + e) * (HC // 2)
                        h_split_vector(first, 0)
                        plain(dve)
                        with dve.Fori(0, HC // 2 - 1) as f:
                            n = first + f
                            h_split_vector(n, 1)
                            h_hidden_vector(n, 0)
                            h_split_vector(n + 1, 0)
                            h_hidden_vector(n, 1)
                        last = first + HC // 2 - 1
                        h_split_vector(last, 1)
                        h_hidden_vector(last, 0)
                        h_hidden_vector(last, 1)
                        dve.wait_ge(sem("h_y_ps"), i * 2 + e + 1)
                        for j in range(TB):
                            n = i * TB + j
                            dve.scalar_tensor_tensor(X[:, n, :], ps[:, 4 + j, :], h_l[:, 5, j, e:e + 1], X[:, n, :], ALU.mult, ALU.add)\
                                .then_inc(sem("h_y_used"), 1)
                        dve.wait_ge(sem("h_y_used"), TB * (i * 2 + e + 1))
                    k.leave(o, B, per)
                end_stage(dve, 7)

        @block.tensor
        def _(pe):
            pe.wait_ge(sem("consts"), 1)
            pe.wait_ge(sem("weights"), READY["a"])
            with pe.Fori(0, B) as i:
                norm_tensor(pe, "a", i)
                mm3(pe, ps[:, 2, :], a_wk_hi[:, :], a_wk_lo[:, :], a_ctx_hi[:, bass.ts(i, S)], a_ctx_lo[:, bass.ts(i, S)],
                    True, True).then_inc(sem("a_kvT_ps"), 1)
                pe.wait_ge(sem("a_kvT"), i + 1)
                for j in range(TB):
                    t = pe.transpose(ps[:, 3, j * P:(j + 1) * P], a_kvT[:, j * P:(j + 1) * P], ident[:, :])
                t.then_inc(sem("a_kv_ps"), 1)
                pe.wait_ge(sem("a_kv"), i + 1)
                for j in range(TB):
                    t = mm3(pe, ps[:, 4, :], a_kv_hi[:, j, :], a_kv_lo[:, j, :], xT_hi[:, j, :], xT_lo[:, j, :], j == 0, j == TB - 1)
                t.then_inc(sem("a_oT_ps"), 1)
                pe.wait_ge(sem("a_oT"), i + 1)
                for j in range(TB):
                    if j >= 2:
                        pe.wait_ge(sem("a_sim_used"), i * TB + j - 1)
                    q = slice(j * P, (j + 1) * P)
                    mm3(pe, ps[:, 5 + j % 2, :], a_oT_hi[:, q], a_oT_lo[:, q], a_kvT_hi[:, :], a_kvT_lo[:, :], True, True)\
                        .then_inc(sem("a_sim_ps"), 1)
            end_stage(pe, 0)
            if stages > 1:
                for w in range(2):
                    pe.wait_ge(sem("b_abs"), w + 1)
                    pe.matmul(ps[:, 2, 0:1], ones[:, :], b_st[:, w:w + 1], start=True, stop=True).then_inc(sem("b_abs_ps"), 1)
                pe.wait_ge(sem("weights"), READY["b"])
                with pe.Fori(0, B) as i:
                    norm_tensor(pe, "b", i)
                    for j in range(TB):
                        for q in range(4):
                            n = (i * TB + j) * 4 + q
                            if j >= 1:
                                pe.wait_ge(sem("b_z_used"), n - 3)
                            for c in range(C):
                                for part in (xT_hi, xT_lo):
                                    t = pe.matmul(ps[:, 4 + q, :], part[:, c, j * P:(j + 1) * P], b_tsyn[:, c, q * BANK:(q + 1) * BANK],
                                                  start=(c == 0 and part is xT_hi), stop=(c == C - 1 and part is xT_lo))
                            t.then_inc(sem("b_z_ps"), 1)
                    for j in range(TB):
                        n = i * TB + j
                        pe.wait_ge(sem("b_h"), n + 1)
                        for q in range(4):
                            for c in range(4):
                                t = pe.transpose(ps[:, q, c * P:(c + 1) * P], b_z[:, j, (4 * q + c) * P:(4 * q + c + 1) * P], ident[:, :])
                            t.then_inc(sem("b_hT_ps"), 1)
                        pe.wait_ge(sem("b_hT"), 4 * (n + 1))
                        for c in range(HC):
                            for part in (b_hT_hi, b_hT_lo):
                                t = pe.matmul(ps[:, 4, :], part[:, c, :], b_tout[:, c, :],
                                              start=(c == 0 and part is b_hT_hi), stop=(c == HC - 1 and part is b_hT_lo))
                        t.then_inc(sem("b_y_ps"), 1)
                        pe.wait_ge(sem("b_y_used"), n + 1)
                end_stage(pe, 1)
            if stages > 2:
                pe.wait_ge(sem("weights"), READY["c"])
                with pe.Fori(0, B) as i:
                    norm_tensor(pe, "c", i)
                    for w in range(2):
                        mm3(pe, ps[:, 2 + w, :], c_w_hi[:, w, :], c_w_lo[:, w, :], c_ctx_hi[:, bass.ts(i, S)],
                            c_ctx_lo[:, bass.ts(i, S)], True, True).then_inc(sem("c_qk_ps"), 1)
                    pe.wait_ge(sem("c_qk"), 2 * (i + 1))
                    for j in range(TB):
                        if j >= 2:
                            pe.wait_ge(sem("c_sim"), i * TB + j - 1)
                        q = slice(j * P, (j + 1) * P)
                        mm3(pe, ps[:, 4 + j % 2, :], c_qk_hi[:, 0, q], c_qk_lo[:, 0, q], c_qk_hi[:, 1, :], c_qk_lo[:, 1, :],
                            True, True).then_inc(sem("c_sim_ps"), 1)
                    pe.wait_ge(sem("c_A"), i + 1)
                    for j in range(TB):
                        if j >= 2:
                            pe.wait_ge(sem("c_AT_used"), i * TB + j - 1)
                        for c in range(TB):
                            t = pe.transpose(ps[:, 6 + j % 2, c * P:(c + 1) * P], c_a[:, c, j * P:(j + 1) * P], ident[:, :])
                        t.then_inc(sem("c_AT_ps"), 1)
                    pe.wait_ge(sem("c_AT_used"), TB * (i + 1))
                end_stage(pe, 2)
            if stages > 3:
                pe.wait_ge(sem("weights"), READY["d"])
                with pe.Fori(0, B) as i:
                    norm_tensor(pe, "d", i)
                    for j in range(TB):
                        if j >= 2:
                            pe.wait_ge(sem("y_used"), i * TB + j - 1)
                        q = slice(j * P, (j + 1) * P)
                        for c in range(C):
                            t = mm3(pe, ps[:, 2 + j % 2, :], xT_hi[:, c, q], xT_lo[:, c, q], d_w_hi[:, c, :], d_w_lo[:, c, :],
                                    c == 0, c == C - 1)
                        t.then_inc(sem("y_ps"), 1)
                    pe.wait_ge(sem("y_used"), TB * (i + 1))
                end_stage(pe, 3)
            if stages > 4:
                def e_qk_tensor(turn, d):
                    u = d % 2
                    pe.wait_ge(sem(f"e_qkw_in{u}"), 16 * (turn + d // 2 + 1))
                    w = [e_qkw[:, u, q, :] for q in range(2)]
                    for c in range(C):
                        t = mm3(pe, ps[:, 2, :], w[0][:, c * P:(c + 1) * P], w[1][:, c * P:(c + 1) * P], xT_hi[:, c, :], xT_lo[:, c, :],
                                c == 0, c == C - 1)
                    t.then_inc(sem("qk_ps"), 1)
                    t = mm3(pe, ps[:, 3, :], w[0][:, 4 * P:5 * P], w[1][:, 4 * P:5 * P], e_kT_hi[:, :], e_kT_lo[:, :], True, True)
                    t.then_inc(sem("qk_ps"), 1)

                def e_scores_tensor(h, a, u, first=False):
                    r = slice(a * E_R, (a + 1) * E_R)
                    for t_ in range(TB):
                        if t_ >= 2 or not first:
                            pe.wait_ge(sem("exp"), h * TB + t_ - 1)
                        q = slice(t_ * P, (t_ + 1) * P)
                        mm3(pe, ps[:, t_ % 2, :], e_qk_hi[r, u, 0, q], e_qk_lo[r, u, 0, q], e_qk_hi[r, u, 1, :], e_qk_lo[r, u, 1, :], True, True)\
                            .then_inc(sem("scores_ps"), 1)

                def e_out_tensor(turn, hh):
                    pe.wait_ge(sem("head_out"), turn * E_BODY + hh + 1)
                    u, a = hh // 2, hh % 2
                    if a == 0:
                        pe.wait_ge(sem(f"e_g_in{u}"), 16 * (turn + 1))
                    gw = [e_g[:, u, q, a * D:(a + 1) * D] for q in range(2)]
                    for j in range(TB):
                        q = slice(j * P, (j + 1) * P)
                        for l, r in ((e_cT_hi, 0), (e_cT_hi, 1), (e_cT_lo, 0)):
                            t = pe.matmul(ps[:, 4 + j, :], l[:, a, q], gw[r], start=False, stop=False, skip_group_check=True)
                    if a == 1:
                        t.then_inc(sem(f"e_g_used{u}"), 1)

                def e_head_tensor(turn, hh, tail):
                    h = turn * E_BODY + hh
                    more = not (tail and hh == E_BODY - 1)
                    if more:
                        if hh % 2 == 1:
                            pe.wait_ge(sem("qk"), turn * E_BODY + 2 * ((hh + 1) // 2 + 1))
                        e_scores_tensor(h + 1, (hh + 1) % 2, (hh + 1) // 2 % 2)
                    for c in range(TB):
                        if c >= 2:
                            pe.wait_ge(sem("pT"), h * TB + c - 1)
                        for t_ in range(TB):
                            if c == 0:
                                pe.wait_ge(sem("e_p"), h * TB + t_ + 1)
                            t = pe.transpose(ps[:, 2 + c % 2, t_ * P:(t_ + 1) * P], e_p[:, hh % 2, t_, c * P:(c + 1) * P], ident[:, :])
                        t.then_inc(sem("pT_ps"), 1)
                    if more:
                        pe.wait_ge(sem("exp"), (h + 2) * TB)
                    for c in range(TB):
                        pe.wait_ge(sem("pT"), h * TB + c + 1)
                        t = mm3(pe, ps[:, 1, :], e_kvr_hi[:, c, :], e_kvr_lo[:, c, :], e_pT_hi[:, c, :], e_pT_lo[:, c, :], c == 0, c == TB - 1)
                    t.then_inc(sem("head_ps"), 1)
                    if hh:
                        e_out_tensor(turn, hh - 1)
                    if hh == E_BODY - 1:
                        e_out_tensor(turn, hh)
                    if hh % 2 == 0 and not (tail and hh == E_BODY - 2):
                        e_qk_tensor(turn, hh // 2 + 1)
                    pe.wait_ge(sem("head_out"), h + 1)

                with pe.Fori(0, E_HEADS // 2) as i:
                    for u in range(2):
                        n = i * 2 + u
                        if u == 0:
                            pe.wait_ge(sem("e_blob_in"), 32 * (i + 1))
                        raw = e_blob[:, u, :]
                        kcq, wqr, wq, wkv, wo = (raw[:, a:b] for a, b in zip(E_CUTS, E_CUTS[1:]))
                        for c in range(3):
                            t = pe.matmul(ps[:, 0, 0:E_R], kcq[:, c * P:(c + 1) * P], wqr[:, c * E_R:(c + 1) * E_R], start=c == 0, stop=c == 2)
                        t.then_inc(sem("e_u_ps"), 1)
                        pe.wait_ge(sem("e_mg"), 2 * n + 1)
                        pe.matmul(ps[:, 2, :], wkv, wo, start=True, stop=True)
                        pe.wait_ge(sem("e_u"), n + 1)
                        for c in range(C):
                            t = pe.matmul(ps[:, 1, c * E_R:(c + 1) * E_R], wq[:, c * P:(c + 1) * P], e_u[:, u, :], start=True, stop=True)
                        t.then_inc(sem("e_mg_ps"), 1)
                    pe.wait_ge(sem("e_mg"), 4 * (i + 1) + 1)
                with pe.Fori(0, B) as i:
                    norm_tensor(pe, "e", i)
                    pe.wait_ge(sem("e_kvr"), i + 1)
                    for t_ in range(TB):
                        t = pe.transpose(ps[:, 2, t_ * P:(t_ + 1) * P], e_kvr[:, t_, :], ident[:, :])
                    t.then_inc(sem("e_kT_ps"), 1)
                    pe.wait_ge(sem("e_kT"), i + 1)
                    pe.wait_ge(sem("e_zero"), 1)
                    for j in range(TB):
                        pe.matmul(ps[:, 4 + j, :], e_zero[:, 0:P], e_zero[:, :], start=True, stop=False, skip_group_check=True)
                    e_qk_tensor(i * E_TURNS, 0)
                    pe.wait_ge(sem("qk"), i * E_HEADS + 2)
                    e_scores_tensor(i * E_HEADS, 0, 0, True)
                    plain(pe)
                    with pe.Fori(0, E_TURNS - 1) as g:
                        for hh in range(E_BODY):
                            e_head_tensor(i * E_TURNS + g, hh, False)
                    for hh in range(E_BODY):
                        e_head_tensor((i + 1) * E_TURNS - 1, hh, True)
                    for j in range(TB):
                        t = pe.matmul(ps[:, 4 + j, :], e_zero[:, 0:P], e_zero[:, :], start=False, stop=True, skip_group_check=True)
                    t.then_inc(sem("e_y_ps"), 1)
                    pe.wait_ge(sem("e_y_used"), TB * (i + 1))
                end_stage(pe, 4)
            if stages > 5:
                pe.wait_ge(sem("weights"), READY["f"])
                for c in range(C):
                    t = pe.matmul(ps[:, 2, 0:F_N], ones[:, :], f_q[:, c, :], start=c == 0, stop=c == C - 1)
                t.then_inc(sem("f_const_ps"), 1)
                with pe.Fori(0, B) as i:
                    norm_tensor(pe, "f", i)
                    for j in range(TB):
                        if j >= 2:
                            pe.wait_ge(sem("f_a"), i * TB + j - 1)
                        q = slice(j * P, (j + 1) * P)
                        for c in range(C):
                            t = mm3(pe, ps[:, 2 + j % 2, 0:F_N], xT_hi[:, c, q], xT_lo[:, c, q], f_w_hi[:, c, :], f_w_lo[:, c, :], c == 0, c == C - 1)
                        t.then_inc(sem("f_a_ps"), 1)
                    pe.wait_ge(sem("f_m"), TB * (i + 1))
                    for j in range(TB):
                        t = pe.transpose(ps[0:F_K, 4, j * P:(j + 1) * P], f_m[:, j, :], ident[:, :])
                    t.then_inc(sem("f_mT_ps"), 1)
                    pe.wait_ge(sem("f_mT"), i + 1)
                    for j in range(TB):
                        if j >= 2:
                            pe.wait_ge(sem("y_used"), 1 * TILES + i * TB + j - 1)
                        q = slice(j * P, (j + 1) * P)
                        mm3(pe, ps[:, 6 + j % 2, :], f_mT_hi[:, q], f_mT_lo[:, q], f_d_hi[:, :], f_d_lo[:, :], True, True).then_inc(sem("y_ps"), 1)
                    pe.wait_ge(sem("y_used"), 1 * TILES + TB * (i + 1))
                end_stage(pe, 5)
            if stages > 6:
                pe.wait_ge(sem("weights"), READY["g"])
                with pe.Fori(0, B) as i:
                    norm_tensor(pe, "g", i)
                    pe.wait_ge(sem("g_ctx_used"), i + 2)
                    for m_ in range(C):
                        q = slice(m_ * P, (m_ + 1) * P)
                        if m_ >= 2:
                            pe.wait_ge(sem("g_q"), i * C + m_ - 1)
                        for c in range(C):
                            t = mm3(pe, ps[:, 2 + m_ % 2, :], g_wq_hi[:, c, q], g_wq_lo[:, c, q], xT_hi[:, c, :], xT_lo[:, c, :], c == 0, c == C - 1)
                        t.then_inc(sem("g_q_ps"), 1)
                        if m_ >= 2:
                            pe.wait_ge(sem("g_k"), i * C + m_ - 1)
                        mm3(pe, ps[:, 4 + m_ % 2, :], g_wkv_hi[:, q], g_wkv_lo[:, q], g_ctx_hi[:, :], g_ctx_lo[:, :], True, True).then_inc(sem("g_k_ps"), 1)
                    for t_ in range(TB):
                        q = slice(t_ * P, (t_ + 1) * P)
                        if t_ >= 2:
                            pe.wait_ge(sem("g_v"), i * TB + t_ - 1)
                        mm3(pe, ps[:, 6 + t_ % 2, :], g_ctx_hi[:, q], g_ctx_lo[:, q], g_wkv_hi[:, D:], g_wkv_lo[:, D:], True, True).then_inc(sem("g_v_ps"), 1)
                    pe.wait_ge(sem("g_k"), C * (i + 1))
                    pe.wait_ge(sem("g_v"), TB * (i + 1))
                    plain(pe)
                    with pe.Fori(0, C) as g:
                        n = i * C + g
                        pe.wait_ge(sem("qk"), G_HEADS_BEFORE + 2 * (n + 1))
                        for hh in range(4):
                            h = G_HEADS_BEFORE + n * 4 + hh
                            r = slice(hh * G_HD, (hh + 1) * G_HD)
                            for t_ in range(TB):
                                if t_ >= 2:
                                    pe.wait_ge(sem("exp"), h * TB + t_ - 1)
                                q, w = slice(t_ * P, (t_ + 1) * P), (t_ + 1) * P
                                mm3(pe, ps[:, t_ % 2, 0:w], g_qk_hi[r, 0, q], g_qk_lo[r, 0, q], g_qk_hi[r, 1, 0:w], g_qk_lo[r, 1, 0:w], True, True)\
                                    .then_inc(sem("scores_ps"), 1)
                            pe.wait_ge(sem("exp"), TB * (h + 1))
                            for c in range(TB):
                                if c >= 2:
                                    pe.wait_ge(sem("pT"), h * TB + c - 1)
                                for t_ in range(c, TB):
                                    t = pe.transpose(ps[:, 2 + c % 2, t_ * P:(t_ + 1) * P], g_p[:, t_, c * P:(c + 1) * P], ident[:, :])
                                t.then_inc(sem("pT_ps"), 1)
                            pe.wait_ge(sem("pT"), TB * (h + 1))
                            pe.wait_ge(sem("head_out"), h)
                            vcol = bass.ds(g * P + hh * G_HD, G_HD)
                            for t_ in range(TB):
                                q = slice(t_ * P, (t_ + 1) * P)
                                for c in range(t_ + 1):
                                    t = mm3(pe, ps[:, 4, t_ * G_HD:(t_ + 1) * G_HD], g_pT_hi[:, c, q], g_pT_lo[:, c, q],
                                            g_v_hi[:, c, vcol], g_v_lo[:, c, vcol], c == 0, c == t_)
                            t.then_inc(sem("head_ps"), 1)
                    norm_tensor(pe, "g2", i)
                    for j in range(TB):
                        if j >= 2:
                            pe.wait_ge(sem("y_used"), 2 * TILES + i * TB + j - 1)
                        q = slice(j * P, (j + 1) * P)
                        for c in range(C):
                            t = mm3(pe, ps[:, 2 + j % 2, :], xT_hi[:, c, q], xT_lo[:, c, q], g_wo_hi[:, c, :], g_wo_lo[:, c, :], c == 0, c == C - 1)
                        t.then_inc(sem("y_ps"), 1)
                    pe.wait_ge(sem("y_used"), 2 * TILES + TB * (i + 1))
                end_stage(pe, 6)
            if stages > 7:
                pe.wait_ge(sem("weights"), READY["h"])
                pe.wait_ge(sem("h_zero"), 1)

                def h_gate_up(n, u):
                    pe.wait_ge(sem(f"h_w_used{u}"), n + 2)
                    pe.wait_ge(sem(f"h_h{u}"), n + 1)
                    for w in range(2):
                        for c in range(C):
                            q = slice(w * D + c * P, w * D + (c + 1) * P)
                            t = mm3(pe, ps[:, 2 * w + u, :], h_w_hi[:, u, q], h_w_lo[:, u, q], xT_hi[:, c, :], xT_lo[:, c, :], c == 0, c == C - 1)
                    t.then_inc(sem(f"h_gu_ps{u}"), 1)

                def h_down(n, u):
                    pe.wait_ge(sem(f"h_h_lo{u}"), n + 1)
                    for j in range(TB):
                        q = slice(j * P, (j + 1) * P)
                        for a, b in ((h_h_hi, h_w_hi), (h_h_hi, h_w_lo), (h_h_lo, h_w_hi)):
                            t = pe.matmul(ps[:, 4 + j, :], a[:, u, q], b[:, u, 2 * D:], start=False, stop=False, skip_group_check=True)
                    t.then_inc(sem(f"h_down{u}"), 1)

                with pe.Fori(0, B) as i:
                    norm_tensor(pe, "h", i)
                    for j in range(TB):
                        q = slice(j * P, (j + 1) * P)
                        for c in range(C):
                            t = mm3(pe, ps[:, 0, 2 * j:2 * j + 2], xT_hi[:, c, q], xT_lo[:, c, q], h_gw_hi[:, c, :], h_gw_lo[:, c, :], c == 0, c == C - 1)
                    t.then_inc(sem("h_l_ps"), 1)
                    pe.wait_ge(sem("h_logit"), i + 1)
                    for e in range(2):
                        for j in range(TB):
                            pe.matmul(ps[:, 4 + j, :], h_zero[:, 0:P], h_zero[:, :], start=True, stop=False, skip_group_check=True)
                        first = (i * 2 + e) * (HC // 2)
                        h_gate_up(first, 0)
                        plain(pe)
                        with pe.Fori(0, HC // 2 - 1) as f:
                            n = first + f
                            h_gate_up(n, 1)
                            h_down(n, 0)
                            h_gate_up(n + 1, 0)
                            h_down(n, 1)
                        last = first + HC // 2 - 1
                        h_gate_up(last, 1)
                        h_down(last, 0)
                        h_down(last, 1)
                        for j in range(TB):
                            t = pe.matmul(ps[:, 4 + j, :], h_zero[:, 0:P], h_zero[:, :], start=False, stop=True, skip_group_check=True)
                        t.then_inc(sem("h_y_ps"), 1)
                        pe.wait_ge(sem("h_y_used"), TB * (i * 2 + e + 1))
                end_stage(pe, 7)


NEG = -1.0e30
HI_BEFORE = {"a": 0, "c": 2, "d": 4, "f": 5, "g": 7, "h": 10}
READY = {stage: n + 1 for n, stage in enumerate("abcdfgh")}
E_HEADS, E_R, E_CQ = 16, 64, 384
E_CUTS = np.cumsum([0, E_CQ, 3 * E_R, D, DC, D]).tolist()
E_RAW = E_CUTS[-1]
E_QKW = C * P + P
E_BODY = 4
QK_AHEAD = 3
E_TURNS = E_HEADS // E_BODY
F_N, F_K = 136, 72
G_HD = 32
G_HEADS_BEFORE = B * E_HEADS
G_SCALE = float(1.0 / np.sqrt(np.float32(32)))
H_BLOB = 3 * D
SYN_K = max(1, int(HID * (1.0 - 0.9)))
SYN_STEPS = 26
SIM_K = max(1, int(S * 0.3))
SIM_STEPS = 26
SIM1_SCALE = 1.0 / (math.sqrt(32.0) * 4)


def layout(v):
    f = np.ascontiguousarray

    def cut(a):
        return f(a.reshape(a.shape[0] // P, P, a.shape[1]).transpose(1, 0, 2))

    ctx2 = v["ctx_512"].reshape(B * S, DC)
    return {
        "x": cut(v["x"].reshape(B * S, D)),
        "g_xattn": f(v["g_xattn"]), "g_ffn": f(v["g_ffn"]),
        "ctxT": f(ctx2.T),
        "l0_wkT": f(v["L0_xattn_W_k"].T), "l0_bk": f(v["L0_xattn_b_k"].reshape(DC, 1)),
        "l0_gamma": f(v["L0_xattn_ln_gamma"]), "l0_beta": f(v["L0_xattn_ln_beta"]),
        "wsynT": cut(v["L0_ffn_W_syn"].T).reshape(P, -1), "woutT": cut(v["L0_ffn_W_out"].T).reshape(P, -1),
        "b_syn": f(v["L0_ffn_b_syn"]), "b_out": f(v["L0_ffn_b_out"]),
        "ffn_gamma": f(v["L0_ffn_gamma"]), "ffn_beta": f(v["L0_ffn_beta"]),
        "l1_wqkT": f(np.stack([v["L1_xattn_Wq"].T, v["L1_xattn_Wk"].T], 1)),
        "l1_gamma_raw": f(v["L1_xattn_gamma_raw"].reshape(1)),
        **rope(),
        "ctx": f(ctx2.reshape(B, TB, P, DC).transpose(0, 2, 1, 3)),
        "l2_heads": heads(v), "l2_wkr": f(v["L2_xattn_W_kr"].reshape(8, 2, DC, E_R).transpose(0, 2, 1, 3).reshape(8, DC, P)),
        **select_ffn(v, cut),
        "l3_wqT": cut(v["L3_xattn_Wq"].T), "l3_woT": cut(v["L3_xattn_Wout"].T), "l3_wkvT": f(v["L3_xattn_Wkv_expand"].T),
        "l3_gateT": cut(v["L3_ffn_gate_w"].T), "l3_blob": experts(v),
        "l1_wT": cut(v["L1_ffn_weight"].T), "l1_scale": f(v["L1_ffn_scale_weight"]), "l1_bias": f(v["L1_ffn_bias"]),
    }


def rope():
    inv = (1.0 / np.float32(10000.0) ** (np.arange(0, DC, 2, dtype=np.float32) / np.float32(DC))).astype(np.float32)
    freqs = np.arange(S, dtype=np.float32)[:, None] * inv[None, :]
    sin, cos = (np.repeat(t(freqs).astype(np.float32), 2, axis=-1) for t in (np.sin, np.cos))
    sin = np.concatenate([-sin[:, :DC // 2], sin[:, DC // 2:]], 1)
    return {n: np.ascontiguousarray(t.reshape(TB, P, DC).transpose(1, 0, 2)) for n, t in (("cos", cos), ("sin", sin))}


def heads(v):
    h = E_HEADS
    kcq = v["L2_xattn_w_kc_q"].transpose(0, 2, 1).reshape(h, 3, P, P).transpose(0, 2, 1, 3).reshape(h, P, -1)
    wqr = v["L2_xattn_W_qr"].reshape(h, 3, P, E_R).transpose(0, 2, 1, 3).reshape(h, P, -1)
    wq = v["L2_xattn_Wq"].reshape(h, P, D)
    wkv = v["L2_xattn_w_kc_kv"]
    wo = v["L2_xattn_Wo"].T.reshape(h, P, D)
    a = np.concatenate([kcq, wqr, wq, wkv, wo], 2)
    return np.ascontiguousarray(a.reshape(h // 2, 2, P, -1).transpose(0, 2, 1, 3))


def select_ffn(v, cut):
    sw, up = (v[n].transpose(1, 0, 2) for n in ("L2_ffn_select_weight", "L2_ffn_lora_update"))
    mean, deb = v["L2_ffn_select_mean_diff"].T, v["L2_ffn_debias_w"].T
    w = np.concatenate([sw.reshape(D, 64), up.reshape(D, 64), mean], 1)
    q = np.concatenate([np.repeat(mean, 8, 1), np.repeat(deb, 8, 1), mean], 1)
    d = np.concatenate([v["L2_ffn_lora_degen"].transpose(0, 2, 1).reshape(64, D), v["L2_ffn_bias_w"]], 0)
    return {"l2_fw": cut(w), "l2_fq": cut(q), "l2_fd": np.ascontiguousarray(d),
            "l2_center": v["L2_ffn_imp_center"], "l2_slope": v["L2_ffn_imp_slope"],
            "order": np.arange(8, 0, -1).astype(np.float32)}


def experts(v):
    g, u = (v[n].reshape(2, HC, P, C, P).transpose(0, 1, 4, 3, 2).reshape(2, HC, P, D) for n in ("L3_ffn_w_gate", "L3_ffn_w_up"))
    d = v["L3_ffn_w_down"].transpose(0, 2, 1).reshape(2, HC, P, D)
    return np.ascontiguousarray(np.concatenate([g, u, d], 3))


def kernel(**inputs):
    import concourse.bacc as _bacc
    from concourse.bass_utils import run_bass_kernel_spmd as _run

    nc = _bacc.Bacc("TRN2", target_bir_lowering=False, num_devices=1)
    arrays = {f"in_{name}": a for name, a in layout({k: np.asarray(a) for k, a in inputs.items()}).items()}
    args = {name[3:]: nc.dram_tensor(name, a.shape, mybir.dt.from_np(a.dtype), kind="ExternalInput").ap()
            for name, a in arrays.items()}
    out = nc.dram_tensor("out_0", (P, TILES, D), F32, kind="ExternalOutput").ap()
    program(nc, args, out)
    r = _run(nc, [arrays], core_ids=[0])
    return np.ascontiguousarray(r.results[0]["out_0"].transpose(1, 0, 2)).reshape(B, S, D)
```

```python
import math
from contextlib import ExitStack

import numpy as np

import concourse.bass as bass
from concourse import mybir

F32 = mybir.dt.float32
F32R = mybir.dt.float32r
ALU = mybir.AluOpType
ACT = mybir.ActivationFunctionType
AX = mybir.AxisListType

P = 128
B, S, D, DC = 4, 512, 512, 128
TILES = B * S // P
TB = S // P
C = D // P
HID = 2048
HC = HID // P
BANK = 512
LN_EPS = 1e-5


class InOrder:

    def __init__(self, eng, sem):
        self.eng, self.sem, self.base, self.n = eng, sem, 0, 0

    def __call__(self, instruction):
        self.n += 1
        instruction.then_inc(self.sem, 1)
        self.eng.wait_ge(self.sem, self.base + self.n)

    def later(self, instruction):
        self.n += 1
        instruction.then_inc(self.sem, 1)

    def enter(self, i, per):
        outer = (self.base, self.n)
        self.base, self.n = self.base + self.n + i * per, 0
        return outer

    def leave(self, outer, turns, per):
        assert self.n == per, f"{self.sem}: {self.n} steps a turn, not {per}"
        self.base, self.n = outer[0], outer[1] + turns * per


def program(nc, inp, out, stages=8):
    ctx = ExitStack()
    with ctx:
        sems = {}

        def sem(name):
            if name not in sems:
                sems[name] = ctx.enter_context(nc.semaphore(name))
            return sems[name]

        def sb(name, shape, dt=F32, where=ctx):
            return where.enter_context(nc.sbuf_tensor(name, shape, dt))

        ps = ctx.enter_context(nc.psum_tensor("ps", [P, 8, BANK], F32))

        X = sb("X", [P, TILES, D])
        tg = sb("tg", [P, 8])
        ident = sb("ident", [P, P])
        ones = sb("ones", [P, P])
        minus_half = sb("minus_half", [P, TB])
        xn = sb("xn", [P, TB, D])
        xT_hi = sb("xT_hi", [P, C, S], F32R)
        xT_lo = sb("xT_lo", [P, C, S], F32R)
        ln_stats = sb("ln_stats", [P, TB, 6])
        ln_mv = sb("ln_mv", [P, TB, 2])
        ln_var = sb("ln_var", [P, TB])
        ln_rstd = sb("ln_rstd", [P, TB])
        small = sb("small", [P, 64])

        def mm3(pe, o, l_hi, l_lo, r_hi, r_lo, start, stop):
            pe.matmul(o, l_hi, r_hi, start=start, stop=False)
            pe.matmul(o, l_hi, r_lo, start=False, stop=False)
            return pe.matmul(o, l_lo, r_hi, start=False, stop=stop)

        def plain(eng):
            eng.sem_inc(sem("plain"), 1)

        def end_stage(eng, n):
            eng.drain().then_inc(sem("stage_done"), 1)
            eng.wait_ge(sem("stage_done"), 4 * (n + 1))

        def ln_turn(s, i):
            return B * "abcdefgh".index(s) + i

        def norm_vector(dve, k, s, i, X=X):
            for j in range(TB):
                k(dve.bn_stats(ln_stats[:, j, :], X[:, i * TB + j, :]))
            for j in range(TB):
                plain(dve)
                k(dve.bn_aggr(ln_mv[:, j, :], ln_stats[:, j, :]))
            dve.tensor_scalar(ln_var[:, :], ln_mv[:, :, 1], LN_EPS, None, ALU.add).then_inc(sem("ln_var"), 1)
            dve.wait_ge(sem("ln_rstd"), ln_turn(s, i) + 1)
            for j in range(TB):
                dve.tensor_scalar(xn[:, j, :], X[:, i * TB + j, :], ln_mv[:, j, 0:1], ln_rstd[:, j:j + 1],
                                  ALU.subtract, ALU.mult).then_inc(sem("ln_xn"), 1)
            dve.wait_ge(sem("ln_xn"), TB * (ln_turn(s, i) + 1))
            for j in range(TB):
                dve.wait_ge(sem("ln_xT_hi"), TB * ln_turn(s, i) + j + 1)
                q = slice(j * P, (j + 1) * P)
                dve.tensor_tensor(xT_lo[:, :, q], ps[:, j % 2, :].rearrange("p (c t) -> p c t", c=C),
                                  xT_hi[:, :, q].bitcast(F32), ALU.subtract).then_inc(sem("ln_xT"), 1)
            dve.wait_ge(sem("ln_xT"), TB * (ln_turn(s, i) + 1))

        def norm_pool(pool, s, i):
            pool.wait_ge(sem("ln_var"), ln_turn(s, i) + 1)
            pool.tensor_tensor(ln_rstd[:, :], ln_var[:, :], minus_half[:, :], ALU.pow).then_inc(sem("ln_rstd"), 1)

        def norm_tensor(pe, s, i):
            for j in range(TB):
                pe.wait_ge(sem("ln_xn"), TB * ln_turn(s, i) + j + 1)
                if j >= 2:
                    pe.wait_ge(sem("ln_xT"), TB * ln_turn(s, i) + j - 1)
                for c in range(C):
                    t = pe.transpose(ps[:, j % 2, c * P:(c + 1) * P], xn[:, j, c * P:(c + 1) * P], ident[:, :])
                t.then_inc(sem("ln_xT_ps"), 1)
            pe.wait_ge(sem("ln_xT"), TB * (ln_turn(s, i) + 1))

        def norm_scalar(act, s, i):
            for j in range(TB):
                act.wait_ge(sem("ln_xT_ps"), TB * ln_turn(s, i) + j + 1)
                act.activation(xT_hi[:, :, j * P:(j + 1) * P], ps[:, j % 2, :].rearrange("p (c t) -> p c t", c=C),
                               ACT.Copy).then_inc(sem("ln_xT_hi"), 1)

        def search_turn(s, i):
            return (B * "bc".index(s) + i) * (ROUNDS + 1)

        def search_round(s, i):
            return (B * "bc".index(s) + i) * ROUNDS

        def search_vector(dve, k, i, data, junk, low, step, other, cand, cnt, take, kth):
            mine, theirs = slice(0, 2), slice(2, 4)
            for v in (low, step, cand):
                k.later(dve.tensor_scalar(v[:, theirs], v[:, theirs], -1.0, None, ALU.mult))
            dve.wait_ge(k.sem, k.base + k.n)
            dve.sem_inc(sem("search_set"), 1)
            plain(dve)
            with dve.Fori(0, ROUNDS // 2) as r:
                outer = k.enter(r, 2 * SEARCH_STEPS)
                for now, then in ((step, other), (other, step)):
                    k.later(dve.tensor_scalar(then[:, mine], now[:, mine], 0.5, None, ALU.mult))
                    for j in (0, 1):
                        k(dve.tensor_scalar(junk, data[:, j, :], cand[:, j:j + 1], 0.0, ALU.is_ge, ALU.add, accum_out=cnt[:, j:j + 1]))
                    k(dve.scalar_tensor_tensor(take[:, mine], cnt[:, mine], float(kth), now[:, mine], ALU.is_ge, ALU.mult))
                    k(dve.tensor_tensor(low[:, mine], low[:, mine], take[:, mine], ALU.add))
                    k(dve.tensor_tensor(cand[:, mine], low[:, mine], then[:, mine], ALU.add))
                k.leave(outer, ROUNDS // 2, 2 * SEARCH_STEPS)

        def search_vector_end(dve, k, s, i, low):
            dve.wait_ge(sem("search_try"), search_turn(s, i + 1))
            k(dve.tensor_scalar(low[:, 2:4], low[:, 2:4], -1.0, None, ALU.mult))

        def search_pool(pool, k, s, i, low, step, cand, cnt, take, kth, n):
            theirs = slice(2, 4)
            low, step, cand, cnt, take = (v[:, theirs] for v in (low, step, cand, cnt, take))
            pool.wait_ge(sem("search_set"), B * "bc".index(s) + i + 1)
            pool.sem_inc(sem("search_try"), 1)
            with pool.Fori(0, ROUNDS) as r:
                outer = k.enter(r, 4)
                t = search_round(s, i) + r
                pool.wait_ge(sem("search_count"), 2 * (t + 1))
                plain(pool)
                k(pool.tensor_scalar(take, cnt, float(2 * kth - n), None, ALU.is_ge))
                k(pool.tensor_tensor(take, take, step, ALU.mult))
                k.later(pool.tensor_tensor(low, low, take, ALU.add))
                k(pool.tensor_scalar(step, step, 0.5, None, ALU.mult))
                pool.tensor_tensor(cand, low, step, ALU.add).then_inc(sem("search_try"), 1)
                k.leave(outer, ROUNDS, 4)

        def search_scalar(act, s, i, data, junk, cand, cnt):
            with act.Fori(0, ROUNDS) as r:
                act.wait_ge(sem("search_try"), search_turn(s, i) + r + 1)
                t = search_round(s, i) + r
                for j in (2, 3):
                    act.activation(junk, data[:, j, :], ACT.Sign, bias=cand[:, j:j + 1], accum_out=cnt[:, j:j + 1])\
                        .then_inc(sem("search_count"), 1)
                    act.wait_ge(sem("search_count"), 2 * t + j - 1)

        stack = {}

        def mem(stage):
            stack[stage] = ExitStack()
            return lambda name, shape, dt=F32: sb(name, shape, dt, stack[stage])

        m = mem("A")
        a_ctxT = m("a_ctxT", [P, B * S])
        a_ctx_hi, a_ctx_lo = m("a_ctx_hi", [P, B * S], F32R), m("a_ctx_lo", [P, B * S], F32R)
        a_wk = m("a_wk", [P, DC])
        a_wk_hi, a_wk_lo = m("a_wk_hi", [P, DC], F32R), m("a_wk_lo", [P, DC], F32R)
        a_bk = m("a_bk", [P, 1])
        a_gamma, a_beta = m("a_gamma", [P, S]), m("a_beta", [P, S])
        a_kvT = m("a_kvT", [P, S])
        a_kvT_hi, a_kvT_lo = m("a_kvT_hi", [P, S], F32R), m("a_kvT_lo", [P, S], F32R)
        a_kv_hi, a_kv_lo = m("a_kv_hi", [P, TB, DC], F32R), m("a_kv_lo", [P, TB, DC], F32R)
        a_oT_hi, a_oT_lo = m("a_oT_hi", [P, S], F32R), m("a_oT_lo", [P, S], F32R)
        a_sim = m("a_sim", [P, S])
        a_exp = m("a_exp", [P, S])
        a_st = m("a_st", [P, 16])
        stack["A"].close()
        m = mem("B")
        b_tsyn = m("b_tsyn", [P, C, HID], F32R)
        b_tout = m("b_tout", [P, HC, D], F32R)
        b_z = m("b_z", [P, TB, HID])
        b_bsyn = m("b_bsyn", [P, HID])
        b_hT_hi, b_hT_lo = m("b_hT_hi", [P, HC, P], F32R), m("b_hT_lo", [P, HC, P], F32R)
        b_rows = m("b_rows", [P, 3, D])
        b_y = m("b_y", [P, D])
        b_st = m("b_st", [P, 16])
        b_tk = m("b_tk", [P, 8, TB])
        b_junk = m("b_junk", [P, 2, HID], mybir.dt.bfloat16)
        stack["B"].close()
        b_wraw = b_z[:, :, :].rearrange("p a n -> p (a n)")
        b_tmp = b_junk[:, :, :].rearrange("p a n -> p (a n)")
        m = mem("C")
        c_ctxT = m("c_ctxT", [P, B * S])
        c_ctx_hi, c_ctx_lo = m("c_ctx_hi", [P, B * S], F32R), m("c_ctx_lo", [P, B * S], F32R)
        c_w = m("c_w", [P, 2, DC])
        c_w_hi, c_w_lo = m("c_w_hi", [P, 2, DC], F32R), m("c_w_lo", [P, 2, DC], F32R)
        c_qk_hi, c_qk_lo = m("c_qk_hi", [P, 2, S], F32R), m("c_qk_lo", [P, 2, S], F32R)
        c_sim = m("c_sim", [P, TB, S])
        c_a = m("c_a", [P, TB, S])
        c_tk = m("c_tk", [P, 8, TB])
        c_g = m("c_g", [P, 4])
        c_junk = m("c_junk", [P, 2, S])
        c_t = m("c_t", [P, S])
        stack["C"].close()
        m = mem("D")
        d_w = m("d_w", [P, C, D])
        d_w_hi, d_w_lo = m("d_w_hi", [P, C, D], F32R), m("d_w_lo", [P, C, D], F32R)
        d_rows = m("d_rows", [P, 2, D])
        stack["D"].close()

        m = mem("E")
        e_blob = m("e_blob", [P, 2, E_RAW])
        e_wkr = m("e_wkr", [P, P])
        e_u = m("e_u", [P, 2, E_R])
        e_qkw = m("e_qkw", [P, 2, 2, E_QKW], F32R)
        e_g = m("e_g", [P, 2, 2, 2 * D], F32R)
        e_ctx = m("e_ctx", [P, TB, DC])
        e_cos, e_sin = m("e_cos", [P, TB, DC]), m("e_sin", [P, TB, DC])
        e_rot = m("e_rot", [P, TB, DC])
        e_kvr = m("e_kvr", [P, TB, DC])
        e_kvr_hi, e_kvr_lo = m("e_kvr_hi", [P, TB, DC], F32R), m("e_kvr_lo", [P, TB, DC], F32R)
        e_kT_hi, e_kT_lo = m("e_kT_hi", [P, S], F32R), m("e_kT_lo", [P, S], F32R)
        e_qk_hi, e_qk_lo = m("e_qk_hi", [P, 2, 2, S], F32R), m("e_qk_lo", [P, 2, 2, S], F32R)
        e_p = m("e_p", [P, 2, TB, S])
        e_pT_hi, e_pT_lo = m("e_pT_hi", [P, TB, S], F32R), m("e_pT_lo", [P, TB, S], F32R)
        e_cT_hi, e_cT_lo = m("e_cT_hi", [P, 2, S], F32R), m("e_cT_lo", [P, 2, S], F32R)
        e_st = m("e_st", [P, 2, 16])
        e_zero = m("e_zero", [P, S], F32R)
        stack["E"].close()
        e_qkw_kept = nc.dram_tensor("e_qkw_kept", (E_HEADS // 2, P, 2, E_QKW), F32, kind="Internal").ap()
        e_g_kept = nc.dram_tensor("e_g_kept", (E_HEADS // 2, P, 2, 2 * D), F32, kind="Internal").ap()
        m = mem("F")
        f_w, f_q = m("f_w", [P, C, F_N]), m("f_q", [P, C, F_N])
        f_w_hi, f_w_lo = m("f_w_hi", [P, C, F_N], F32R), m("f_w_lo", [P, C, F_N], F32R)
        f_d = m("f_d", [F_K, D])
        f_d_hi, f_d_lo = m("f_d_hi", [F_K, D], F32R), m("f_d_lo", [F_K, D], F32R)
        f_const = m("f_const", [P, F_N])
        f_rows = m("f_rows", [P, 3, 8])
        f_a = m("f_a", [P, TB, F_N])
        f_sq = m("f_sq", [P, TB, 64])
        f_xx = m("f_xx", [P, TB])
        f_g = m("f_g", [P, 6, TB, 8])
        f_s = m("f_s", [P, 4, TB])
        f_m = m("f_m", [P, TB, F_K])
        f_junk = m("f_junk", [P, D])
        f_mT_hi, f_mT_lo = m("f_mT_hi", [F_K, S], F32R), m("f_mT_lo", [F_K, S], F32R)
        stack["F"].close()
        m = mem("G")
        g_w = m("g_w", [P, C, D])
        g_wq_hi, g_wq_lo = m("g_wq_hi", [P, C, D], F32R), m("g_wq_lo", [P, C, D], F32R)
        g_wo_hi, g_wo_lo = m("g_wo_hi", [P, C, D], F32R), m("g_wo_lo", [P, C, D], F32R)
        g_wkv_hi, g_wkv_lo = m("g_wkv_hi", [P, 2 * D], F32R), m("g_wkv_lo", [P, 2 * D], F32R)
        g_ctxT = m("g_ctxT", [P, S])
        g_ctx_hi, g_ctx_lo = m("g_ctx_hi", [P, S], F32R), m("g_ctx_lo", [P, S], F32R)
        g_qT, g_kT = m("g_qT", [P, C, S]), m("g_kT", [P, C, S])
        g_v_hi, g_v_lo = m("g_v_hi", [P, TB, P], F32R), m("g_v_lo", [P, TB, P], F32R)
        g_qk_hi, g_qk_lo = m("g_qk_hi", [P, 2, S], F32R), m("g_qk_lo", [P, 2, S], F32R)
        g_mask = m("g_mask", [P, P])
        g_p = m("g_p", [P, TB, S])
        g_pT_hi, g_pT_lo = m("g_pT_hi", [P, TB, S], F32R), m("g_pT_lo", [P, TB, S], F32R)
        g_mask_r, g_ident_r = m("g_mask_r", [P, P], F32R), m("g_ident_r", [P, P], F32R)
        g_st = m("g_st", [P, 2, 8])
        g_diag = m("g_diag", [P, TB, P])
        stack["G"].close()
        m = mem("H")
        h_w = m("h_w", [P, 2, H_BLOB])
        h_w_hi, h_w_lo = m("h_w_hi", [P, 2, H_BLOB], F32R), m("h_w_lo", [P, 2, H_BLOB], F32R)
        h_diag, h_gain = m("h_diag", [P, 2, S]), m("h_gain", [P, 2, S])
        h_gw = m("h_gw", [P, C, 2])
        h_gw_hi, h_gw_lo = m("h_gw_hi", [P, C, 2], F32R), m("h_gw_lo", [P, C, 2], F32R)
        h_sg = m("h_sg", [P, 2, S])
        h_h = m("h_h", [P, 2, S])
        h_h_hi, h_h_lo = m("h_h_hi", [P, 2, S], F32R), m("h_h_lo", [P, 2, S], F32R)
        h_l = m("h_l", [P, 6, TB, 2])
        h_s = m("h_s", [P, 4, TB])
        h_zero = m("h_zero", [P, S], F32R)
        stack["H"].close()

        block = ctx.enter_context(nc.Block())

        @block.sync
        def _(sp):
            for name in ("e_blob_used", "e_ctx_used", "e_g_used0", "e_g_used1", "g_ctx_used", "h_gu_used", "h_gu_used", "h_d_used", "h_d_used",
                         "h_down", "h_down", "h_gu_ps", "h_gu_ps", "h_h", "h_h", "e_mg", "e_pair_kept"):
                sp.sem_inc(sem(name), 1)
            sp.sem_inc(sem("qk_ps"), QK_AHEAD)
            sp.dma_start(X[:, :, :], inp["x"]).then_inc(sem("x_in"), 16)
            sp.dma_start(tg[:, 0:4], inp["g_xattn"].partition_broadcast(P)).then_inc(sem("x_in"), 16)
            sp.dma_start(tg[:, 4:8], inp["g_ffn"].partition_broadcast(P)).then_inc(sem("x_in"), 16)
            for dst, src in ((a_ctxT[:, :], inp["ctxT"]), (a_wk[:, :], inp["l0_wkT"]), (a_bk[:, :], inp["l0_bk"]),
                             (a_gamma[:, :], inp["l0_gamma"].partition_broadcast(P)),
                             (a_beta[:, :], inp["l0_beta"].partition_broadcast(P))):
                sp.dma_start(dst, src).then_inc(sem("a_in"), 16)
            if stages > 1:
                sp.wait_ge(sem("stage_done"), 4)
                sp.dma_start(b_wraw, inp["wsynT"]).then_inc(sem("b_in"), 16)
                for dst, src in ((b_bsyn[:, :], inp["b_syn"]), (b_rows[:, 0, :], inp["b_out"]),
                                 (b_rows[:, 1, :], inp["ffn_gamma"]), (b_rows[:, 2, :], inp["ffn_beta"])):
                    sp.dma_start(dst, src.partition_broadcast(P)).then_inc(sem("b_rows_in"), 16)
                sp.wait_ge(sem("b_raw_used"), 1)
                sp.dma_start(b_wraw, inp["woutT"]).then_inc(sem("b_in"), 16)
            if stages > 2:
                sp.wait_ge(sem("stage_done"), 8)
                for dst, src in ((c_ctxT[:, :], inp["ctxT"]), (c_w[:, :, :], inp["l1_wqkT"]),
                                 (c_g[:, 0:1], inp["l1_gamma_raw"].partition_broadcast(P))):
                    sp.dma_start(dst, src).then_inc(sem("c_in"), 16)
            if stages > 3:
                sp.wait_ge(sem("stage_done"), 12)
                for dst, src in ((d_w[:, :, :], inp["l1_wT"]), (d_rows[:, 0, :], inp["l1_scale"].partition_broadcast(P)),
                                 (d_rows[:, 1, :], inp["l1_bias"].partition_broadcast(P))):
                    sp.dma_start(dst, src).then_inc(sem("d_in"), 16)
            if stages > 4:
                sp.wait_ge(sem("stage_done"), 16)
                sp.dma_start(e_cos[:, :, :], inp["cos"]).then_inc(sem("e_tables"), 16)
                sp.dma_start(e_sin[:, :, :], inp["sin"]).then_inc(sem("e_tables"), 16)
                with sp.Fori(0, E_HEADS // 2) as i:
                    sp.wait_ge(sem("e_blob_used"), i + 1)
                    sp.dma_start(e_blob[:, :, :], inp["l2_heads"][i]).then_inc(sem("e_blob_in"), 16)
                    sp.dma_start(e_wkr[:, :], inp["l2_wkr"][i]).then_inc(sem("e_blob_in"), 16)
                    sp.wait_ge(sem("e_pair_made"), i + 1)
                    sp.dma_start(e_qkw_kept[i], e_qkw[:, 0, :, :].bitcast(F32)).then_inc(sem("e_pair_kept"), 16)
                    sp.dma_start(e_g_kept[i], e_g[:, 0, :, :].bitcast(F32)).then_inc(sem("e_pair_kept"), 16)
                sp.wait_ge(sem("e_pair_kept"), 32 * (E_HEADS // 2) + 1)
                with sp.Fori(0, B) as i:
                    sp.wait_ge(sem("e_ctx_used"), i + 1)
                    sp.dma_start(e_ctx[:, :, :], inp["ctx"][i]).then_inc(sem("e_ctx_in"), 16)
                    with sp.Fori(0, E_HEADS // 4) as g:
                        for u in range(2):
                            n = (i * (E_HEADS // 4) + g)
                            sp.wait_ge(sem("qk_ps"), n * E_BODY + 2 * u - 2 + QK_AHEAD)
                            sp.dma_start(e_qkw[:, u, :, :].bitcast(F32), e_qkw_kept[g * 2 + u]).then_inc(sem(f"e_qkw_in{u}"), 16)
                            sp.wait_ge(sem(f"e_g_used{u}"), n + 1)
                            sp.dma_start(e_g[:, u, :, :].bitcast(F32), e_g_kept[g * 2 + u]).then_inc(sem(f"e_g_in{u}"), 16)
            if stages > 5:
                sp.wait_ge(sem("stage_done"), 20)
                for dst, src in ((f_w[:, :, :], inp["l2_fw"]), (f_q[:, :, :], inp["l2_fq"]), (f_d[:, :], inp["l2_fd"]),
                                 (f_rows[:, 0, :], inp["l2_center"].partition_broadcast(P)),
                                 (f_rows[:, 1, :], inp["l2_slope"].partition_broadcast(P)),
                                 (f_rows[:, 2, :], inp["order"].partition_broadcast(P))):
                    sp.dma_start(dst, src).then_inc(sem("f_in"), 16)
            if stages > 6:
                sp.wait_ge(sem("stage_done"), 24)
                for n, src in enumerate(("l3_wqT", "l3_woT", "l3_wkvT")):
                    sp.wait_ge(sem("g_raw_used"), n)
                    dst = g_w[:, :, :] if n < 2 else g_w[:, 0:2, :].rearrange("p a n -> p (a n)")
                    sp.dma_start(dst, inp[src]).then_inc(sem("g_in"), 16)
                with sp.Fori(0, B) as i:
                    sp.wait_ge(sem("g_ctx_used"), i + 1)
                    sp.dma_start(g_ctxT[:, :], inp["ctxT"][:, bass.ts(i, S)]).then_inc(sem("g_ctx_in"), 16)
            if stages > 7:
                sp.wait_ge(sem("stage_done"), 28)
                sp.dma_start(h_gw[:, :, :], inp["l3_gateT"]).then_inc(sem("h_gw_in"), 16)
                with sp.Fori(0, B) as i:
                    with sp.Fori(0, HC) as f:
                        for u in range(2):
                            n = i * (2 * HC) + f * 2 + u
                            sp.wait_ge(sem("h_gu_used"), n + 1)
                            sp.dma_start(h_w[:, u, 0:2 * D], inp["l3_blob"][f * 2 + u, :, 0:2 * D]).then_inc(sem(f"h_gu_in{u}"), 16)
                            sp.wait_ge(sem("h_d_used"), n + 1)
                            sp.dma_start(h_w[:, u, 2 * D:], inp["l3_blob"][f * 2 + u, :, 2 * D:]).then_inc(sem(f"h_d_in{u}"), 16)
            sp.wait_ge(sem("stage_done"), 4 * stages)
            sp.dma_start(out, X[:, :, :]).then_inc(sem("x_out"), 16)
            sp.wait_ge(sem("x_out"), 16)

        @block.gpsimd
        def _(pool):
            k = InOrder(pool, sem("pool_steps"))
            k(pool.memset(ident[:, :], 0.0))
            k(pool.memset(ones[:, :], 1.0))
            k(pool.memset(minus_half[:, :], -0.5))
            pool.affine_select(out=ident[:, :], in_=ident[:, :], compare_op=ALU.not_equal, fill=1.0, base=0,
                               pattern=[[-1, P]], channel_multiplier=1).then_inc(sem("consts"), 1)
            with pool.Fori(0, B) as i:
                norm_pool(pool, "a", i)
                for j in range(TB):
                    pool.wait_ge(sem("a_sim_var"), i * TB + j + 1)
                    pool.tensor_tensor(a_st[:, 8:9], a_st[:, 7:8], minus_half[:, 0:1], ALU.pow).then_inc(sem("a_sim_rstd"), 1)
            end_stage(pool, 0)
            if stages > 1:
                with pool.Fori(0, B) as i:
                    o = k.enter(i, 4 * ROUNDS)
                    norm_pool(pool, "b", i)
                    search_pool(pool, k, "b", i, *(b_tk[:, r, :] for r in (0, 1, 3, 4, 5)), SYN_K, HID)
                    k.leave(o, B, 4 * ROUNDS)
                    for j in range(TB):
                        pool.wait_ge(sem("b_y_var"), i * TB + j + 1)
                        pool.tensor_tensor(b_st[:, 8:9], b_st[:, 7:8], minus_half[:, 0:1], ALU.pow).then_inc(sem("b_y_rstd"), 1)
                end_stage(pool, 1)
            for n, name in enumerate("cdefgh", 2):
                if stages > n:
                    if name == "g":
                        k(pool.memset(g_mask[:, :], 0.0))
                        pool.affine_select(out=g_mask[:, :], in_=g_mask[:, :], compare_op=ALU.is_ge, fill=NEG, base=0,
                                           pattern=[[-1, P]], channel_multiplier=1).then_inc(sem("g_mask"), 1)
                    with pool.Fori(0, B) as i:
                        norm_pool(pool, name, i)
                        if name == "c":
                            o = k.enter(i, 4 * ROUNDS)
                            search_pool(pool, k, "c", i, *(c_tk[:, r, :] for r in (0, 1, 3, 4, 5)), SIM_K, S)
                            k.leave(o, B, 4 * ROUNDS)
                    end_stage(pool, n)

        @block.scalar
        def _(act):
            act.wait_ge(sem("x_in"), 48)
            act.activation(tg[:, :], tg[:, :], ACT.Tanh).then_inc(sem("tg"), 1)
            act.wait_ge(sem("a_in"), 80)
            act.activation(a_ctx_hi[:, :], a_ctxT[:, :], ACT.Copy).then_inc(sem("weights_hi"), 1)
            act.activation(a_wk_hi[:, :], a_wk[:, :], ACT.Copy).then_inc(sem("weights_hi"), 1)
            with act.Fori(0, B) as i:
                norm_scalar(act, "a", i)
                act.wait_ge(sem("a_kvT_ps"), i + 1)
                act.activation(a_kvT[:, :], ps[:, 2, :], ACT.Identity, bias=a_bk[:, 0:1]).then_inc(sem("a_kvT_f"), 1)
                act.wait_ge(sem("a_kvT_f"), i + 1)
                act.activation(a_kvT_hi[:, :], a_kvT[:, :], ACT.Copy).then_inc(sem("a_kvT_hi"), 1)
                act.wait_ge(sem("a_kv_ps"), i + 1)
                act.activation(a_kv_hi[:, :, :], ps[:, 3, :].rearrange("p (t d) -> p t d", t=TB), ACT.Copy)\
                    .then_inc(sem("a_kv_hi"), 1)
                act.wait_ge(sem("a_oT_ps"), i + 1)
                act.activation(a_oT_hi[:, :], ps[:, 4, :], ACT.Copy).then_inc(sem("a_oT_hi"), 1)
                for j in range(TB):
                    act.wait_ge(sem("a_max"), i * TB + j + 1)
                    act.activation(a_exp[:, :], a_sim[:, :], ACT.Exp, bias=a_st[:, 9:10],
                                   accum_out=a_st[:, 10:11]).then_inc(sem("a_exp"), 1)
            end_stage(act, 0)
            if stages > 1:
                with act.Fori(0, B) as i:
                    norm_scalar(act, "b", i)
                    search_scalar(act, "b", i, b_z, b_junk[:, 1, :], b_tk[:, 3, :], b_tk[:, 4, :])
                    for j in range(TB):
                        for q in range(4):
                            act.wait_ge(sem("b_hT_ps"), (i * TB + j) * 4 + q + 1)
                            act.activation(b_hT_hi[:, 4 * q:4 * q + 4, :], ps[:, q, :].rearrange("p (c t) -> p c t", c=4),
                                           ACT.Copy).then_inc(sem("b_hT_hi"), 1)
                end_stage(act, 1)
            if stages > 2:
                act.wait_ge(sem("c_in"), 48)
                act.activation(c_ctx_hi[:, :], c_ctxT[:, :], ACT.Copy).then_inc(sem("weights_hi"), 1)
                act.activation(c_w_hi[:, :, :], c_w[:, :, :], ACT.Copy).then_inc(sem("weights_hi"), 1)
                act.activation(c_g[:, 1:2], c_g[:, 0:1], ACT.Exp, scale=-1.0).then_inc(sem("c_g"), 1)
                with act.Fori(0, B) as i:
                    norm_scalar(act, "c", i)
                    for w in range(2):
                        act.wait_ge(sem("c_qk_ps"), i * 2 + w + 1)
                        act.activation(c_qk_hi[:, w, :], ps[:, 2 + w, :], ACT.Copy).then_inc(sem("c_qk_hi"), 1)
                    for j in range(TB):
                        act.wait_ge(sem("c_sim_ps"), i * TB + j + 1)
                        act.activation(c_sim[:, j, :], ps[:, 4 + j % 2, :], ACT.Copy, scale=SIM1_SCALE).then_inc(sem("c_sim"), 1)
                    for j in range(TB):
                        act.wait_ge(sem("c_sim"), i * TB + j + 1)
                        act.activation(c_a[:, j, :], c_sim[:, j, :], ACT.Exp, scale=-1.0).then_inc(sem("c_e"), 1)
                    search_scalar(act, "c", i, c_sim, c_junk[:, 1, :], c_tk[:, 3, :], c_tk[:, 4, :])
                end_stage(act, 2)
            if stages > 3:
                act.wait_ge(sem("d_ws"), 4)
                act.activation(d_w_hi[:, :, :], d_w[:, :, :], ACT.Copy).then_inc(sem("weights_hi"), 1)
                with act.Fori(0, B) as i:
                    norm_scalar(act, "d", i)
                end_stage(act, 3)

            if stages > 4:
                def e_qk_scalar(turn, d):
                    u = d % 2
                    for w in range(2):
                        act.wait_ge(sem("qk_ps"), QK_AHEAD + turn * E_BODY + d * 2 + w + 1)
                        act.activation(e_qk_hi[:, u, w, :], ps[:, 2 + w, :], ACT.Copy).then_inc(sem("qk_hi"), 1)

                def e_exp_scalar(h, a):
                    for t in range(TB):
                        act.wait_ge(sem("score_max"), h * TB + t + 1)
                        act.activation(e_p[:, a, t, :], ps[:, t % 2, :], ACT.Exp, bias=e_st[:, a, t:t + 1],
                                       accum_out=e_st[:, a, 4 + t:5 + t]).then_inc(sem("exp"), 1)

                def e_head_scalar(turn, hh, tail):
                    h = turn * E_BODY + hh
                    if not (tail and hh == E_BODY - 1):
                        e_exp_scalar(h + 1, (hh + 1) % 2)
                    for c in range(TB):
                        act.wait_ge(sem("pT_ps"), h * TB + c + 1)
                        act.activation(e_pT_hi[:, c, :], ps[:, 2 + c % 2, :], ACT.Copy).then_inc(sem("pT_hi"), 1)
                    act.wait_ge(sem("head_ps"), h + 1)
                    act.activation(e_cT_hi[:, hh % 2, :], ps[:, 1, :], ACT.Copy).then_inc(sem("head_hi"), 1)
                    if hh % 2 == 0 and not (tail and hh == E_BODY - 2):
                        e_qk_scalar(turn, hh // 2 + 1)

                with act.Fori(0, E_HEADS // 2) as i:
                    for u in range(2):
                        n = i * 2 + u
                        act.wait_ge(sem("e_u_ps"), n + 1)
                        act.activation(e_u[:, u, :], ps[:, 0, 0:E_R], ACT.Copy).then_inc(sem("e_u"), 1)
                        act.wait_ge(sem("e_mg_ps"), n + 1)
                        if u == 0:
                            act.wait_ge(sem("e_pair_kept"), 32 * i + 1)
                        act.activation(e_qkw[:, 0, 0, 0:4 * P].rearrange("p (c n) -> p c n", c=C)[:, :, u * E_R:(u + 1) * E_R],
                                       ps[:, 1, 0:C * E_R].rearrange("p (c n) -> p c n", c=C), ACT.Copy).then_inc(sem("e_mg_hi"), 1)
                        act.activation(e_g[:, 0, 0, u * D:(u + 1) * D], ps[:, 2, :], ACT.Copy).then_inc(sem("e_mg_hi"), 1)
                    act.wait_ge(sem("e_blob_in"), 32 * (i + 1))
                    act.activation(e_qkw[:, 0, 0, 4 * P:5 * P], e_wkr[:, :], ACT.Copy).then_inc(sem("e_wkr_hi"), 1)
                with act.Fori(0, B) as i:
                    norm_scalar(act, "e", i)
                    act.wait_ge(sem("e_kvr"), i + 1)
                    act.activation(e_kvr_hi[:, :, :], e_kvr[:, :, :], ACT.Copy).then_inc(sem("e_kvr_hi"), 1)
                    act.wait_ge(sem("e_kT_ps"), i + 1)
                    act.activation(e_kT_hi[:, :], ps[:, 2, :], ACT.Copy).then_inc(sem("e_kT_hi"), 1)
                    e_qk_scalar(i * E_TURNS, 0)
                    e_exp_scalar(i * E_HEADS, 0)
                    with act.Fori(0, E_TURNS - 1) as g:
                        for hh in range(E_BODY):
                            e_head_scalar(i * E_TURNS + g, hh, False)
                    for hh in range(E_BODY):
                        e_head_scalar((i + 1) * E_TURNS - 1, hh, True)
                end_stage(act, 4)
            if stages > 5:
                act.wait_ge(sem("f_in"), 96)
                act.activation(f_w_hi[:, :, :], f_w[:, :, :], ACT.Copy).then_inc(sem("weights_hi"), 1)
                act.activation(f_d_hi[:, :], f_d[:, :], ACT.Copy).then_inc(sem("weights_hi"), 1)
                with act.Fori(0, B) as i:
                    norm_scalar(act, "f", i)
                    act.wait_ge(sem("ln_xn"), TB * (ln_turn("f", i) + 1))
                    for j in range(TB):
                        act.activation(f_junk[:, :], xn[:, j, :], ACT.Square, accum_out=f_xx[:, j:j + 1]).then_inc(sem("f_xx"), 1)
                        act.wait_ge(sem("f_xx"), i * TB + j + 1)
                    act.wait_ge(sem("f_z"), i + 1)
                    act.activation(f_g[:, 1, :, :], f_g[:, 0, :, :], ACT.Exp, scale=-1.0).then_inc(sem("f_e"), 1)
                    act.wait_ge(sem("f_mT_ps"), i + 1)
                    act.activation(f_mT_hi[:, :], ps[0:F_K, 4, :], ACT.Copy).then_inc(sem("f_mT_hi"), 1)
                end_stage(act, 5)
            if stages > 6:
                for n, dst in enumerate((g_wq_hi, g_wo_hi)):
                    act.wait_ge(sem("g_in"), 16 * (n + 1))
                    act.activation(dst[:, :, :], g_w[:, :, :], ACT.Copy).then_inc(sem("weights_hi"), 1)
                act.wait_ge(sem("g_in"), 48)
                act.activation(g_wkv_hi[:, :], g_w[:, 0:2, :].rearrange("p a n -> p (a n)"), ACT.Copy).then_inc(sem("weights_hi"), 1)
                act.wait_ge(sem("g_mask"), 1)
                act.activation(g_mask_r[:, :], g_mask[:, :], ACT.Copy).then_inc(sem("weights_hi"), 1)
                act.activation(g_ident_r[:, :], ident[:, :], ACT.Copy).then_inc(sem("weights_hi"), 1)

                def g_qk_scalar(n, g):
                    act.wait_ge(sem("scores_ps"), TB * (G_HEADS_BEFORE + n * 4))
                    act.activation(g_qk_hi[:, 0, :], g_qT[:, g, :], ACT.Copy).then_inc(sem("qk_hi"), 1)
                    act.activation(g_qk_hi[:, 1, :], g_kT[:, g, :], ACT.Copy).then_inc(sem("qk_hi"), 1)

                def g_v_scalar(n):
                    act.wait_ge(sem("g_v_ps"), n + 1)
                    act.activation(g_v_hi[:, :, :], ps[:, 6, :].rearrange("p (t d) -> p t d", t=TB), ACT.Copy).then_inc(sem("g_v_hi"), 1)

                def g_exp_scalar(h, hh):
                    for t in range(TB):
                        act.wait_ge(sem("score_max"), h * TB + t + 1)
                        act.activation(g_p[:, t, 0:(t + 1) * P], ps[:, t, 0:(t + 1) * P], ACT.Exp, bias=g_st[:, hh % 2, t:t + 1],
                                       accum_out=g_st[:, hh % 2, 4 + t:5 + t]).then_inc(sem("exp"), 1)

                def g_heads_scalar(n, g, tail):
                    for hh in range(4):
                        h = G_HEADS_BEFORE + n * 4 + hh
                        if hh == 3 and not tail:
                            g_qk_scalar(n + 1, g + 1)
                        for c in range(TB):
                            act.wait_ge(sem("pT_ps"), h * TB + c + 1)
                            act.activation(g_pT_hi[:, c, c * P:], ps[:, 4 + c % 3, c * P:], ACT.Copy).then_inc(sem("pT_hi"), 1)
                        if hh < 3 or not tail:
                            g_exp_scalar(h + 1, hh + 1)
                        r = slice(hh * G_HD, (hh + 1) * G_HD)
                        act.wait_ge(sem("head_ps"), h + 1)
                        act.activation(xT_hi[r, g, :], ps[r, 7, :], ACT.Copy).then_inc(sem("g_oT_hi"), 1)
                        if hh == 3 and not tail:
                            g_v_scalar(n + 1)

                with act.Fori(0, B) as i:
                    norm_scalar(act, "g", i)
                    act.wait_ge(sem("g_ctx_in"), 16 * (i + 1))
                    act.activation(g_ctx_hi[:, :], g_ctxT[:, :], ACT.Copy).then_inc(sem("g_ctx_hi"), 1)
                    for m_ in range(C):
                        act.wait_ge(sem("g_q_ps"), i * C + m_ + 1)
                        act.activation(g_qT[:, m_, :], ps[:, 2 + m_ % 2, :], ACT.Copy, scale=G_SCALE).then_inc(sem("g_q"), 1)
                        act.wait_ge(sem("g_k_ps"), i * C + m_ + 1)
                        act.activation(g_kT[:, m_, :], ps[:, 4 + m_ % 2, :], ACT.Copy).then_inc(sem("g_k"), 1)
                    g_v_scalar(i * C)
                    act.wait_ge(sem("g_k"), C * (i + 1))
                    g_qk_scalar(i * C, 0)
                    g_exp_scalar(G_HEADS_BEFORE + i * C * 4, 0)
                    with act.Fori(0, C - 1) as g:
                        g_heads_scalar(i * C + g, g, False)
                    g_heads_scalar(i * C + C - 1, C - 1, True)
                end_stage(act, 6)
            if stages > 7:
                act.wait_ge(sem("h_gw_in"), 16)
                act.activation(h_gw_hi[:, :, :], h_gw[:, :, :], ACT.Copy).then_inc(sem("weights_hi"), 1)

                def h_gu_scalar(m_, u):
                    n = 2 * m_ + u
                    act.wait_ge(sem(f"h_gu_in{u}"), 16 * (m_ + 1))
                    act.wait_ge(sem("h_gu_ps"), n + 1)
                    act.activation(h_w_hi[:, u, 0:2 * D], h_w[:, u, 0:2 * D], ACT.Copy).then_inc(sem("h_gu_hi"), 1)

                def h_d_scalar(m_, u):
                    n = 2 * m_ + u
                    act.wait_ge(sem(f"h_d_in{u}"), 16 * (m_ + 1))
                    act.wait_ge(sem("h_down"), n + 1)
                    act.activation(h_w_hi[:, u, 2 * D:], h_w[:, u, 2 * D:], ACT.Copy).then_inc(sem("h_d_hi"), 1)

                def h_hidden_scalar(n, u):
                    act.wait_ge(sem("h_gu_ps"), n + 3)
                    act.activation(h_sg[:, u, :], ps[:, u, :], ACT.Silu).then_inc(sem("h_sg"), 1)
                    act.wait_ge(sem("h_h"), n + 3)
                    act.activation(h_h_hi[:, u, :], h_h[:, u, :], ACT.Copy).then_inc(sem("h_h_hi"), 1)

                with act.Fori(0, B) as i:
                    h_gu_scalar(i * HC, 0)
                    h_gu_scalar(i * HC, 1)
                    h_d_scalar(i * HC, 0)
                    norm_scalar(act, "h", i)
                    act.wait_ge(sem("h_logit"), i + 1)
                    act.activation(h_l[:, 2, :, :], h_l[:, 1, :, :], ACT.Exp).then_inc(sem("h_le"), 1)
                    with act.Fori(0, HC - 1) as f:
                        m_ = i * HC + f
                        h_hidden_scalar(2 * m_, 0)
                        h_gu_scalar(m_ + 1, 0)
                        h_d_scalar(m_, 1)
                        h_hidden_scalar(2 * m_ + 1, 1)
                        h_gu_scalar(m_ + 1, 1)
                        h_d_scalar(m_ + 1, 0)
                    last = (i + 1) * HC - 1
                    h_hidden_scalar(2 * last, 0)
                    h_d_scalar(last, 1)
                    h_hidden_scalar(2 * last + 1, 1)
                end_stage(act, 7)

        @block.vector
        def _(dve):
            k = InOrder(dve, sem("dve_steps"))
            dve.wait_ge(sem("x_in"), 48)
            dve.wait_ge(sem("consts"), 1)
            dve.wait_ge(sem("tg"), 1)
            dve.wait_ge(sem("weights_hi"), HI_BEFORE["a"] + 2)
            k(dve.tensor_tensor(a_ctx_lo[:, :], a_ctxT[:, :], a_ctx_hi[:, :].bitcast(F32), ALU.subtract))
            dve.tensor_tensor(a_wk_lo[:, :], a_wk[:, :], a_wk_hi[:, :].bitcast(F32), ALU.subtract).then_inc(sem("weights"), 1)
            dve.wait_ge(sem("weights"), READY["a"])
            with dve.Fori(0, B) as i:
                per = 2 * TB + TB * 9
                o = k.enter(i, per)
                norm_vector(dve, k, "a", i)
                dve.wait_ge(sem("a_kvT_hi"), i + 1)
                dve.tensor_tensor(a_kvT_lo[:, :], a_kvT[:, :], a_kvT_hi[:, :].bitcast(F32), ALU.subtract).then_inc(sem("a_kvT"), 1)
                dve.wait_ge(sem("a_kv_hi"), i + 1)
                dve.tensor_tensor(a_kv_lo[:, :, :], ps[:, 3, :].rearrange("p (t d) -> p t d", t=TB),
                                  a_kv_hi[:, :, :].bitcast(F32), ALU.subtract).then_inc(sem("a_kv"), 1)
                dve.wait_ge(sem("a_oT_hi"), i + 1)
                dve.tensor_tensor(a_oT_lo[:, :], ps[:, 4, :], a_oT_hi[:, :].bitcast(F32), ALU.subtract).then_inc(sem("a_oT"), 1)
                for j in range(TB):
                    n = i * TB + j
                    sim = ps[:, 5 + j % 2, :]
                    dve.wait_ge(sem("a_sim_ps"), n + 1)
                    k(dve.bn_stats(a_st[:, 0:6], sim))
                    plain(dve)
                    k(dve.bn_aggr(a_st[:, 11:13], a_st[:, 0:6]))
                    dve.tensor_scalar(a_st[:, 7:8], a_st[:, 12:13], float(D) ** -1, 1e-6, ALU.mult, ALU.add).then_inc(sem("a_sim_var"), 1)
                    dve.wait_ge(sem("a_sim_rstd"), n + 1)
                    k(dve.tensor_scalar(a_st[:, 13:14], a_st[:, 8:9], float(D) ** -0.5, None, ALU.mult))
                    dve.tensor_scalar(a_sim[:, :], sim, a_st[:, 11:12], a_st[:, 13:14], ALU.subtract, ALU.mult)\
                        .then_inc(sem("a_sim_used"), 1)
                    dve.wait_ge(sem("a_sim_used"), n + 1)
                    k(dve.tensor_tensor(a_sim[:, :], a_sim[:, :], a_gamma[:, :], ALU.mult))
                    k(dve.tensor_tensor(a_sim[:, :], a_sim[:, :], a_beta[:, :], ALU.add))
                    k(dve.tensor_reduce(a_st[:, 6:7], a_sim[:, :], AX.X, ALU.max))
                    dve.tensor_scalar(a_st[:, 9:10], a_st[:, 6:7], -1.0, None, ALU.mult).then_inc(sem("a_max"), 1)
                    dve.wait_ge(sem("a_exp"), n + 1)
                    k(dve.reciprocal(a_st[:, 14:15], a_st[:, 10:11]))
                    k(dve.tensor_tensor(a_st[:, 15:16], a_st[:, 14:15], tg[:, 0:1], ALU.mult))
                    k(dve.scalar_tensor_tensor(X[:, n, :], a_exp[:, :], a_st[:, 15:16], X[:, n, :], ALU.mult, ALU.add))
                k.leave(o, B, per)
            end_stage(dve, 0)

            if stages > 1:
                for w, dst in enumerate((b_tsyn[:, :, :].rearrange("p c n -> p (c n)"), b_tout[:, :, :].rearrange("p c n -> p (c n)"))):
                    dve.wait_ge(sem("b_in"), 16 * (w + 1))
                    dve.tensor_reduce(b_st[:, w:w + 1], b_wraw, AX.X, ALU.add, apply_absolute_value=True).then_inc(sem("b_abs"), 1)
                    dve.wait_ge(sem("b_abs_ps"), w + 1)
                    k(dve.tensor_scalar(b_st[:, 2 + w:3 + w], ps[:, 2, 0:1], 1.0 / (HID * D), None, ALU.mult))
                    k(dve.tensor_scalar(b_st[:, 4:5], b_st[:, 2 + w:3 + w], 1e-8, 0.5, ALU.add, ALU.mult))
                    k(dve.tensor_scalar(b_st[:, 5:6], b_st[:, 4:5], -1.0, None, ALU.mult))
                    for h in range(2):
                        half = slice(h * 2 * HID, (h + 1) * 2 * HID)
                        k(dve.tensor_scalar(b_tmp, b_wraw[:, half], b_st[:, 5:6], None, ALU.is_lt))
                        k(dve.scalar_tensor_tensor(dst[:, half], b_wraw[:, half], b_st[:, 4:5], b_tmp, ALU.is_gt, ALU.subtract))
                    dve.sem_inc(sem("b_raw_used"), 1)
                dve.wait_ge(sem("b_raw_used"), 2)
                dve.wait_ge(sem("b_rows_in"), 64)
                k(dve.tensor_scalar(b_rows[:, 1:3, :], b_rows[:, 1:3, :], tg[:, 4:5], None, ALU.mult))
                dve.sem_inc(sem("weights"), 1)
                with dve.Fori(0, B) as i:
                    per = 2 * TB + TB + 3 + 3 + ROUNDS * SEARCH_STEPS + 1 + TB + TB * 7
                    o = k.enter(i, per)
                    norm_vector(dve, k, "b", i)
                    for j in range(TB):
                        for q in range(4):
                            n = (i * TB + j) * 4 + q
                            dve.wait_ge(sem("b_z_ps"), n + 1)
                            dve.scalar_tensor_tensor(b_z[:, j, q * BANK:(q + 1) * BANK], ps[:, 4 + q, :], b_st[:, 2:3],
                                                     b_bsyn[:, q * BANK:(q + 1) * BANK], ALU.mult, ALU.add).then_inc(sem("b_z_used"), 1)
                    low, step, other, cand, cnt, take = (b_tk[:, r, :] for r in range(6))
                    dve.wait_ge(sem("b_z_used"), 16 * (i + 1))
                    for j in range(TB):
                        k(dve.tensor_reduce(step[:, j:j + 1], b_z[:, j, :], AX.X, ALU.max))
                    k(dve.tensor_scalar(step, step, 0.0, 0.5, ALU.max, ALU.mult))
                    k(dve.memset(low, 0.0))
                    k(dve.tensor_copy(cand, step))
                    search_vector(dve, k, i, b_z, b_junk[:, 0, :], low, step, other, cand, cnt, take, SYN_K)
                    search_vector_end(dve, k, "b", i, low)
                    for j in range(TB):
                        k(dve.scalar_tensor_tensor(b_z[:, j, :], b_z[:, j, :], low[:, j:j + 1], b_z[:, j, :], ALU.is_ge, ALU.mult))
                        dve.sem_inc(sem("b_h"), 1)
                    for j in range(TB):
                        n = i * TB + j
                        for q in range(4):
                            dve.wait_ge(sem("b_hT_hi"), n * 4 + q + 1)
                            dve.tensor_tensor(b_hT_lo[:, 4 * q:4 * q + 4, :], ps[:, q, :].rearrange("p (c t) -> p c t", c=4),
                                              b_hT_hi[:, 4 * q:4 * q + 4, :].bitcast(F32), ALU.subtract).then_inc(sem("b_hT"), 1)
                        dve.wait_ge(sem("b_y_ps"), n + 1)
                        dve.scalar_tensor_tensor(b_y[:, :], ps[:, 4, :], b_st[:, 3:4], xn[:, j, :], ALU.mult, ALU.add)\
                            .then_inc(sem("b_y_used"), 1)
                        dve.wait_ge(sem("b_y_used"), n + 1)
                        k(dve.tensor_tensor(b_y[:, :], b_y[:, :], b_rows[:, 0, :], ALU.add))
                        k(dve.bn_stats(b_st[:, 9:15], b_y[:, :]))
                        plain(dve)
                        k(dve.bn_aggr(b_st[:, 4:6], b_st[:, 9:15]))
                        dve.tensor_scalar(b_st[:, 7:8], b_st[:, 5:6], LN_EPS, None, ALU.add).then_inc(sem("b_y_var"), 1)
                        dve.wait_ge(sem("b_y_rstd"), n + 1)
                        k(dve.tensor_scalar(b_y[:, :], b_y[:, :], b_st[:, 4:5], b_st[:, 8:9], ALU.subtract, ALU.mult))
                        k(dve.tensor_tensor(b_y[:, :], b_y[:, :], b_rows[:, 1, :], ALU.mult))
                        k(dve.tensor_tensor(b_y[:, :], b_y[:, :], b_rows[:, 2, :], ALU.add))
                        k(dve.tensor_tensor(X[:, n, :], X[:, n, :], b_y[:, :], ALU.add))
                    k.leave(o, B, per)
                end_stage(dve, 1)

            if stages > 2:
                dve.wait_ge(sem("c_in"), 48)
                dve.wait_ge(sem("weights_hi"), HI_BEFORE["c"] + 2)
                k(dve.tensor_tensor(c_ctx_lo[:, :], c_ctxT[:, :], c_ctx_hi[:, :].bitcast(F32), ALU.subtract))
                dve.tensor_tensor(c_w_lo[:, :, :], c_w[:, :, :], c_w_hi[:, :, :].bitcast(F32), ALU.subtract).then_inc(sem("weights"), 1)
                dve.wait_ge(sem("c_g"), 1)
                k(dve.tensor_scalar(c_g[:, 1:2], c_g[:, 1:2], 1.0, None, ALU.add))
                k(dve.reciprocal(c_g[:, 1:2], c_g[:, 1:2]))
                k(dve.tensor_scalar(c_g[:, 2:3], c_g[:, 1:2], -1.0, 1.0, ALU.mult, ALU.add))
                k(dve.tensor_tensor(c_g[:, 2:3], c_g[:, 2:3], tg[:, 1:2], ALU.mult))
                k(dve.tensor_scalar(c_g[:, 3:4], c_g[:, 1:2], 0.5, None, ALU.mult))
                k(dve.tensor_tensor(c_g[:, 3:4], c_g[:, 3:4], tg[:, 1:2], ALU.mult))
                with dve.Fori(0, B) as i:
                    per = 2 * TB + 2 * TB + 3 + 3 + ROUNDS * SEARCH_STEPS + 1 + 3 * TB + 2 * TB
                    o = k.enter(i, per)
                    norm_vector(dve, k, "c", i)
                    for w in range(2):
                        dve.wait_ge(sem("c_qk_hi"), i * 2 + w + 1)
                        dve.tensor_tensor(c_qk_lo[:, w, :], ps[:, 2 + w, :], c_qk_hi[:, w, :].bitcast(F32), ALU.subtract)\
                            .then_inc(sem("c_qk"), 1)
                    low, step, other, cand, cnt, take = (c_tk[:, r, :] for r in range(6))
                    dve.wait_ge(sem("c_sim"), TB * (i + 1))
                    for j in range(TB):
                        k(dve.tensor_reduce(step[:, j:j + 1], c_sim[:, j, :], AX.X, ALU.max))
                        k(dve.tensor_reduce(low[:, j:j + 1], c_sim[:, j, :], AX.X, ALU.min))
                    k(dve.tensor_tensor(step, step, low, ALU.subtract))
                    k(dve.tensor_scalar(step, step, 0.5, None, ALU.mult))
                    k(dve.tensor_tensor(cand, low, step, ALU.add))
                    search_vector(dve, k, i, c_sim, c_junk[:, 0, :], low, step, other, cand, cnt, take, SIM_K)
                    search_vector_end(dve, k, "c", i, low)
                    dve.wait_ge(sem("c_e"), TB * (i + 1))
                    for j in range(TB):
                        k(dve.tensor_scalar(c_a[:, j, :], c_a[:, j, :], 1.0, None, ALU.add))
                        k(dve.reciprocal(c_a[:, j, :], c_a[:, j, :]))
                        k(dve.scalar_tensor_tensor(c_a[:, j, :], c_sim[:, j, :], low[:, j:j + 1], c_a[:, j, :], ALU.is_ge, ALU.mult))
                    dve.sem_inc(sem("c_A"), 1)
                    for j in range(TB):
                        n = i * TB + j
                        k(dve.scalar_tensor_tensor(X[:, n, :], xn[:, j, :], c_g[:, 2:3], X[:, n, :], ALU.mult, ALU.add))
                        dve.wait_ge(sem("c_AT_ps"), n + 1)
                        dve.tensor_tensor(c_t[:, :], ps[:, 6 + j % 2, :], c_a[:, j, :], ALU.add).then_inc(sem("c_AT_used"), 1)
                        dve.wait_ge(sem("c_AT_used"), n + 1)
                        k(dve.scalar_tensor_tensor(X[:, n, :], c_t[:, :], c_g[:, 3:4], X[:, n, :], ALU.mult, ALU.add))
                    k.leave(o, B, per)
                end_stage(dve, 2)

            if stages > 3:
                dve.wait_ge(sem("d_in"), 48)
                for c in range(C):
                    dve.tensor_tensor(d_w[:, c, :], d_w[:, c, :], d_rows[:, 0, :], ALU.mult).then_inc(sem("d_ws"), 1)
                k(dve.tensor_scalar(d_rows[:, 1, :], d_rows[:, 1, :], tg[:, 5:6], None, ALU.mult))
                dve.wait_ge(sem("weights_hi"), HI_BEFORE["d"] + 1)
                dve.tensor_tensor(d_w_lo[:, :, :], d_w[:, :, :], d_w_hi[:, :, :].bitcast(F32), ALU.subtract).then_inc(sem("weights"), 1)
                with dve.Fori(0, B) as i:
                    per = 2 * TB + TB
                    o = k.enter(i, per)
                    norm_vector(dve, k, "d", i)
                    for j in range(TB):
                        n = i * TB + j
                        k(dve.tensor_tensor(X[:, n, :], X[:, n, :], d_rows[:, 1, :], ALU.add))
                        dve.wait_ge(sem("y_ps"), n + 1)
                        dve.scalar_tensor_tensor(X[:, n, :], ps[:, 2 + j % 2, :], tg[:, 5:6], X[:, n, :], ALU.mult, ALU.add)\
                            .then_inc(sem("y_used"), 1)
                    dve.wait_ge(sem("y_used"), TB * (i + 1))
                    k.leave(o, B, per)
                end_stage(dve, 3)

            if stages > 4:
                dve.wait_ge(sem("e_tables"), 32)
                dve.memset(e_zero[:, :].bitcast(F32), 0.0).then_inc(sem("e_zero"), 1)

                def e_qk_vector(turn, d):
                    u = d % 2
                    for w in range(2):
                        dve.wait_ge(sem("qk_hi"), turn * E_BODY + d * 2 + w + 1)
                        dve.tensor_tensor(e_qk_lo[:, u, w, :], ps[:, 2 + w, :], e_qk_hi[:, u, w, :].bitcast(F32), ALU.subtract)\
                            .then_inc(sem("qk"), 1)

                def e_max_vector(h, a):
                    for t in range(TB):
                        dve.wait_ge(sem("scores_ps"), h * TB + t + 1)
                        dve.tensor_reduce(e_st[:, a, t:t + 1], ps[:, t % 2, :], AX.X, ALU.max, negate=True).then_inc(sem("score_max"), 1)

                def e_scale_vector(h, a):
                    dve.wait_ge(sem("exp"), TB * (h + 1))
                    k(dve.reciprocal(e_st[:, a, 8:12], e_st[:, a, 4:8]))
                    for t in range(TB):
                        dve.tensor_scalar(e_p[:, a, t, :], e_p[:, a, t, :], e_st[:, a, 8 + t:9 + t], None, ALU.mult).then_inc(sem("e_p"), 1)

                def e_head_vector(turn, hh, tail):
                    h = turn * E_BODY + hh
                    more = not (tail and hh == E_BODY - 1)
                    if more:
                        e_max_vector(h + 1, (hh + 1) % 2)
                    for c in range(TB):
                        dve.wait_ge(sem("pT_hi"), h * TB + c + 1)
                        dve.tensor_tensor(e_pT_lo[:, c, :], ps[:, 2 + c % 2, :], e_pT_hi[:, c, :].bitcast(F32), ALU.subtract)\
                            .then_inc(sem("pT"), 1)
                    if more:
                        e_scale_vector(h + 1, (hh + 1) % 2)
                    dve.wait_ge(sem("head_hi"), h + 1)
                    dve.tensor_tensor(e_cT_lo[:, hh % 2, :], ps[:, 1, :], e_cT_hi[:, hh % 2, :].bitcast(F32), ALU.subtract)\
                        .then_inc(sem("head_out"), 1)
                    if hh % 2 == 0 and not (tail and hh == E_BODY - 2):
                        e_qk_vector(turn, hh // 2 + 1)

                with dve.Fori(0, E_HEADS // 2) as i:
                    for u in range(2):
                        n = i * 2 + u
                        dve.wait_ge(sem("e_mg_hi"), 2 * (n + 1))
                        m_ = [e_qkw[:, 0, q, 0:4 * P].rearrange("p (c n) -> p c n", c=C)[:, :, u * E_R:(u + 1) * E_R] for q in range(2)]
                        g_ = [e_g[:, 0, q, u * D:(u + 1) * D] for q in range(2)]
                        dve.tensor_tensor(m_[1], ps[:, 1, 0:C * E_R].rearrange("p (c n) -> p c n", c=C), m_[0].bitcast(F32),
                                          ALU.subtract).then_inc(sem("e_mg"), 1)
                        dve.tensor_tensor(g_[1], ps[:, 2, :], g_[0].bitcast(F32), ALU.subtract).then_inc(sem("e_mg"), 1)
                    dve.wait_ge(sem("e_wkr_hi"), i + 1)
                    dve.wait_ge(sem("e_mg"), 4 * (i + 1) + 1)
                    dve.tensor_tensor(e_qkw[:, 0, 1, 4 * P:5 * P], e_wkr[:, :], e_qkw[:, 0, 0, 4 * P:5 * P].bitcast(F32), ALU.subtract)\
                        .then_inc(sem("e_pair_made"), 1)
                    dve.wait_ge(sem("e_pair_made"), i + 1)
                    dve.sem_inc(sem("e_blob_used"), 1)
                with dve.Fori(0, B) as i:
                    per = 2 * TB + 4 + E_HEADS
                    o = k.enter(i, per)
                    norm_vector(dve, k, "e", i)
                    dve.wait_ge(sem("e_ctx_in"), 16 * (i + 1))
                    hd = DC // 2
                    k(dve.tensor_tensor(e_rot[:, :, 0:hd], e_ctx[:, :, hd:DC], e_sin[:, :, 0:hd], ALU.mult))
                    k(dve.tensor_tensor(e_rot[:, :, hd:DC], e_ctx[:, :, 0:hd], e_sin[:, :, hd:DC], ALU.mult))
                    k(dve.tensor_tensor(e_kvr[:, :, :], e_ctx[:, :, :], e_cos[:, :, :], ALU.mult))
                    dve.tensor_tensor(e_kvr[:, :, :], e_kvr[:, :, :], e_rot[:, :, :], ALU.add).then_inc(sem("e_kvr"), 1)
                    dve.wait_ge(sem("e_kvr"), i + 1)
                    dve.sem_inc(sem("e_ctx_used"), 1)
                    dve.wait_ge(sem("e_kvr_hi"), i + 1)
                    k(dve.tensor_tensor(e_kvr_lo[:, :, :], e_kvr[:, :, :], e_kvr_hi[:, :, :].bitcast(F32), ALU.subtract))
                    dve.wait_ge(sem("e_kT_hi"), i + 1)
                    dve.tensor_tensor(e_kT_lo[:, :], ps[:, 2, :], e_kT_hi[:, :].bitcast(F32), ALU.subtract).then_inc(sem("e_kT"), 1)
                    plain(dve)
                    e_qk_vector(i * E_TURNS, 0)
                    e_max_vector(E_HEADS * i, 0)
                    e_scale_vector(E_HEADS * i, 0)
                    plain(dve)
                    with dve.Fori(0, E_TURNS - 1) as g:
                        p2 = k.enter(g, E_BODY)
                        for hh in range(E_BODY):
                            e_head_vector(i * E_TURNS + g, hh, False)
                        k.leave(p2, E_TURNS - 1, E_BODY)
                    for hh in range(E_BODY):
                        e_head_vector((i + 1) * E_TURNS - 1, hh, True)
                    dve.wait_ge(sem("e_y_ps"), i + 1)
                    for j in range(TB):
                        n = i * TB + j
                        dve.scalar_tensor_tensor(X[:, n, :], ps[:, 4 + j, :], tg[:, 2:3], X[:, n, :], ALU.mult, ALU.add)\
                            .then_inc(sem("e_y_used"), 1)
                    dve.wait_ge(sem("e_y_used"), TB * (i + 1))
                    k.leave(o, B, per)
                end_stage(dve, 4)

            if stages > 5:
                dve.wait_ge(sem("weights_hi"), HI_BEFORE["f"] + 2)
                k(dve.tensor_tensor(f_w_lo[:, :, :], f_w[:, :, :], f_w_hi[:, :, :].bitcast(F32), ALU.subtract))
                k(dve.tensor_tensor(f_d_lo[:, :], f_d[:, :], f_d_hi[:, :].bitcast(F32), ALU.subtract))
                dve.tensor_tensor(f_q[:, :, :], f_q[:, :, :], f_w[:, :, :], ALU.mult).then_inc(sem("weights"), 1)
                dve.wait_ge(sem("f_const_ps"), 1)
                k(dve.tensor_copy(f_const[:, :], ps[:, 2, 0:F_N]))
                with dve.Fori(0, B) as i:
                    per = 2 * TB + 36
                    o = k.enter(i, per)
                    norm_vector(dve, k, "f", i)
                    for j in range(TB):
                        n = i * TB + j
                        dve.wait_ge(sem("f_a_ps"), n + 1)
                        k(dve.tensor_tensor(f_a[:, j, 0:P], ps[:, 2 + j % 2, 0:P], f_const[:, 0:P], ALU.subtract))
                        dve.scalar_tensor_tensor(f_a[:, j, P:F_N], ps[:, 2 + j % 2, P:F_N], -2.0, f_const[:, P:F_N], ALU.mult, ALU.add)\
                            .then_inc(sem("f_a"), 1)
                    dve.wait_ge(sem("f_a"), TB * (i + 1))
                    k(dve.tensor_tensor(f_sq[:, :, :], f_a[:, :, 0:64], f_a[:, :, 0:64], ALU.mult))
                    score, pri = f_g[:, 2, :, :], f_g[:, 3, :, :]
                    k(dve.tensor_reduce(score, f_sq[:, :, :].rearrange("p t (n s) -> p t n s", n=8), AX.X, ALU.add))
                    dve.wait_ge(sem("f_xx"), TB * (i + 1))
                    for j in range(TB):
                        k(dve.tensor_scalar(f_a[:, j, P:F_N], f_a[:, j, P:F_N], f_xx[:, j:j + 1], None, ALU.add))
                    k(dve.reciprocal(f_g[:, 4, :, :], f_a[:, :, P:F_N]))
                    k(dve.tensor_tensor(score, score, f_g[:, 4, :, :], ALU.mult))
                    for j in range(TB):
                        k(dve.tensor_tensor(f_g[:, 4, j, :], score[:, j, :], f_rows[:, 0, :], ALU.subtract))
                    for j in range(TB):
                        k(dve.tensor_tensor(f_g[:, 0, j, :], f_g[:, 4, j, :], f_rows[:, 1, :], ALU.mult))
                    dve.sem_inc(sem("f_z"), 1)
                    dve.wait_ge(sem("f_e"), i + 1)
                    gate = f_g[:, 1, :, :]
                    k(dve.tensor_scalar(gate, gate, 1.0, None, ALU.add))
                    k(dve.reciprocal(gate, gate))
                    top = f_s[:, 0, :]
                    k(dve.tensor_reduce(top, gate, AX.X, ALU.max))
                    k(dve.tensor_tensor(pri, gate, top.unsqueeze(2).broadcast_to([P, TB, 8]), ALU.is_ge))
                    for j in range(TB):
                        k(dve.tensor_tensor(pri[:, j, :], pri[:, j, :], f_rows[:, 2, :], ALU.mult))
                    k(dve.tensor_reduce(f_s[:, 1, :], pri, AX.X, ALU.max))
                    hot = f_m[:, :, 64:72]
                    k(dve.tensor_tensor(hot, pri, f_s[:, 1, :].unsqueeze(2).broadcast_to([P, TB, 8]), ALU.is_equal))
                    for j in range(TB):
                        dve.tensor_tensor(f_m[:, j, 0:64].rearrange("p (n h) -> p n h", n=8),
                                          f_a[:, j, 64:P].rearrange("p (n h) -> p n h", n=8),
                                          hot[:, j, :].unsqueeze(2).broadcast_to([P, 8, 8]), ALU.mult).then_inc(sem("f_m"), 1)
                    k(dve.tensor_scalar(f_s[:, 2, :], top, tg[:, 6:7], None, ALU.mult))
                    k(dve.tensor_scalar(f_s[:, 3, :], f_s[:, 2, :], -1.0, tg[:, 6:7], ALU.mult, ALU.add))
                    dve.wait_ge(sem("f_mT_hi"), i + 1)
                    dve.tensor_tensor(f_mT_lo[:, :], ps[0:F_K, 4, :], f_mT_hi[:, :].bitcast(F32), ALU.subtract).then_inc(sem("f_mT"), 1)
                    for j in range(TB):
                        n = i * TB + j
                        k(dve.scalar_tensor_tensor(X[:, n, :], xn[:, j, :], f_s[:, 3, j:j + 1], X[:, n, :], ALU.mult, ALU.add))
                        dve.wait_ge(sem("y_ps"), 1 * TILES + n + 1)
                        dve.scalar_tensor_tensor(X[:, n, :], ps[:, 6 + j % 2, :], f_s[:, 2, j:j + 1], X[:, n, :], ALU.mult, ALU.add)\
                            .then_inc(sem("y_used"), 1)
                    dve.wait_ge(sem("y_used"), 1 * TILES + TB * (i + 1))
                    k.leave(o, B, per)
                end_stage(dve, 5)

            if stages > 6:
                for n, (dst, hi) in enumerate(((g_wq_lo, g_wq_hi), (g_wo_lo, g_wo_hi))):
                    dve.wait_ge(sem("weights_hi"), HI_BEFORE["g"] + n + 1)
                    dve.tensor_tensor(dst[:, :, :], g_w[:, :, :], hi[:, :, :].bitcast(F32), ALU.subtract).then_inc(sem("g_raw_used"), 1)
                dve.wait_ge(sem("weights_hi"), HI_BEFORE["g"] + 5)
                dve.tensor_tensor(g_wkv_lo[:, :], g_w[:, 0:2, :].rearrange("p a n -> p (a n)"), g_wkv_hi[:, :].bitcast(F32), ALU.subtract)\
                    .then_inc(sem("weights"), 1)

                def g_qk_vector(n, g):
                    for w, src in enumerate((g_qT, g_kT)):
                        dve.wait_ge(sem("qk_hi"), G_HEADS_BEFORE + n * 2 + w + 1)
                        dve.tensor_tensor(g_qk_lo[:, w, :], src[:, g, :], g_qk_hi[:, w, :].bitcast(F32), ALU.subtract).then_inc(sem("qk"), 1)

                def g_v_vector(n):
                    dve.wait_ge(sem("g_v_hi"), n + 1)
                    dve.tensor_tensor(g_v_lo[:, :, :], ps[:, 6, :].rearrange("p (t d) -> p t d", t=TB), g_v_hi[:, :, :].bitcast(F32), ALU.subtract)\
                        .then_inc(sem("g_v"), 1)

                def g_diag_vector(h, hh):
                    dve.wait_ge(sem("exp"), (h + 1) * TB)
                    k(dve.reciprocal(g_st[:, hh % 2, 4:8], g_st[:, hh % 2, 4:8]))
                    for t in range(TB):
                        dve.tensor_scalar(g_diag[:, t, :], ident[:, :], g_st[:, hh % 2, 4 + t:5 + t], None, ALU.mult).then_inc(sem("g_diag"), 1)

                def g_max_vector(h, hh):
                    for t in range(TB):
                        dve.wait_ge(sem("scores_ps"), h * TB + t + 1)
                        dve.tensor_reduce(g_st[:, hh % 2, t:t + 1], ps[:, t, 0:(t + 1) * P], AX.X, ALU.max, negate=True).then_inc(sem("score_max"), 1)

                def g_heads_vector(n, g, tail):
                    for hh in range(4):
                        h = G_HEADS_BEFORE + n * 4 + hh
                        if hh == 3 and not tail:
                            g_qk_vector(n + 1, g + 1)
                        for c in range(TB):
                            dve.wait_ge(sem("pT_hi"), h * TB + c + 1)
                            dve.tensor_tensor(g_pT_lo[:, c, c * P:], ps[:, 4 + c % 3, c * P:], g_pT_hi[:, c, c * P:].bitcast(F32), ALU.subtract)\
                                .then_inc(sem("pT"), 1)
                        if hh < 3 or not tail:
                            g_max_vector(h + 1, hh + 1)
                            g_diag_vector(h + 1, hh + 1)
                        r = slice(hh * G_HD, (hh + 1) * G_HD)
                        dve.wait_ge(sem("g_oT_hi"), h - G_HEADS_BEFORE + 1)
                        dve.tensor_tensor(xT_lo[r, g, :], ps[r, 7, :], xT_hi[r, g, :].bitcast(F32), ALU.subtract).then_inc(sem("head_out"), 1)
                        if hh == 3 and not tail:
                            g_v_vector(n + 1)

                with dve.Fori(0, B) as i:
                    per = 2 * TB + C * 4
                    o = k.enter(i, per)
                    norm_vector(dve, k, "g", i)
                    dve.wait_ge(sem("g_ctx_hi"), i + 1)
                    dve.tensor_tensor(g_ctx_lo[:, :], g_ctxT[:, :], g_ctx_hi[:, :].bitcast(F32), ALU.subtract).then_inc(sem("g_ctx_used"), 1)
                    g_v_vector(i * C)
                    plain(dve)
                    g_qk_vector(i * C, 0)
                    g_max_vector(G_HEADS_BEFORE + i * C * 4, 0)
                    g_diag_vector(G_HEADS_BEFORE + i * C * 4, 0)
                    plain(dve)
                    with dve.Fori(0, C - 1) as g:
                        o2 = k.enter(g, 4)
                        g_heads_vector(i * C + g, g, False)
                    k.leave(o2, C - 1, 4)
                    g_heads_vector(i * C + C - 1, C - 1, True)
                    for j in range(TB):
                        n = i * TB + j
                        dve.wait_ge(sem("y_ps"), 2 * TILES + n + 1)
                        dve.scalar_tensor_tensor(X[:, n, :], ps[:, 2 + j % 2, :], tg[:, 3:4], X[:, n, :], ALU.mult, ALU.add)\
                            .then_inc(sem("y_used"), 1)
                    dve.wait_ge(sem("y_used"), 2 * TILES + TB * (i + 1))
                    k.leave(o, B, per)
                end_stage(dve, 6)

            if stages > 7:
                dve.wait_ge(sem("weights_hi"), HI_BEFORE["h"] + 1)
                dve.memset(h_zero[:, :].bitcast(F32), 0.0).then_inc(sem("h_zero"), 1)
                dve.tensor_tensor(h_gw_lo[:, :, :], h_gw[:, :, :], h_gw_hi[:, :, :].bitcast(F32), ALU.subtract).then_inc(sem("weights"), 1)

                def h_gu_vector(n, u):
                    dve.wait_ge(sem("h_gu_hi"), n + 1)
                    dve.tensor_tensor(h_w_lo[:, u, 0:2 * D], h_w[:, u, 0:2 * D], h_w_hi[:, u, 0:2 * D].bitcast(F32), ALU.subtract)\
                        .then_inc(sem("h_gu_used"), 1)

                def h_d_vector(n, u):
                    dve.wait_ge(sem("h_d_hi"), n + 1)
                    dve.tensor_tensor(h_w_lo[:, u, 2 * D:], h_w[:, u, 2 * D:], h_w_hi[:, u, 2 * D:].bitcast(F32), ALU.subtract)\
                        .then_inc(sem("h_d_used"), 1)

                def h_hidden_vector(n, u, e):
                    dve.wait_ge(sem("h_sg"), n + 1)
                    k(dve.tensor_tensor(h_sg[:, u, :], ps[:, 2 + u, :], h_sg[:, u, :], ALU.mult))
                    dve.tensor_tensor(h_h[:, u, :], h_sg[:, u, :], h_gain[:, e, :], ALU.mult).then_inc(sem("h_h"), 1)
                    dve.wait_ge(sem("h_h_hi"), n + 1)
                    dve.tensor_tensor(h_h_lo[:, u, :], h_h[:, u, :], h_h_hi[:, u, :].bitcast(F32), ALU.subtract).then_inc(sem("h_h_lo"), 1)

                with dve.Fori(0, B) as i:
                    per = 2 * TB + 9 + 2 * TB - 1 + 2 * HC
                    o = k.enter(i, per)
                    first = i * 2 * HC
                    h_gu_vector(first, 0)
                    h_gu_vector(first + 1, 1)
                    h_d_vector(first, 0)
                    norm_vector(dve, k, "h", i)
                    dve.wait_ge(sem("h_l_ps"), i + 1)
                    k(dve.tensor_copy(h_l[:, 0, :, :], ps[:, 0, 0:2 * TB].rearrange("p (t e) -> p t e", t=TB)))
                    k(dve.tensor_reduce(h_s[:, 0, :], h_l[:, 0, :, :], AX.X, ALU.max))
                    dve.tensor_tensor(h_l[:, 1, :, :], h_l[:, 0, :, :], h_s[:, 0, :].unsqueeze(2).broadcast_to([P, TB, 2]), ALU.subtract)\
                        .then_inc(sem("h_logit"), 1)
                    dve.wait_ge(sem("h_le"), i + 1)
                    ee = h_l[:, 2, :, :]
                    k(dve.tensor_reduce(h_s[:, 1, :], ee, AX.X, ALU.add))
                    k(dve.reciprocal(h_s[:, 1, :], h_s[:, 1, :]))
                    k(dve.tensor_tensor(h_l[:, 3, :, :], ee, h_s[:, 1, :].unsqueeze(2).broadcast_to([P, TB, 2]), ALU.mult))
                    p0, p1 = h_l[:, 3, :, 0], h_l[:, 3, :, 1]
                    k(dve.tensor_tensor(h_l[:, 4, :, 1], p1, p0, ALU.is_gt))
                    k(dve.tensor_scalar(h_l[:, 4, :, 0], h_l[:, 4, :, 1], -1.0, 1.0, ALU.mult, ALU.add))
                    k(dve.tensor_tensor(h_l[:, 5, :, :], h_l[:, 4, :, :], h_l[:, 3, :, :], ALU.mult))
                    k(dve.tensor_scalar(h_l[:, 5, :, :], h_l[:, 5, :, :], tg[:, 7:8], None, ALU.mult))
                    for n in range(2 * TB):
                        e, j = n // TB, n % TB
                        t = dve.tensor_scalar(h_diag[:, e, j * P:(j + 1) * P], ident[:, :], h_l[:, 5, j, e:e + 1], None, ALU.mult)
                        k(t) if n < 2 * TB - 1 else t.then_inc(sem("h_diag"), 1)
                    dve.wait_ge(sem("h_gain_ps"), i + 1)
                    dve.tensor_copy(h_gain[:, :, :], ps[:, 2:4, :]).then_inc(sem("h_gain"), 1)
                    dve.wait_ge(sem("h_gain"), i + 1)
                    for e in range(2):
                        turns = HC // 2 - e
                        plain(dve)
                        with dve.Fori(0, turns) as f:
                            o2 = k.enter(f, 2)
                            n = first + e * HC + 2 * f
                            h_hidden_vector(n, 0, e)
                            h_gu_vector(n + 2, 0)
                            h_d_vector(n + 1, 1)
                            h_hidden_vector(n + 1, 1, e)
                            h_gu_vector(n + 3, 1)
                            h_d_vector(n + 2, 0)
                        k.leave(o2, turns, 2)
                    last = first + 2 * HC - 2
                    h_hidden_vector(last, 0, 1)
                    h_d_vector(last + 1, 1)
                    h_hidden_vector(last + 1, 1, 1)
                    dve.wait_ge(sem("h_y_ps"), i + 1)
                    for j in range(TB):
                        n = i * TB + j
                        dve.tensor_tensor(X[:, n, :], ps[:, 4 + j, :], X[:, n, :], ALU.add).then_inc(sem("h_y_used"), 1)
                    dve.wait_ge(sem("h_y_used"), TB * (i + 1))
                    k.leave(o, B, per)
                end_stage(dve, 7)

        @block.tensor
        def _(pe):
            pe.wait_ge(sem("consts"), 1)
            pe.wait_ge(sem("weights"), READY["a"])
            with pe.Fori(0, B) as i:
                norm_tensor(pe, "a", i)
                mm3(pe, ps[:, 2, :], a_wk_hi[:, :], a_wk_lo[:, :], a_ctx_hi[:, bass.ts(i, S)], a_ctx_lo[:, bass.ts(i, S)],
                    True, True).then_inc(sem("a_kvT_ps"), 1)
                pe.wait_ge(sem("a_kvT"), i + 1)
                for j in range(TB):
                    t = pe.transpose(ps[:, 3, j * P:(j + 1) * P], a_kvT[:, j * P:(j + 1) * P], ident[:, :])
                t.then_inc(sem("a_kv_ps"), 1)
                pe.wait_ge(sem("a_kv"), i + 1)
                for j in range(TB):
                    t = mm3(pe, ps[:, 4, :], a_kv_hi[:, j, :], a_kv_lo[:, j, :], xT_hi[:, j, :], xT_lo[:, j, :], j == 0, j == TB - 1)
                t.then_inc(sem("a_oT_ps"), 1)
                pe.wait_ge(sem("a_oT"), i + 1)
                for j in range(TB):
                    if j >= 2:
                        pe.wait_ge(sem("a_sim_used"), i * TB + j - 1)
                    q = slice(j * P, (j + 1) * P)
                    mm3(pe, ps[:, 5 + j % 2, :], a_oT_hi[:, q], a_oT_lo[:, q], a_kvT_hi[:, :], a_kvT_lo[:, :], True, True)\
                        .then_inc(sem("a_sim_ps"), 1)
            end_stage(pe, 0)
            if stages > 1:
                for w in range(2):
                    pe.wait_ge(sem("b_abs"), w + 1)
                    pe.matmul(ps[:, 2, 0:1], ones[:, :], b_st[:, w:w + 1], start=True, stop=True).then_inc(sem("b_abs_ps"), 1)
                pe.wait_ge(sem("weights"), READY["b"])
                with pe.Fori(0, B) as i:
                    norm_tensor(pe, "b", i)
                    for j in range(TB):
                        for q in range(4):
                            n = (i * TB + j) * 4 + q
                            if j >= 1:
                                pe.wait_ge(sem("b_z_used"), n - 3)
                            for c in range(C):
                                for part in (xT_hi, xT_lo):
                                    t = pe.matmul(ps[:, 4 + q, :], part[:, c, j * P:(j + 1) * P], b_tsyn[:, c, q * BANK:(q + 1) * BANK],
                                                  start=(c == 0 and part is xT_hi), stop=(c == C - 1 and part is xT_lo))
                            t.then_inc(sem("b_z_ps"), 1)
                    for j in range(TB):
                        n = i * TB + j
                        pe.wait_ge(sem("b_h"), n + 1)
                        for q in range(4):
                            for c in range(4):
                                t = pe.transpose(ps[:, q, c * P:(c + 1) * P], b_z[:, j, (4 * q + c) * P:(4 * q + c + 1) * P], ident[:, :])
                            t.then_inc(sem("b_hT_ps"), 1)
                        pe.wait_ge(sem("b_hT"), 4 * (n + 1))
                        for c in range(HC):
                            for part in (b_hT_hi, b_hT_lo):
                                t = pe.matmul(ps[:, 4, :], part[:, c, :], b_tout[:, c, :],
                                              start=(c == 0 and part is b_hT_hi), stop=(c == HC - 1 and part is b_hT_lo))
                        t.then_inc(sem("b_y_ps"), 1)
                        pe.wait_ge(sem("b_y_used"), n + 1)
                end_stage(pe, 1)
            if stages > 2:
                pe.wait_ge(sem("weights"), READY["c"])
                with pe.Fori(0, B) as i:
                    norm_tensor(pe, "c", i)
                    for w in range(2):
                        mm3(pe, ps[:, 2 + w, :], c_w_hi[:, w, :], c_w_lo[:, w, :], c_ctx_hi[:, bass.ts(i, S)],
                            c_ctx_lo[:, bass.ts(i, S)], True, True).then_inc(sem("c_qk_ps"), 1)
                    pe.wait_ge(sem("c_qk"), 2 * (i + 1))
                    for j in range(TB):
                        if j >= 2:
                            pe.wait_ge(sem("c_sim"), i * TB + j - 1)
                        q = slice(j * P, (j + 1) * P)
                        mm3(pe, ps[:, 4 + j % 2, :], c_qk_hi[:, 0, q], c_qk_lo[:, 0, q], c_qk_hi[:, 1, :], c_qk_lo[:, 1, :],
                            True, True).then_inc(sem("c_sim_ps"), 1)
                    pe.wait_ge(sem("c_A"), i + 1)
                    for j in range(TB):
                        if j >= 2:
                            pe.wait_ge(sem("c_AT_used"), i * TB + j - 1)
                        for c in range(TB):
                            t = pe.transpose(ps[:, 6 + j % 2, c * P:(c + 1) * P], c_a[:, c, j * P:(j + 1) * P], ident[:, :])
                        t.then_inc(sem("c_AT_ps"), 1)
                    pe.wait_ge(sem("c_AT_used"), TB * (i + 1))
                end_stage(pe, 2)
            if stages > 3:
                pe.wait_ge(sem("weights"), READY["d"])
                with pe.Fori(0, B) as i:
                    norm_tensor(pe, "d", i)
                    for j in range(TB):
                        if j >= 2:
                            pe.wait_ge(sem("y_used"), i * TB + j - 1)
                        q = slice(j * P, (j + 1) * P)
                        for c in range(C):
                            t = mm3(pe, ps[:, 2 + j % 2, :], xT_hi[:, c, q], xT_lo[:, c, q], d_w_hi[:, c, :], d_w_lo[:, c, :],
                                    c == 0, c == C - 1)
                        t.then_inc(sem("y_ps"), 1)
                    pe.wait_ge(sem("y_used"), TB * (i + 1))
                end_stage(pe, 3)
            if stages > 4:
                def e_qk_tensor(turn, d):
                    u = d % 2
                    pe.wait_ge(sem(f"e_qkw_in{u}"), 16 * (turn + d // 2 + 1))
                    w = [e_qkw[:, u, q, :] for q in range(2)]
                    for c in range(C):
                        t = mm3(pe, ps[:, 2, :], w[0][:, c * P:(c + 1) * P], w[1][:, c * P:(c + 1) * P], xT_hi[:, c, :], xT_lo[:, c, :],
                                c == 0, c == C - 1)
                    t.then_inc(sem("qk_ps"), 1)
                    t = mm3(pe, ps[:, 3, :], w[0][:, 4 * P:5 * P], w[1][:, 4 * P:5 * P], e_kT_hi[:, :], e_kT_lo[:, :], True, True)
                    t.then_inc(sem("qk_ps"), 1)

                def e_scores_tensor(h, a, u, first=False):
                    r = slice(a * E_R, (a + 1) * E_R)
                    for t_ in range(TB):
                        if t_ >= 2 or not first:
                            pe.wait_ge(sem("exp"), h * TB + t_ - 1)
                        q = slice(t_ * P, (t_ + 1) * P)
                        mm3(pe, ps[:, t_ % 2, :], e_qk_hi[r, u, 0, q], e_qk_lo[r, u, 0, q], e_qk_hi[r, u, 1, :], e_qk_lo[r, u, 1, :], True, True)\
                            .then_inc(sem("scores_ps"), 1)

                def e_out_tensor(turn, hh):
                    pe.wait_ge(sem("head_out"), turn * E_BODY + hh + 1)
                    u, a = hh // 2, hh % 2
                    if a == 0:
                        pe.wait_ge(sem(f"e_g_in{u}"), 16 * (turn + 1))
                    gw = [e_g[:, u, q, a * D:(a + 1) * D] for q in range(2)]
                    for j in range(TB):
                        q = slice(j * P, (j + 1) * P)
                        for l, r in ((e_cT_hi, 0), (e_cT_hi, 1), (e_cT_lo, 0)):
                            t = pe.matmul(ps[:, 4 + j, :], l[:, a, q], gw[r], start=False, stop=False, skip_group_check=True)
                    if a == 1:
                        t.then_inc(sem(f"e_g_used{u}"), 1)

                def e_head_tensor(turn, hh, tail):
                    h = turn * E_BODY + hh
                    more = not (tail and hh == E_BODY - 1)
                    if more:
                        if hh % 2 == 1:
                            pe.wait_ge(sem("qk"), turn * E_BODY + 2 * ((hh + 1) // 2 + 1))
                        e_scores_tensor(h + 1, (hh + 1) % 2, (hh + 1) // 2 % 2)
                    for c in range(TB):
                        if c >= 2:
                            pe.wait_ge(sem("pT"), h * TB + c - 1)
                        for t_ in range(TB):
                            if c == 0:
                                pe.wait_ge(sem("e_p"), h * TB + t_ + 1)
                            t = pe.transpose(ps[:, 2 + c % 2, t_ * P:(t_ + 1) * P], e_p[:, hh % 2, t_, c * P:(c + 1) * P], ident[:, :])
                        t.then_inc(sem("pT_ps"), 1)
                    if more:
                        pe.wait_ge(sem("exp"), (h + 2) * TB)
                    for c in range(TB):
                        pe.wait_ge(sem("pT"), h * TB + c + 1)
                        t = mm3(pe, ps[:, 1, :], e_kvr_hi[:, c, :], e_kvr_lo[:, c, :], e_pT_hi[:, c, :], e_pT_lo[:, c, :], c == 0, c == TB - 1)
                    t.then_inc(sem("head_ps"), 1)
                    if hh:
                        e_out_tensor(turn, hh - 1)
                    if hh == E_BODY - 1:
                        e_out_tensor(turn, hh)
                    if hh % 2 == 0 and not (tail and hh == E_BODY - 2):
                        e_qk_tensor(turn, hh // 2 + 1)
                    pe.wait_ge(sem("head_out"), h + 1)

                with pe.Fori(0, E_HEADS // 2) as i:
                    for u in range(2):
                        n = i * 2 + u
                        if u == 0:
                            pe.wait_ge(sem("e_blob_in"), 32 * (i + 1))
                        raw = e_blob[:, u, :]
                        kcq, wqr, wq, wkv, wo = (raw[:, a:b] for a, b in zip(E_CUTS, E_CUTS[1:]))
                        for c in range(3):
                            t = pe.matmul(ps[:, 0, 0:E_R], kcq[:, c * P:(c + 1) * P], wqr[:, c * E_R:(c + 1) * E_R], start=c == 0, stop=c == 2)
                        t.then_inc(sem("e_u_ps"), 1)
                        pe.wait_ge(sem("e_mg"), 2 * n + 1)
                        pe.matmul(ps[:, 2, :], wkv, wo, start=True, stop=True)
                        pe.wait_ge(sem("e_u"), n + 1)
                        for c in range(C):
                            t = pe.matmul(ps[:, 1, c * E_R:(c + 1) * E_R], wq[:, c * P:(c + 1) * P], e_u[:, u, :], start=True, stop=True)
                        t.then_inc(sem("e_mg_ps"), 1)
                    pe.wait_ge(sem("e_mg"), 4 * (i + 1) + 1)
                with pe.Fori(0, B) as i:
                    norm_tensor(pe, "e", i)
                    pe.wait_ge(sem("e_kvr"), i + 1)
                    for t_ in range(TB):
                        t = pe.transpose(ps[:, 2, t_ * P:(t_ + 1) * P], e_kvr[:, t_, :], ident[:, :])
                    t.then_inc(sem("e_kT_ps"), 1)
                    pe.wait_ge(sem("e_kT"), i + 1)
                    pe.wait_ge(sem("e_zero"), 1)
                    for j in range(TB):
                        pe.matmul(ps[:, 4 + j, :], e_zero[:, 0:P], e_zero[:, :], start=True, stop=False, skip_group_check=True)
                    e_qk_tensor(i * E_TURNS, 0)
                    pe.wait_ge(sem("qk"), i * E_HEADS + 2)
                    e_scores_tensor(i * E_HEADS, 0, 0, True)
                    plain(pe)
                    with pe.Fori(0, E_TURNS - 1) as g:
                        for hh in range(E_BODY):
                            e_head_tensor(i * E_TURNS + g, hh, False)
                    for hh in range(E_BODY):
                        e_head_tensor((i + 1) * E_TURNS - 1, hh, True)
                    for j in range(TB):
                        t = pe.matmul(ps[:, 4 + j, :], e_zero[:, 0:P], e_zero[:, :], start=False, stop=True, skip_group_check=True)
                    t.then_inc(sem("e_y_ps"), 1)
                    pe.wait_ge(sem("e_y_used"), TB * (i + 1))
                end_stage(pe, 4)
            if stages > 5:
                pe.wait_ge(sem("weights"), READY["f"])
                for c in range(C):
                    t = pe.matmul(ps[:, 2, 0:F_N], ones[:, :], f_q[:, c, :], start=c == 0, stop=c == C - 1)
                t.then_inc(sem("f_const_ps"), 1)
                with pe.Fori(0, B) as i:
                    norm_tensor(pe, "f", i)
                    for j in range(TB):
                        if j >= 2:
                            pe.wait_ge(sem("f_a"), i * TB + j - 1)
                        q = slice(j * P, (j + 1) * P)
                        for c in range(C):
                            t = mm3(pe, ps[:, 2 + j % 2, 0:F_N], xT_hi[:, c, q], xT_lo[:, c, q], f_w_hi[:, c, :], f_w_lo[:, c, :], c == 0, c == C - 1)
                        t.then_inc(sem("f_a_ps"), 1)
                    pe.wait_ge(sem("f_m"), TB * (i + 1))
                    for j in range(TB):
                        t = pe.transpose(ps[0:F_K, 4, j * P:(j + 1) * P], f_m[:, j, :], ident[:, :])
                    t.then_inc(sem("f_mT_ps"), 1)
                    pe.wait_ge(sem("f_mT"), i + 1)
                    for j in range(TB):
                        if j >= 2:
                            pe.wait_ge(sem("y_used"), 1 * TILES + i * TB + j - 1)
                        q = slice(j * P, (j + 1) * P)
                        mm3(pe, ps[:, 6 + j % 2, :], f_mT_hi[:, q], f_mT_lo[:, q], f_d_hi[:, :], f_d_lo[:, :], True, True).then_inc(sem("y_ps"), 1)
                    pe.wait_ge(sem("y_used"), 1 * TILES + TB * (i + 1))
                end_stage(pe, 5)
            if stages > 6:
                pe.wait_ge(sem("weights"), READY["g"])

                def g_scores_tensor(h, hh):
                    r = slice(hh * G_HD, (hh + 1) * G_HD)
                    for t_ in range(TB):
                        pe.wait_ge(sem("exp"), h * TB + t_ - TB + 1)
                        q, w = slice(t_ * P, (t_ + 1) * P), (t_ + 1) * P
                        mm3(pe, ps[:, t_, 0:w], g_qk_hi[r, 0, q], g_qk_lo[r, 0, q], g_qk_hi[r, 1, 0:w], g_qk_lo[r, 1, 0:w], True, False)
                        pe.matmul(ps[:, t_, q], g_ident_r[:, :], g_mask_r[:, :], start=False, stop=True).then_inc(sem("scores_ps"), 1)

                def g_v_tensor(n, g):
                    for t_ in range(TB):
                        q, col = slice(t_ * P, (t_ + 1) * P), bass.ds(g * P + D, P)
                        t = mm3(pe, ps[:, 6, q], g_ctx_hi[:, q], g_ctx_lo[:, q], g_wkv_hi[:, col], g_wkv_lo[:, col], True, True)
                    t.then_inc(sem("g_v_ps"), 1)

                def g_heads_tensor(n, g, tail):
                    for hh in range(4):
                        h = G_HEADS_BEFORE + n * 4 + hh
                        pe.wait_ge(sem("g_diag"), TB * (h + 1 - G_HEADS_BEFORE))
                        for c in range(TB):
                            if hh == 0 and c == 2:
                                pe.wait_ge(sem("g_v"), n + 1)
                            if c == 3:
                                pe.wait_ge(sem("pT"), h * TB + 1)
                            for t_ in range(c, TB):
                                t = pe.matmul(ps[:, 4 + c % 3, t_ * P:(t_ + 1) * P], g_p[:, t_, c * P:(c + 1) * P], g_diag[:, t_, :], start=True, stop=True)
                            t.then_inc(sem("pT_ps"), 1)
                        if hh < 3 or not tail:
                            if hh == 3:
                                pe.wait_ge(sem("qk"), G_HEADS_BEFORE + 2 * (n + 2))
                            g_scores_tensor(h + 1, (hh + 1) % 4)
                        pe.wait_ge(sem("pT"), TB * (h + 1))
                        pe.wait_ge(sem("head_out"), h)
                        if hh == 3 and not tail:
                            g_v_tensor(n + 1, g + 1)
                        for c in range(TB):
                            t = mm3(pe, ps[:, 7, c * P:], g_v_hi[:, c, :], g_v_lo[:, c, :], g_pT_hi[:, c, c * P:], g_pT_lo[:, c, c * P:], c == 0, c == TB - 1)
                        t.then_inc(sem("head_ps"), 1)

                with pe.Fori(0, B) as i:
                    norm_tensor(pe, "g", i)
                    pe.wait_ge(sem("g_ctx_used"), i + 2)
                    for m_ in range(C):
                        q = slice(m_ * P, (m_ + 1) * P)
                        if m_ >= 2:
                            pe.wait_ge(sem("g_q"), i * C + m_ - 1)
                        for c in range(C):
                            t = mm3(pe, ps[:, 2 + m_ % 2, :], g_wq_hi[:, c, q], g_wq_lo[:, c, q], xT_hi[:, c, :], xT_lo[:, c, :], c == 0, c == C - 1)
                        t.then_inc(sem("g_q_ps"), 1)
                        if m_ >= 2:
                            pe.wait_ge(sem("g_k"), i * C + m_ - 1)
                        mm3(pe, ps[:, 4 + m_ % 2, :], g_wkv_hi[:, q], g_wkv_lo[:, q], g_ctx_hi[:, :], g_ctx_lo[:, :], True, True).then_inc(sem("g_k_ps"), 1)
                    g_v_tensor(i * C, 0)
                    pe.wait_ge(sem("g_k"), C * (i + 1))
                    pe.wait_ge(sem("g_q"), C * (i + 1))
                    pe.wait_ge(sem("qk"), G_HEADS_BEFORE + 2 * (i * C + 1))
                    g_scores_tensor(G_HEADS_BEFORE + i * C * 4, 0)
                    plain(pe)
                    with pe.Fori(0, C - 1) as g:
                        g_heads_tensor(i * C + g, g, False)
                    g_heads_tensor(i * C + C - 1, C - 1, True)
                    pe.wait_ge(sem("head_out"), G_HEADS_BEFORE + (i + 1) * C * 4)
                    for j in range(TB):
                        if j >= 2:
                            pe.wait_ge(sem("y_used"), 2 * TILES + i * TB + j - 1)
                        q = slice(j * P, (j + 1) * P)
                        for c in range(C):
                            t = mm3(pe, ps[:, 2 + j % 2, :], xT_hi[:, c, q], xT_lo[:, c, q], g_wo_hi[:, c, :], g_wo_lo[:, c, :], c == 0, c == C - 1)
                        t.then_inc(sem("y_ps"), 1)
                    pe.wait_ge(sem("y_used"), 2 * TILES + TB * (i + 1))
                end_stage(pe, 6)
            if stages > 7:
                pe.wait_ge(sem("weights"), READY["h"])
                pe.wait_ge(sem("h_zero"), 1)

                def h_gate_up(n, u):
                    pe.wait_ge(sem("h_gu_used"), n + 3)
                    pe.wait_ge(sem("h_h"), n + 1)
                    for w in range(2):
                        for c in range(C):
                            q = slice(w * D + c * P, w * D + (c + 1) * P)
                            t = mm3(pe, ps[:, 2 * w + u, :], h_w_hi[:, u, q], h_w_lo[:, u, q], xT_hi[:, c, :], xT_lo[:, c, :], c == 0, c == C - 1)
                    t.then_inc(sem("h_gu_ps"), 1)

                def h_down(n, u):
                    pe.wait_ge(sem("h_d_used"), n + 3)
                    pe.wait_ge(sem("h_h_lo"), n + 1)
                    for j in range(TB):
                        q = slice(j * P, (j + 1) * P)
                        for a, b in ((h_h_hi, h_w_hi), (h_h_hi, h_w_lo), (h_h_lo, h_w_hi)):
                            t = pe.matmul(ps[:, 4 + j, :], a[:, u, q], b[:, u, 2 * D:], start=False, stop=False, skip_group_check=True)
                    t.then_inc(sem("h_down"), 1)

                with pe.Fori(0, B) as i:
                    norm_tensor(pe, "h", i)
                    for j in range(TB):
                        q = slice(j * P, (j + 1) * P)
                        for c in range(C):
                            t = mm3(pe, ps[:, 0, 2 * j:2 * j + 2], xT_hi[:, c, q], xT_lo[:, c, q], h_gw_hi[:, c, :], h_gw_lo[:, c, :], c == 0, c == C - 1)
                    t.then_inc(sem("h_l_ps"), 1)
                    pe.wait_ge(sem("h_logit"), i + 1)
                    for j in range(TB):
                        pe.matmul(ps[:, 4 + j, :], h_zero[:, 0:P], h_zero[:, :], start=True, stop=False, skip_group_check=True)
                    pe.wait_ge(sem("h_diag"), i + 1)
                    for e in range(2):
                        t = pe.matmul(ps[:, 2 + e, :], ones[:, :], h_diag[:, e, :], start=True, stop=True)
                    t.then_inc(sem("h_gain_ps"), 1)
                    pe.wait_ge(sem("h_gain"), i + 1)
                    first = i * 2 * HC
                    h_gate_up(first, 0)
                    plain(pe)
                    with pe.Fori(0, HC - 1) as f:
                        n = first + 2 * f
                        h_gate_up(n + 1, 1)
                        h_down(n, 0)
                        h_gate_up(n + 2, 0)
                        h_down(n + 1, 1)
                    last = first + 2 * HC - 2
                    h_gate_up(last + 1, 1)
                    h_down(last, 0)
                    h_down(last + 1, 1)
                    for j in range(TB):
                        t = pe.matmul(ps[:, 4 + j, :], h_zero[:, 0:P], h_zero[:, :], start=False, stop=True, skip_group_check=True)
                    t.then_inc(sem("h_y_ps"), 1)
                    pe.wait_ge(sem("h_y_used"), TB * (i + 1))
                end_stage(pe, 7)


NEG = -1.0e30
HI_BEFORE = {"a": 0, "c": 2, "d": 4, "f": 5, "g": 7, "h": 12}
READY = {stage: n + 1 for n, stage in enumerate("abcdfgh")}
E_HEADS, E_R, E_CQ = 16, 64, 384
E_CUTS = np.cumsum([0, E_CQ, 3 * E_R, D, DC, D]).tolist()
E_RAW = E_CUTS[-1]
E_QKW = C * P + P
E_BODY = 4
QK_AHEAD = 3
E_TURNS = E_HEADS // E_BODY
F_N, F_K = 136, 72
G_HD = 32
G_HEADS_BEFORE = B * E_HEADS
G_SCALE = float(1.0 / np.sqrt(np.float32(32)))
H_BLOB = 3 * D
SYN_K = max(1, int(HID * (1.0 - 0.9)))
ROUNDS = 26
SEARCH_STEPS = 6
SIM_K = max(1, int(S * 0.3))
SIM1_SCALE = 1.0 / (math.sqrt(32.0) * 4)


def layout(v):
    f = np.ascontiguousarray

    def cut(a):
        return f(a.reshape(a.shape[0] // P, P, a.shape[1]).transpose(1, 0, 2))

    ctx2 = v["ctx_512"].reshape(B * S, DC)
    return {
        "x": cut(v["x"].reshape(B * S, D)),
        "g_xattn": f(v["g_xattn"]), "g_ffn": f(v["g_ffn"]),
        "ctxT": f(ctx2.T),
        "l0_wkT": f(v["L0_xattn_W_k"].T), "l0_bk": f(v["L0_xattn_b_k"].reshape(DC, 1)),
        "l0_gamma": f(v["L0_xattn_ln_gamma"]), "l0_beta": f(v["L0_xattn_ln_beta"]),
        "wsynT": cut(v["L0_ffn_W_syn"].T).reshape(P, -1), "woutT": cut(v["L0_ffn_W_out"].T).reshape(P, -1),
        "b_syn": f(v["L0_ffn_b_syn"]), "b_out": f(v["L0_ffn_b_out"]),
        "ffn_gamma": f(v["L0_ffn_gamma"]), "ffn_beta": f(v["L0_ffn_beta"]),
        "l1_wqkT": f(np.stack([v["L1_xattn_Wq"].T, v["L1_xattn_Wk"].T], 1)),
        "l1_gamma_raw": f(v["L1_xattn_gamma_raw"].reshape(1)),
        **rope(),
        "ctx": f(ctx2.reshape(B, TB, P, DC).transpose(0, 2, 1, 3)),
        "l2_heads": heads(v), "l2_wkr": f(v["L2_xattn_W_kr"].reshape(8, 2, DC, E_R).transpose(0, 2, 1, 3).reshape(8, DC, P)),
        **select_ffn(v, cut),
        "l3_wqT": cut(v["L3_xattn_Wq"].T), "l3_woT": cut(v["L3_xattn_Wout"].T), "l3_wkvT": f(v["L3_xattn_Wkv_expand"].T),
        "l3_gateT": cut(v["L3_ffn_gate_w"].T), "l3_blob": experts(v),
        "l1_wT": cut(v["L1_ffn_weight"].T), "l1_scale": f(v["L1_ffn_scale_weight"]), "l1_bias": f(v["L1_ffn_bias"]),
    }


def rope():
    inv = (1.0 / np.float32(10000.0) ** (np.arange(0, DC, 2, dtype=np.float32) / np.float32(DC))).astype(np.float32)
    freqs = np.arange(S, dtype=np.float32)[:, None] * inv[None, :]
    sin, cos = (np.repeat(t(freqs).astype(np.float32), 2, axis=-1) for t in (np.sin, np.cos))
    sin = np.concatenate([-sin[:, :DC // 2], sin[:, DC // 2:]], 1)
    return {n: np.ascontiguousarray(t.reshape(TB, P, DC).transpose(1, 0, 2)) for n, t in (("cos", cos), ("sin", sin))}


def heads(v):
    h = E_HEADS
    kcq = v["L2_xattn_w_kc_q"].transpose(0, 2, 1).reshape(h, 3, P, P).transpose(0, 2, 1, 3).reshape(h, P, -1)
    wqr = v["L2_xattn_W_qr"].reshape(h, 3, P, E_R).transpose(0, 2, 1, 3).reshape(h, P, -1)
    wq = v["L2_xattn_Wq"].reshape(h, P, D)
    wkv = v["L2_xattn_w_kc_kv"]
    wo = v["L2_xattn_Wo"].T.reshape(h, P, D)
    a = np.concatenate([kcq, wqr, wq, wkv, wo], 2)
    return np.ascontiguousarray(a.reshape(h // 2, 2, P, -1).transpose(0, 2, 1, 3))


def select_ffn(v, cut):
    sw, up = (v[n].transpose(1, 0, 2) for n in ("L2_ffn_select_weight", "L2_ffn_lora_update"))
    mean, deb = v["L2_ffn_select_mean_diff"].T, v["L2_ffn_debias_w"].T
    w = np.concatenate([sw.reshape(D, 64), up.reshape(D, 64), mean], 1)
    q = np.concatenate([np.repeat(mean, 8, 1), np.repeat(deb, 8, 1), mean], 1)
    d = np.concatenate([v["L2_ffn_lora_degen"].transpose(0, 2, 1).reshape(64, D), v["L2_ffn_bias_w"]], 0)
    return {"l2_fw": cut(w), "l2_fq": cut(q), "l2_fd": np.ascontiguousarray(d),
            "l2_center": v["L2_ffn_imp_center"], "l2_slope": v["L2_ffn_imp_slope"],
            "order": np.arange(8, 0, -1).astype(np.float32)}


def experts(v):
    g, u = (v[n].reshape(2, HC, P, C, P).transpose(0, 1, 4, 3, 2).reshape(2, HC, P, D) for n in ("L3_ffn_w_gate", "L3_ffn_w_up"))
    d = v["L3_ffn_w_down"].transpose(0, 2, 1).reshape(2, HC, P, D)
    return np.ascontiguousarray(np.concatenate([g, u, d], 3)).reshape(2 * HC, P, H_BLOB)


def kernel(**inputs):
    import concourse.bacc as _bacc
    from concourse.bass_utils import run_bass_kernel_spmd as _run

    nc = _bacc.Bacc("TRN2", target_bir_lowering=False, num_devices=1)
    arrays = {f"in_{name}": a for name, a in layout({k: np.asarray(a) for k, a in inputs.items()}).items()}
    args = {name[3:]: nc.dram_tensor(name, a.shape, mybir.dt.from_np(a.dtype), kind="ExternalInput").ap()
            for name, a in arrays.items()}
    out = nc.dram_tensor("out_0", (P, TILES, D), F32, kind="ExternalOutput").ap()
    program(nc, args, out)
    r = _run(nc, [arrays], core_ids=[0])
    return np.ascontiguousarray(r.results[0]["out_0"].transpose(1, 0, 2)).reshape(B, S, D)
```

```python
import math
from contextlib import ExitStack

import numpy as np

import concourse.bass as bass
from concourse import mybir

F32 = mybir.dt.float32
F32R = mybir.dt.float32r
ALU = mybir.AluOpType
ACT = mybir.ActivationFunctionType
AX = mybir.AxisListType

P = 128
B, S, D, DC = 4, 512, 512, 128
TILES = B * S // P
TB = S // P
C = D // P
HID = 2048
HC = HID // P
A_WORDS = 3 * B * S + 3 * DC + 1 + 11 * S + 32
BANK = 512
LN_EPS = 1e-5


class InOrder:

    def __init__(self, eng, sem):
        self.eng, self.sem, self.base, self.n = eng, sem, 0, 0

    def __call__(self, instruction):
        self.n += 1
        instruction.then_inc(self.sem, 1)
        self.eng.wait_ge(self.sem, self.base + self.n)

    def later(self, instruction):
        self.n += 1
        instruction.then_inc(self.sem, 1)

    def enter(self, i, per):
        outer = (self.base, self.n)
        self.base, self.n = self.base + self.n + i * per, 0
        return outer

    def leave(self, outer, turns, per):
        assert self.n == per, f"{self.sem}: {self.n} steps a turn, not {per}"
        self.base, self.n = outer[0], outer[1] + turns * per


def program(nc, inp, out, stages=8):
    ctx = ExitStack()
    with ctx:
        sems = {}

        def sem(name):
            if name not in sems:
                sems[name] = ctx.enter_context(nc.semaphore(name))
            return sems[name]

        def sb(name, shape, dt=F32, where=ctx):
            return where.enter_context(nc.sbuf_tensor(name, shape, dt))

        ps = ctx.enter_context(nc.psum_tensor("ps", [P, 8, BANK], F32))

        X = sb("X", [P, TILES, D])
        tg = sb("tg", [P, 8])
        ident = sb("ident", [P, P])
        ones = sb("ones", [P, P])
        minus_half = sb("minus_half", [P, TB])
        xn = sb("xn", [P, TB, D])
        xT_hi = sb("xT_hi", [P, C, S], F32R)
        xT_lo = sb("xT_lo", [P, C, S], F32R)
        ln_stats = sb("ln_stats", [P, TB, 6])
        ln_mv = sb("ln_mv", [P, TB, 2])
        ln_var = sb("ln_var", [P, TB])
        ln_rstd = sb("ln_rstd", [P, TB])

        def mm3(pe, o, l_hi, l_lo, r_hi, r_lo, start, stop):
            pe.matmul(o, l_hi, r_hi, start=start, stop=False)
            pe.matmul(o, l_hi, r_lo, start=False, stop=False)
            return pe.matmul(o, l_lo, r_hi, start=False, stop=stop)

        def plain(eng):
            eng.sem_inc(sem("plain"), 1)

        def end_stage(eng, n):
            eng.drain().then_inc(sem("stage_done"), 1)
            eng.wait_ge(sem("stage_done"), 4 * (n + 1))

        def ln_turn(s, i):
            return B * "abcdefgh".index(s) + i

        def norm_vector(dve, k, s, i):
            for j in range(TB):
                (k.later if j < TB - 1 else k)(dve.bn_stats(ln_stats[:, j, :], X[:, i * TB + j, :]))
            plain(dve)
            for j in range(TB):
                (k.later if j < TB - 1 else k)(dve.bn_aggr(ln_mv[:, j, :], ln_stats[:, j, :]))
            dve.tensor_scalar(ln_var[:, :], ln_mv[:, :, 1], LN_EPS, None, ALU.add).then_inc(sem("ln_var"), 1)
            dve.wait_ge(sem("ln_rstd"), ln_turn(s, i) + 1)
            for j in range(TB):
                dve.tensor_scalar(xn[:, j, :], X[:, i * TB + j, :], ln_mv[:, j, 0:1], ln_rstd[:, j:j + 1],
                                  ALU.subtract, ALU.mult).then_inc(sem("ln_xn"), 1)
            dve.wait_ge(sem("ln_xn"), TB * (ln_turn(s, i) + 1))
            for j in range(TB):
                dve.wait_ge(sem("ln_xT_hi"), TB * ln_turn(s, i) + j + 1)
                q = slice(j * P, (j + 1) * P)
                dve.tensor_tensor(xT_lo[:, :, q], ps[:, j, :].rearrange("p (c t) -> p c t", c=C),
                                  xT_hi[:, :, q].bitcast(F32), ALU.subtract).then_inc(sem("ln_xT"), 1)
            dve.wait_ge(sem("ln_xT"), TB * (ln_turn(s, i) + 1))

        def norm_pool(pool, s, i):
            pool.wait_ge(sem("ln_var"), ln_turn(s, i) + 1)
            pool.tensor_tensor(ln_rstd[:, :], ln_var[:, :], minus_half[:, :], ALU.pow).then_inc(sem("ln_rstd"), 1)

        def norm_tensor(pe, s, i):
            for j in range(TB):
                pe.wait_ge(sem("ln_xn"), TB * ln_turn(s, i) + j + 1)
                for c in range(C):
                    t = pe.transpose(ps[:, j, c * P:(c + 1) * P], xn[:, j, c * P:(c + 1) * P], ident[:, :])
                t.then_inc(sem("ln_xT_ps"), 1)
            pe.wait_ge(sem("ln_xT"), TB * (ln_turn(s, i) + 1))

        def norm_scalar(act, s, i):
            for j in range(TB):
                act.wait_ge(sem("ln_xT_ps"), TB * ln_turn(s, i) + j + 1)
                act.activation(xT_hi[:, :, j * P:(j + 1) * P], ps[:, j, :].rearrange("p (c t) -> p c t", c=C),
                               ACT.Copy).then_inc(sem("ln_xT_hi"), 1)

        def search_turn(s, i):
            return (B * "bc".index(s) + i) * (ROUNDS + 1)

        def search_round(s, i):
            return (B * "bc".index(s) + i) * ROUNDS

        def search_vector(dve, k, i, data, junk, low, step, other, cand, cnt, take, kth):
            mine, theirs = slice(0, 2), slice(2, 4)
            for v in (low, step, cand):
                k.later(dve.tensor_scalar(v[:, theirs], v[:, theirs], -1.0, None, ALU.mult))
            dve.wait_ge(k.sem, k.base + k.n)
            dve.sem_inc(sem("search_set"), 1)
            plain(dve)
            with dve.Fori(0, ROUNDS // 2) as r:
                outer = k.enter(r, 2 * SEARCH_STEPS)
                for now, then in ((step, other), (other, step)):
                    k.later(dve.tensor_scalar(then[:, mine], now[:, mine], 0.5, None, ALU.mult))
                    for j in (0, 1):
                        k(dve.tensor_scalar(junk, data[:, j, :], cand[:, j:j + 1], 0.0, ALU.is_ge, ALU.add, accum_out=cnt[:, j:j + 1]))
                    k(dve.scalar_tensor_tensor(take[:, mine], cnt[:, mine], float(kth), now[:, mine], ALU.is_ge, ALU.mult))
                    k(dve.tensor_tensor(low[:, mine], low[:, mine], take[:, mine], ALU.add))
                    k(dve.tensor_tensor(cand[:, mine], low[:, mine], then[:, mine], ALU.add))
                k.leave(outer, ROUNDS // 2, 2 * SEARCH_STEPS)

        def search_vector_end(dve, k, s, i, low):
            dve.wait_ge(sem("search_try"), search_turn(s, i + 1))
            k(dve.tensor_scalar(low[:, 2:4], low[:, 2:4], -1.0, None, ALU.mult))

        def search_pool(pool, k, s, i, low, step, half, cand, cnt, take, kth, n):
            low, step, half, cand, cnt, take = (v[:, 2:4] for v in (low, step, half, cand, cnt, take))
            pool.wait_ge(sem("search_set"), B * "bc".index(s) + i + 1)
            pool.sem_inc(sem("search_try"), 1)
            k(pool.tensor_scalar(half, step, 0.5, None, ALU.mult))
            plain(pool)
            with pool.Fori(0, ROUNDS) as r:
                outer = k.enter(r, SEARCH_POOL_STEPS)
                pool.wait_ge(sem("search_count"), 2 * (search_round(s, i) + r + 1))
                plain(pool)
                k(pool.tensor_scalar(take, cnt, float(2 * kth - n), None, ALU.is_ge))
                k(pool.tensor_tensor(take, take, step, ALU.mult))
                k(pool.tensor_tensor(low, low, take, ALU.add))
                pool.tensor_tensor(cand, low, half, ALU.add).then_inc(sem("search_try"), 1)
                k(pool.tensor_scalar(step, step, 0.5, None, ALU.mult))
                pool.wait_ge(sem("search_try"), search_turn(s, i) + r + 2)
                plain(pool)
                k(pool.tensor_scalar(half, step, 0.5, None, ALU.mult))
                k.leave(outer, ROUNDS, SEARCH_POOL_STEPS)

        def search_scalar(act, s, i, data, junk, cand, cnt):
            with act.Fori(0, ROUNDS) as r:
                act.wait_ge(sem("search_try"), search_turn(s, i) + r + 1)
                t = search_round(s, i) + r
                for j in (2, 3):
                    act.activation(junk, data[:, j, :], ACT.Sign, bias=cand[:, j:j + 1], accum_out=cnt[:, j:j + 1])\
                        .then_inc(sem("search_count"), 1)
                    act.wait_ge(sem("search_count"), 2 * t + j - 1)

        stack = {}

        def mem(stage):
            stack[stage] = ExitStack()
            return lambda name, shape, dt=F32: sb(name, shape, dt, stack[stage])

        m = mem("A")
        a_ctxT = m("a_ctxT", [P, B * S])
        a_ctx_hi, a_ctx_lo = m("a_ctx_hi", [P, B * S], F32R), m("a_ctx_lo", [P, B * S], F32R)
        a_wk = m("a_wk", [P, DC])
        a_wk_hi, a_wk_lo = m("a_wk_hi", [P, DC], F32R), m("a_wk_lo", [P, DC], F32R)
        a_bk = m("a_bk", [P, 1])
        a_gamma, a_beta = m("a_gamma", [P, S]), m("a_beta", [P, S])
        a_kvT = m("a_kvT", [P, S])
        a_kvT_hi, a_kvT_lo = m("a_kvT_hi", [P, S], F32R), m("a_kvT_lo", [P, S], F32R)
        a_kv_hi, a_kv_lo = m("a_kv_hi", [P, TB, DC], F32R), m("a_kv_lo", [P, TB, DC], F32R)
        a_oT_hi, a_oT_lo = m("a_oT_hi", [P, S], F32R), m("a_oT_lo", [P, S], F32R)
        a_sim = m("a_sim", [P, 2, S])
        a_st = m("a_st", [P, 2, 16])
        m("a_pad", [P, C * HID + 2 * HID - A_WORDS])
        b_raw_syn, b_raw_out = m("b_raw_syn", [P, C * HID]), m("b_raw_out", [P, C * HID])
        stack["A"].close()
        m = mem("B")
        b_tsyn = m("b_tsyn", [P, C, HID], F32R)
        b_junk = m("b_junk", [P, 2, HID], mybir.dt.bfloat16)
        b_bsyn = m("b_bsyn", [P, HID])
        b_tout = m("b_tout", [P, HC, D], F32R)
        b_z = m("b_z", [P, TB, HID])
        b_y = m("b_y", [P, D])
        b_hT_hi, b_hT_lo = m("b_hT_hi", [P, HC, P], F32R), m("b_hT_lo", [P, HC, P], F32R)
        b_rows = m("b_rows", [P, 3, D])
        b_st = m("b_st", [P, 16])
        b_tk = m("b_tk", [P, 8, TB])
        stack["B"].close()
        b_weights = [w[:, :, :].rearrange("p a n -> p (a n)") for w in (b_tsyn, b_tout)]
        b_raw = [w[:, :] for w in (b_raw_syn, b_raw_out)]
        b_hT = [(b_hT_hi, b_hT_lo), tuple(w[:, :, :].rearrange("p c (a t) -> p (c a) t", t=P) for w in (xT_hi, xT_lo))]
        b_tmp = b_junk[:, :, :].rearrange("p a n -> p (a n)")
        m = mem("C")
        c_ctxT = m("c_ctxT", [P, B * S])
        c_ctx_hi, c_ctx_lo = m("c_ctx_hi", [P, B * S], F32R), m("c_ctx_lo", [P, B * S], F32R)
        c_w = m("c_w", [P, 2, DC])
        c_w_hi, c_w_lo = m("c_w_hi", [P, 2, DC], F32R), m("c_w_lo", [P, 2, DC], F32R)
        c_qk_hi, c_qk_lo = m("c_qk_hi", [P, 2, S], F32R), m("c_qk_lo", [P, 2, S], F32R)
        c_sim = m("c_sim", [P, TB, S])
        c_a = m("c_a", [P, TB, S])
        c_tk = m("c_tk", [P, 8, TB])
        c_g = m("c_g", [P, 4])
        c_junk = m("c_junk", [P, 2, S])
        c_t = m("c_t", [P, S])
        stack["C"].close()
        m = mem("D")
        d_w = m("d_w", [P, C, D])
        d_w_hi, d_w_lo = m("d_w_hi", [P, C, D], F32R), m("d_w_lo", [P, C, D], F32R)
        d_rows = m("d_rows", [P, 2, D])
        stack["D"].close()

        m = mem("E")
        e_blob = m("e_blob", [P, 2, E_RAW])
        e_wkr = m("e_wkr", [P, 2, P])
        e_u = m("e_u", [P, 2, E_R])
        e_qkw = m("e_qkw", [P, 2, 2, E_QKW], F32R)
        e_g = m("e_g", [P, 2, 2, 2 * D], F32R)
        e_ctx = m("e_ctx", [P, TB, DC])
        e_cos, e_sin = m("e_cos", [P, TB, DC]), m("e_sin", [P, TB, DC])
        e_rot = m("e_rot", [P, TB, DC])
        e_kvr = m("e_kvr", [P, TB, DC])
        e_kvr_hi, e_kvr_lo = m("e_kvr_hi", [P, TB, DC], F32R), m("e_kvr_lo", [P, TB, DC], F32R)
        e_kT_hi, e_kT_lo = m("e_kT_hi", [P, S], F32R), m("e_kT_lo", [P, S], F32R)
        e_qk_hi, e_qk_lo = m("e_qk_hi", [P, 2, 2, S], F32R), m("e_qk_lo", [P, 2, 2, S], F32R)
        e_p = m("e_p", [P, 2, TB, S])
        e_pT_hi, e_pT_lo = m("e_pT_hi", [P, TB, S], F32R), m("e_pT_lo", [P, TB, S], F32R)
        e_cT_hi, e_cT_lo = m("e_cT_hi", [P, 2, S], F32R), m("e_cT_lo", [P, 2, S], F32R)
        e_st = m("e_st", [P, 2, 16])
        e_zero = m("e_zero", [P, S], F32R)
        stack["E"].close()
        e_blobs = [e_blob[:, :, :], e_p[:, :, :, :].rearrange("p a t s -> p (a t s)")[:, 0:2 * E_RAW].rearrange("p (u n) -> p u n", u=2)]
        e_qkw_kept = nc.dram_tensor("e_qkw_kept", (E_HEADS // 2, P, 2, E_QKW), F32, kind="Internal").ap()
        e_g_kept = nc.dram_tensor("e_g_kept", (E_HEADS // 2, P, 2, 2 * D), F32, kind="Internal").ap()
        m = mem("F")
        f_w, f_q = m("f_w", [P, C, F_N]), m("f_q", [P, C, F_N])
        f_w_hi, f_w_lo = m("f_w_hi", [P, C, F_N], F32R), m("f_w_lo", [P, C, F_N], F32R)
        f_d = m("f_d", [F_K, D])
        f_d_hi, f_d_lo = m("f_d_hi", [F_K, D], F32R), m("f_d_lo", [F_K, D], F32R)
        f_const = m("f_const", [P, F_N])
        f_rows = m("f_rows", [P, 3, 8])
        f_a = m("f_a", [P, TB, F_N])
        f_sq = m("f_sq", [P, TB, 64])
        f_xx = m("f_xx", [P, TB])
        f_g = m("f_g", [P, 6, TB, 8])
        f_s = m("f_s", [P, 4, TB])
        f_m = m("f_m", [P, TB, F_K])
        f_junk = m("f_junk", [P, D])
        f_mT_hi, f_mT_lo = m("f_mT_hi", [F_K, S], F32R), m("f_mT_lo", [F_K, S], F32R)
        stack["F"].close()
        m = mem("G")
        g_w = m("g_w", [P, C, D])
        g_wq_hi, g_wq_lo = m("g_wq_hi", [P, C, D], F32R), m("g_wq_lo", [P, C, D], F32R)
        g_wo_hi, g_wo_lo = m("g_wo_hi", [P, C, D], F32R), m("g_wo_lo", [P, C, D], F32R)
        g_wkv_hi, g_wkv_lo = m("g_wkv_hi", [P, 2 * D], F32R), m("g_wkv_lo", [P, 2 * D], F32R)
        g_ctxT = m("g_ctxT", [P, S])
        g_ctx_hi, g_ctx_lo = m("g_ctx_hi", [P, S], F32R), m("g_ctx_lo", [P, S], F32R)
        g_qT, g_kT = m("g_qT", [P, C, S]), m("g_kT", [P, C, S])
        g_v_hi, g_v_lo = m("g_v_hi", [P, TB, P], F32R), m("g_v_lo", [P, TB, P], F32R)
        g_qk_hi, g_qk_lo = m("g_qk_hi", [P, 2, S], F32R), m("g_qk_lo", [P, 2, S], F32R)
        g_mask = m("g_mask", [P, P])
        g_p = m("g_p", [P, TB, S])
        g_pT_hi, g_pT_lo = m("g_pT_hi", [P, TB, S], F32R), m("g_pT_lo", [P, TB, S], F32R)
        g_mask_r, g_ident_r = m("g_mask_r", [P, P], F32R), m("g_ident_r", [P, P], F32R)
        g_st = m("g_st", [P, 2, 8])
        g_diag = m("g_diag", [P, TB, P])
        stack["G"].close()
        m = mem("H")
        h_w = m("h_w", [P, 2, H_BLOB])
        h_w_hi, h_w_lo = m("h_w_hi", [P, 2, H_BLOB], F32R), m("h_w_lo", [P, 2, H_BLOB], F32R)
        h_diag, h_gain = m("h_diag", [P, 2, S]), m("h_gain", [P, 2, S])
        h_gw = m("h_gw", [P, C, 2])
        h_gw_hi, h_gw_lo = m("h_gw_hi", [P, C, 2], F32R), m("h_gw_lo", [P, C, 2], F32R)
        h_sg = m("h_sg", [P, 2, S])
        h_h = m("h_h", [P, 2, S])
        h_h_hi, h_h_lo = m("h_h_hi", [P, 2, S], F32R), m("h_h_lo", [P, 2, S], F32R)
        h_l = m("h_l", [P, 6, TB, 2])
        h_s = m("h_s", [P, 4, TB])
        h_zero = m("h_zero", [P, S], F32R)
        stack["H"].close()

        block = ctx.enter_context(nc.Block())

        @block.sync
        def _(sp):
            for name in ("e_blob_used", "e_blob_used", "e_ctx_used", "e_g_used0", "e_g_used1", "g_ctx_used", "h_gu_used", "h_gu_used", "h_d_used", "h_d_used",
                         "h_down", "h_down", "h_gu_ps", "h_gu_ps", "h_h", "h_h", "e_mg", "e_pair_kept0", "e_pair_kept1"):
                sp.sem_inc(sem(name), 1)
            sp.sem_inc(sem("qk_ps"), QK_AHEAD)
            sp.dma_start(X[:, 0:TB, :], inp["x"][:, 0:TB, :]).then_inc(sem("x_in"), 16)
            sp.dma_start(tg[:, 0:4], inp["g_xattn"].partition_broadcast(P)).then_inc(sem("tg_in"), 16)
            sp.dma_start(tg[:, 4:8], inp["g_ffn"].partition_broadcast(P)).then_inc(sem("tg_in"), 16)
            for dst, src in ((a_ctxT[:, :], inp["ctxT"]), (a_wk[:, :], inp["l0_wkT"]), (a_bk[:, :], inp["l0_bk"]),
                             (a_gamma[:, :], inp["l0_gamma"].partition_broadcast(P)),
                             (a_beta[:, :], inp["l0_beta"].partition_broadcast(P))):
                sp.dma_start(dst, src).then_inc(sem("a_in"), 16)
            for i in range(1, B):
                sp.wait_ge(sem("x_in"), 16 * i)
                sp.dma_start(X[:, i * TB:(i + 1) * TB, :], inp["x"][:, i * TB:(i + 1) * TB, :]).then_inc(sem("x_in"), 16)
            if stages > 1:
                for dst, src in zip(b_raw, (inp["wsynT"], inp["woutT"])):
                    sp.dma_start(dst, src).then_inc(sem("b_in"), 16)
            if stages > 1:
                sp.wait_ge(sem("stage_done"), 4)
                for dst, src in ((b_bsyn[:, :], inp["b_syn"]), (b_rows[:, 0, :], inp["b_out"]),
                                 (b_rows[:, 1, :], inp["ffn_gamma"]), (b_rows[:, 2, :], inp["ffn_beta"])):
                    sp.dma_start(dst, src.partition_broadcast(P)).then_inc(sem("b_rows_in"), 16)
            if stages > 2:
                sp.wait_ge(sem("stage_done"), 8)
                for dst, src in ((c_ctxT[:, :], inp["ctxT"]), (c_w[:, :, :], inp["l1_wqkT"]),
                                 (c_g[:, 0:1], inp["l1_gamma_raw"].partition_broadcast(P))):
                    sp.dma_start(dst, src).then_inc(sem("stage_in"), 16)
            if stages > 3:
                sp.wait_ge(sem("stage_done"), 12)
                for dst, src in ((d_w[:, :, :], inp["l1_wT"]), (d_rows[:, 0, :], inp["l1_scale"].partition_broadcast(P)),
                                 (d_rows[:, 1, :], inp["l1_bias"].partition_broadcast(P))):
                    sp.dma_start(dst, src).then_inc(sem("stage_in"), 16)
            if stages > 4:
                sp.wait_ge(sem("stage_done"), 16)
                sp.dma_start(e_cos[:, :, :], inp["cos"]).then_inc(sem("e_tables"), 16)
                sp.dma_start(e_sin[:, :, :], inp["sin"]).then_inc(sem("e_tables"), 16)

                def e_blob_load(n, v):
                    sp.wait_ge(sem("e_blob_used"), n + 1)
                    sp.dma_start(e_blobs[v], inp["l2_heads"][n]).then_inc(sem(f"e_blob_in{v}"), 16)
                    sp.dma_start(e_wkr[:, v, :], inp["l2_wkr"][n]).then_inc(sem(f"e_blob_in{v}"), 16)

                def e_pair_store(n, v):
                    sp.wait_ge(sem("e_pair_made"), n + 1)
                    sp.dma_start(e_qkw_kept[n], e_qkw[:, v, :, :].bitcast(F32)).then_inc(sem(f"e_pair_kept{v}"), 16)
                    sp.dma_start(e_g_kept[n], e_g[:, v, :, :].bitcast(F32)).then_inc(sem(f"e_pair_kept{v}"), 16)

                e_blob_load(0, 0)
                with sp.Fori(0, E_HEADS // 4 - 1) as i:
                    e_blob_load(2 * i + 1, 1)
                    e_pair_store(2 * i, 0)
                    e_blob_load(2 * i + 2, 0)
                    e_pair_store(2 * i + 1, 1)
                e_blob_load(E_HEADS // 2 - 1, 1)
                e_pair_store(E_HEADS // 2 - 2, 0)
                e_pair_store(E_HEADS // 2 - 1, 1)
                for v in range(2):
                    sp.wait_ge(sem(f"e_pair_kept{v}"), 32 * (E_HEADS // 4) + 1)
                with sp.Fori(0, B) as i:
                    sp.wait_ge(sem("e_ctx_used"), i + 1)
                    sp.dma_start(e_ctx[:, :, :], inp["ctx"][i]).then_inc(sem("e_ctx_in"), 16)
                    with sp.Fori(0, E_HEADS // 4) as g:
                        for u in range(2):
                            n = (i * (E_HEADS // 4) + g)
                            sp.wait_ge(sem("qk_ps"), n * E_BODY + 2 * u - 2 + QK_AHEAD)
                            sp.dma_start(e_qkw[:, u, :, :].bitcast(F32), e_qkw_kept[g * 2 + u]).then_inc(sem(f"e_qkw_in{u}"), 16)
                            sp.wait_ge(sem(f"e_g_used{u}"), n + 1)
                            sp.dma_start(e_g[:, u, :, :].bitcast(F32), e_g_kept[g * 2 + u]).then_inc(sem(f"e_g_in{u}"), 16)
            if stages > 5:
                sp.wait_ge(sem("stage_done"), 20)
                for dst, src in ((f_w[:, :, :], inp["l2_fw"]), (f_q[:, :, :], inp["l2_fq"]), (f_d[:, :], inp["l2_fd"]),
                                 (f_rows[:, 0, :], inp["l2_center"].partition_broadcast(P)),
                                 (f_rows[:, 1, :], inp["l2_slope"].partition_broadcast(P)),
                                 (f_rows[:, 2, :], inp["order"].partition_broadcast(P))):
                    sp.dma_start(dst, src).then_inc(sem("stage_in"), 16)
            if stages > 6:
                sp.wait_ge(sem("stage_done"), 24)
                for n, src in enumerate(("l3_wqT", "l3_woT", "l3_wkvT")):
                    sp.wait_ge(sem("g_raw_used"), n)
                    dst = g_w[:, :, :] if n < 2 else g_w[:, 0:2, :].rearrange("p a n -> p (a n)")
                    sp.dma_start(dst, inp[src]).then_inc(sem("g_in"), 16)
                with sp.Fori(0, B) as i:
                    sp.wait_ge(sem("g_ctx_used"), i + 1)
                    sp.dma_start(g_ctxT[:, :], inp["ctxT"][:, bass.ts(i, S)]).then_inc(sem("g_ctx_in"), 16)
            if stages > 7:
                sp.wait_ge(sem("stage_done"), 28)
                sp.dma_start(h_gw[:, :, :], inp["l3_gateT"]).then_inc(sem("h_gw_in"), 16)
                with sp.Fori(0, B) as i:
                    with sp.Fori(0, HC) as f:
                        for u in range(2):
                            n = i * (2 * HC) + f * 2 + u
                            sp.wait_ge(sem("h_gu_used"), n + 1)
                            sp.dma_start(h_w[:, u, 0:2 * D], inp["l3_blob"][f * 2 + u, :, 0:2 * D]).then_inc(sem(f"h_gu_in{u}"), 16)
                            sp.wait_ge(sem("h_d_used"), n + 1)
                            sp.dma_start(h_w[:, u, 2 * D:], inp["l3_blob"][f * 2 + u, :, 2 * D:]).then_inc(sem(f"h_d_in{u}"), 16)
            sp.wait_ge(sem("x_out"), 16 * B)

        @block.gpsimd
        def _(pool):
            k = InOrder(pool, sem("pool_steps"))
            k(pool.memset(ident[:, :], 0.0))
            k(pool.memset(ones[:, :], 1.0))
            k(pool.memset(minus_half[:, :], -0.5))
            pool.affine_select(out=ident[:, :], in_=ident[:, :], compare_op=ALU.not_equal, fill=1.0, base=0,
                               pattern=[[-1, P]], channel_multiplier=1).then_inc(sem("consts"), 1)
            with pool.Fori(0, B) as i:
                norm_pool(pool, "a", i)
                for j in range(TB):
                    pool.wait_ge(sem("a_sim_var"), i * TB + j + 1)
                    pool.tensor_tensor(a_st[:, j % 2, 8:9], a_st[:, j % 2, 7:8], minus_half[:, 0:1], ALU.pow).then_inc(sem("a_sim_rstd"), 1)
            end_stage(pool, 0)
            if stages > 1:
                with pool.Fori(0, B) as i:
                    o = k.enter(i, 1 + SEARCH_POOL_STEPS * ROUNDS)
                    norm_pool(pool, "b", i)
                    search_pool(pool, k, "b", i, *(b_tk[:, r, :] for r in range(6)), SYN_K, HID)
                    k.leave(o, B, 1 + SEARCH_POOL_STEPS * ROUNDS)
                    for j in range(TB):
                        pool.wait_ge(sem("b_y_var"), i * TB + j + 1)
                        pool.tensor_tensor(b_st[:, 8:9], b_st[:, 7:8], minus_half[:, 0:1], ALU.pow).then_inc(sem("b_y_rstd"), 1)
                end_stage(pool, 1)
            for n, name in enumerate("cdefgh", 2):
                if stages > n:
                    if name == "g":
                        k(pool.memset(g_mask[:, :], 0.0))
                        pool.affine_select(out=g_mask[:, :], in_=g_mask[:, :], compare_op=ALU.is_ge, fill=NEG, base=0,
                                           pattern=[[-1, P]], channel_multiplier=1).then_inc(sem("g_mask"), 1)
                    with pool.Fori(0, B) as i:
                        norm_pool(pool, name, i)
                        if name == "h":
                            pool.wait_ge(sem("h_y_used"), TB * (i + 1))
                            pool.dma_start(out[:, bass.ts(i, TB), :], X[:, bass.ts(i, TB), :]).then_inc(sem("x_out"), 16)
                        if name == "c":
                            o = k.enter(i, 1 + SEARCH_POOL_STEPS * ROUNDS)
                            search_pool(pool, k, "c", i, *(c_tk[:, r, :] for r in range(6)), SIM_K, S)
                            k.leave(o, B, 1 + SEARCH_POOL_STEPS * ROUNDS)
                    end_stage(pool, n)

        @block.scalar
        def _(act):
            act.wait_ge(sem("tg_in"), 32)
            act.activation(tg[:, :], tg[:, :], ACT.Tanh).then_inc(sem("tg"), 1)
            act.wait_ge(sem("a_in"), 80)
            act.activation(a_ctx_hi[:, :], a_ctxT[:, :], ACT.Copy).then_inc(sem("weights_hi"), 1)
            act.activation(a_wk_hi[:, :], a_wk[:, :], ACT.Copy).then_inc(sem("weights_hi"), 1)
            with act.Fori(0, B) as i:
                norm_scalar(act, "a", i)
                act.wait_ge(sem("a_kvT_ps"), i + 1)
                act.activation(a_kvT[:, :], ps[:, 2, :], ACT.Identity, bias=a_bk[:, 0:1]).then_inc(sem("a_kvT_f"), 1)
                act.wait_ge(sem("a_kvT_f"), i + 1)
                act.activation(a_kvT_hi[:, :], a_kvT[:, :], ACT.Copy).then_inc(sem("a_kvT_hi"), 1)
                act.wait_ge(sem("a_kv_ps"), i + 1)
                act.activation(a_kv_hi[:, :, :], ps[:, 3, :].rearrange("p (t d) -> p t d", t=TB), ACT.Copy)\
                    .then_inc(sem("a_kv_hi"), 1)
                act.wait_ge(sem("a_oT_ps"), i + 1)
                act.activation(a_oT_hi[:, :], ps[:, 4, :], ACT.Copy).then_inc(sem("a_oT_hi"), 1)
                for j in range(TB):
                    act.wait_ge(sem("a_max"), i * TB + j + 1)
                    act.activation(a_sim[:, j % 2, :], a_sim[:, j % 2, :], ACT.Exp, bias=a_st[:, j % 2, 9:10],
                                   accum_out=a_st[:, j % 2, 10:11]).then_inc(sem("a_exp"), 1)
            end_stage(act, 0)
            if stages > 1:
                with act.Fori(0, B) as i:
                    norm_scalar(act, "b", i)
                    search_scalar(act, "b", i, b_z, b_junk[:, 1, :], b_tk[:, 3, :], b_tk[:, 4, :])
                    for j in range(TB):
                        n = i * TB + j
                        if j >= 2:
                            act.wait_ge(sem("b_y_ps"), n - 1)
                        for q in range(4):
                            act.wait_ge(sem("b_hT_ps"), n * 4 + q + 1)
                            act.activation(b_hT[j % 2][0][:, 4 * q:4 * q + 4, :], ps[:, q, :].rearrange("p (c t) -> p c t", c=4),
                                           ACT.Copy).then_inc(sem("b_hT_hi"), 1)
                end_stage(act, 1)
            if stages > 2:
                act.wait_ge(sem("stage_in"), 48)
                act.activation(c_ctx_hi[:, :], c_ctxT[:, :], ACT.Copy).then_inc(sem("weights_hi"), 1)
                act.activation(c_w_hi[:, :, :], c_w[:, :, :], ACT.Copy).then_inc(sem("weights_hi"), 1)
                act.activation(c_g[:, 1:2], c_g[:, 0:1], ACT.Exp, scale=-1.0).then_inc(sem("c_g"), 1)
                with act.Fori(0, B) as i:
                    norm_scalar(act, "c", i)
                    for w in range(2):
                        act.wait_ge(sem("c_qk_ps"), i * 2 + w + 1)
                        act.activation(c_qk_hi[:, w, :], ps[:, 2 + w, :], ACT.Copy).then_inc(sem("c_qk_hi"), 1)
                    for j in range(TB):
                        act.wait_ge(sem("c_sim_ps"), i * TB + j + 1)
                        act.activation(c_sim[:, j, :], ps[:, 4 + j % 2, :], ACT.Copy, scale=SIM1_SCALE).then_inc(sem("c_sim"), 1)
                    for j in range(TB):
                        act.wait_ge(sem("c_sim"), i * TB + j + 1)
                        act.activation(c_a[:, j, :], c_sim[:, j, :], ACT.Sigmoid).then_inc(sem("c_e"), 1)
                    search_scalar(act, "c", i, c_sim, c_junk[:, 1, :], c_tk[:, 3, :], c_tk[:, 4, :])
                end_stage(act, 2)
            if stages > 3:
                act.wait_ge(sem("d_ws"), 4)
                act.activation(d_w_hi[:, :, :], d_w[:, :, :], ACT.Copy).then_inc(sem("weights_hi"), 1)
                with act.Fori(0, B) as i:
                    norm_scalar(act, "d", i)
                end_stage(act, 3)

            if stages > 4:
                def e_qk_scalar(turn, d):
                    u = d % 2
                    for w in range(2):
                        act.wait_ge(sem("qk_ps"), QK_AHEAD + turn * E_BODY + d * 2 + w + 1)
                        act.activation(e_qk_hi[:, u, w, :], ps[:, 2 + w, :], ACT.Copy).then_inc(sem("qk_hi"), 1)

                def e_exp_scalar(h, a, t):
                    act.wait_ge(sem("score_max"), h * TB + t + 1)
                    act.activation(e_p[:, a, t, :], ps[:, t % 2, :], ACT.Exp, bias=e_st[:, a, t:t + 1],
                                   accum_out=e_st[:, a, 4 + t:5 + t]).then_inc(sem("exp"), 1)

                def e_head_scalar(turn, hh, tail=False):
                    h = turn * E_BODY + hh
                    for what, t in E_STEPS:
                        if what == "scores" and not (tail and hh == E_BODY - 1):
                            e_exp_scalar(h + 1, (hh + 1) % 2, t)
                        if what == "turned":
                            act.wait_ge(sem("pT_ps"), h * TB + t + 1)
                            act.activation(e_pT_hi[:, t, :], ps[:, 2 + t % 2, :], ACT.Copy).then_inc(sem("pT_hi"), 1)
                    if hh % 2 == 0 and not (tail and hh == E_BODY - 2):
                        e_qk_scalar(turn, hh // 2 + 1)
                    act.wait_ge(sem("head_ps"), h + 1)
                    act.activation(e_cT_hi[:, hh % 2, :], ps[:, 1, :], ACT.Copy).then_inc(sem("head_hi"), 1)

                with act.Fori(0, E_HEADS // 4) as i:
                    for v in range(2):
                        for u in range(2):
                            n = (2 * i + v) * 2 + u
                            act.wait_ge(sem("e_u_ps"), n + 1)
                            act.activation(e_u[:, u, :], ps[:, 0, 0:E_R], ACT.Copy).then_inc(sem("e_u"), 1)
                            act.wait_ge(sem("e_mg_ps"), n + 1)
                            if u == 0:
                                act.wait_ge(sem(f"e_pair_kept{v}"), 32 * i + 1)
                            act.activation(e_qkw[:, v, 0, 0:4 * P].rearrange("p (c n) -> p c n", c=C)[:, :, u * E_R:(u + 1) * E_R],
                                           ps[:, 1, 0:C * E_R].rearrange("p (c n) -> p c n", c=C), ACT.Copy).then_inc(sem("e_mg_hi"), 1)
                            act.activation(e_g[:, v, 0, u * D:(u + 1) * D], ps[:, 2, :], ACT.Copy).then_inc(sem("e_mg_hi"), 1)
                        act.wait_ge(sem(f"e_blob_in{v}"), 32 * (i + 1))
                        act.activation(e_qkw[:, v, 0, 4 * P:5 * P], e_wkr[:, v, :], ACT.Copy).then_inc(sem("e_wkr_hi"), 1)
                with act.Fori(0, B) as i:
                    norm_scalar(act, "e", i)
                    act.wait_ge(sem("e_kvr"), i + 1)
                    act.activation(e_kvr_hi[:, :, :], e_kvr[:, :, :], ACT.Copy).then_inc(sem("e_kvr_hi"), 1)
                    act.wait_ge(sem("e_kT_ps"), i + 1)
                    act.activation(e_kT_hi[:, :], ps[:, 2, :], ACT.Copy).then_inc(sem("e_kT_hi"), 1)
                    e_qk_scalar(i * E_TURNS, 0)
                    for t in range(TB):
                        e_exp_scalar(i * E_HEADS, 0, t)
                    e_head_scalar(i * E_TURNS, 0)
                    with act.Fori(0, E_TURNS - 1) as g:
                        for hh in (1, 2, 3):
                            e_head_scalar(i * E_TURNS + g, hh)
                        e_head_scalar(i * E_TURNS + g + 1, 0)
                    for hh in (1, 2, 3):
                        e_head_scalar((i + 1) * E_TURNS - 1, hh, True)
                end_stage(act, 4)
            if stages > 5:
                act.wait_ge(sem("stage_in"), 192)
                act.activation(f_w_hi[:, :, :], f_w[:, :, :], ACT.Copy).then_inc(sem("weights_hi"), 1)
                act.activation(f_d_hi[:, :], f_d[:, :], ACT.Copy).then_inc(sem("weights_hi"), 1)
                with act.Fori(0, B) as i:
                    norm_scalar(act, "f", i)
                    act.wait_ge(sem("ln_xn"), TB * (ln_turn("f", i) + 1))
                    for j in range(TB):
                        act.activation(f_junk[:, :], xn[:, j, :], ACT.Square, accum_out=f_xx[:, j:j + 1]).then_inc(sem("f_xx"), 1)
                        act.wait_ge(sem("f_xx"), i * TB + j + 1)
                    act.wait_ge(sem("f_z"), i + 1)
                    act.activation(f_g[:, 1, :, :], f_g[:, 0, :, :], ACT.Exp, scale=-1.0).then_inc(sem("f_e"), 1)
                    act.wait_ge(sem("f_mT_ps"), i + 1)
                    act.activation(f_mT_hi[:, :], ps[0:F_K, 4, :], ACT.Copy).then_inc(sem("f_mT_hi"), 1)
                end_stage(act, 5)
            if stages > 6:
                for n, dst in enumerate((g_wq_hi, g_wo_hi)):
                    act.wait_ge(sem("g_in"), 16 * (n + 1))
                    act.activation(dst[:, :, :], g_w[:, :, :], ACT.Copy).then_inc(sem("weights_hi"), 1)
                act.wait_ge(sem("g_in"), 48)
                act.activation(g_wkv_hi[:, :], g_w[:, 0:2, :].rearrange("p a n -> p (a n)"), ACT.Copy).then_inc(sem("weights_hi"), 1)
                act.wait_ge(sem("g_mask"), 1)
                act.activation(g_mask_r[:, :], g_mask[:, :], ACT.Copy).then_inc(sem("weights_hi"), 1)
                act.activation(g_ident_r[:, :], ident[:, :], ACT.Copy).then_inc(sem("weights_hi"), 1)

                def g_qk_scalar(n, g):
                    act.wait_ge(sem("scores_ps"), TB * (G_HEADS_BEFORE + n * 4))
                    act.activation(g_qk_hi[:, 0, :], g_qT[:, g, :], ACT.Copy).then_inc(sem("qk_hi"), 1)
                    act.activation(g_qk_hi[:, 1, :], g_kT[:, g, :], ACT.Copy).then_inc(sem("qk_hi"), 1)

                def g_v_scalar(n):
                    act.wait_ge(sem("g_v_ps"), n + 1)
                    act.activation(g_v_hi[:, :, :], ps[:, 6, :].rearrange("p (t d) -> p t d", t=TB), ACT.Copy).then_inc(sem("g_v_hi"), 1)

                def g_exp_scalar(h, hh):
                    for t in range(TB):
                        act.wait_ge(sem("score_max"), h * TB + t + 1)
                        act.activation(g_p[:, t, 0:(t + 1) * P], ps[:, t, 0:(t + 1) * P], ACT.Exp, bias=g_st[:, hh % 2, t:t + 1],
                                       accum_out=g_st[:, hh % 2, 4 + t:5 + t]).then_inc(sem("exp"), 1)

                def g_heads_scalar(n, g, tail):
                    for hh in range(4):
                        h = G_HEADS_BEFORE + n * 4 + hh
                        if hh == 3 and not tail:
                            g_qk_scalar(n + 1, g + 1)
                        for c in range(TB):
                            act.wait_ge(sem("pT_ps"), h * TB + c + 1)
                            act.activation(g_pT_hi[:, c, c * P:], ps[:, 4 + c % 3, c * P:], ACT.Copy).then_inc(sem("pT_hi"), 1)
                        if hh < 3 or not tail:
                            g_exp_scalar(h + 1, hh + 1)
                        r = slice(hh * G_HD, (hh + 1) * G_HD)
                        act.wait_ge(sem("head_ps"), h + 1)
                        act.activation(xT_hi[r, g, :], ps[r, 7, :], ACT.Copy).then_inc(sem("g_oT_hi"), 1)
                        if hh == 3 and not tail:
                            g_v_scalar(n + 1)

                with act.Fori(0, B) as i:
                    norm_scalar(act, "g", i)
                    act.wait_ge(sem("g_ctx_in"), 16 * (i + 1))
                    act.activation(g_ctx_hi[:, :], g_ctxT[:, :], ACT.Copy).then_inc(sem("g_ctx_hi"), 1)
                    for m_ in range(C):
                        act.wait_ge(sem("g_q_ps"), i * C + m_ + 1)
                        act.activation(g_qT[:, m_, :], ps[:, 2 + m_ % 2, :], ACT.Copy, scale=G_SCALE).then_inc(sem("g_q"), 1)
                        act.wait_ge(sem("g_k_ps"), i * C + m_ + 1)
                        act.activation(g_kT[:, m_, :], ps[:, 4 + m_ % 2, :], ACT.Copy).then_inc(sem("g_k"), 1)
                    g_v_scalar(i * C)
                    act.wait_ge(sem("g_k"), C * (i + 1))
                    g_qk_scalar(i * C, 0)
                    g_exp_scalar(G_HEADS_BEFORE + i * C * 4, 0)
                    with act.Fori(0, C - 1) as g:
                        g_heads_scalar(i * C + g, g, False)
                    g_heads_scalar(i * C + C - 1, C - 1, True)
                end_stage(act, 6)
            if stages > 7:
                act.wait_ge(sem("h_gw_in"), 16)
                act.activation(h_gw_hi[:, :, :], h_gw[:, :, :], ACT.Copy).then_inc(sem("weights_hi"), 1)

                def h_gu_scalar(m_, u):
                    n = 2 * m_ + u
                    act.wait_ge(sem(f"h_gu_in{u}"), 16 * (m_ + 1))
                    act.wait_ge(sem("h_gu_ps"), n + 1)
                    act.activation(h_w_hi[:, u, 0:2 * D], h_w[:, u, 0:2 * D], ACT.Copy).then_inc(sem("h_gu_hi"), 1)

                def h_d_scalar(m_, u):
                    n = 2 * m_ + u
                    act.wait_ge(sem(f"h_d_in{u}"), 16 * (m_ + 1))
                    act.wait_ge(sem("h_down"), n + 1)
                    act.activation(h_w_hi[:, u, 2 * D:], h_w[:, u, 2 * D:], ACT.Copy).then_inc(sem("h_d_hi"), 1)

                def h_hidden_scalar(n, u):
                    act.wait_ge(sem("h_gu_ps"), n + 3)
                    act.activation(h_sg[:, u, :], ps[:, u, :], ACT.Silu).then_inc(sem("h_sg"), 1)
                    act.wait_ge(sem("h_h"), n + 3)
                    act.activation(h_h_hi[:, u, :], h_h[:, u, :], ACT.Copy).then_inc(sem("h_h_hi"), 1)

                with act.Fori(0, B) as i:
                    h_gu_scalar(i * HC, 0)
                    h_gu_scalar(i * HC, 1)
                    h_d_scalar(i * HC, 0)
                    norm_scalar(act, "h", i)
                    act.wait_ge(sem("h_logit"), i + 1)
                    act.activation(h_l[:, 2, :, :], h_l[:, 1, :, :], ACT.Exp).then_inc(sem("h_le"), 1)
                    with act.Fori(0, HC - 1) as f:
                        m_ = i * HC + f
                        h_hidden_scalar(2 * m_, 0)
                        h_gu_scalar(m_ + 1, 0)
                        h_d_scalar(m_, 1)
                        h_hidden_scalar(2 * m_ + 1, 1)
                        h_gu_scalar(m_ + 1, 1)
                        h_d_scalar(m_ + 1, 0)
                    last = (i + 1) * HC - 1
                    h_hidden_scalar(2 * last, 0)
                    h_d_scalar(last, 1)
                    h_hidden_scalar(2 * last + 1, 1)
                end_stage(act, 7)

        @block.vector
        def _(dve):
            k = InOrder(dve, sem("dve_steps"))
            dve.wait_ge(sem("consts"), 1)
            dve.wait_ge(sem("tg"), 1)
            dve.wait_ge(sem("weights_hi"), HI_BEFORE["a"] + 2)
            k(dve.tensor_tensor(a_ctx_lo[:, :], a_ctxT[:, :], a_ctx_hi[:, :].bitcast(F32), ALU.subtract))
            dve.tensor_tensor(a_wk_lo[:, :], a_wk[:, :], a_wk_hi[:, :].bitcast(F32), ALU.subtract).then_inc(sem("weights"), 1)
            dve.wait_ge(sem("weights"), READY["a"])
            with dve.Fori(0, B) as i:
                per = 2 * TB + TB * 9
                o = k.enter(i, per)
                dve.wait_ge(sem("x_in"), 16 * (i + 1))
                plain(dve)
                norm_vector(dve, k, "a", i)
                dve.wait_ge(sem("a_kvT_hi"), i + 1)
                dve.tensor_tensor(a_kvT_lo[:, :], a_kvT[:, :], a_kvT_hi[:, :].bitcast(F32), ALU.subtract).then_inc(sem("a_kvT"), 1)
                dve.wait_ge(sem("a_kv_hi"), i + 1)
                dve.tensor_tensor(a_kv_lo[:, :, :], ps[:, 3, :].rearrange("p (t d) -> p t d", t=TB),
                                  a_kv_hi[:, :, :].bitcast(F32), ALU.subtract).then_inc(sem("a_kv"), 1)
                dve.wait_ge(sem("a_oT_hi"), i + 1)
                dve.tensor_tensor(a_oT_lo[:, :], ps[:, 4, :], a_oT_hi[:, :].bitcast(F32), ALU.subtract).then_inc(sem("a_oT"), 1)

                def a_stats_vector(j):
                    st = a_st[:, j % 2, :]
                    dve.wait_ge(sem("a_sim_ps"), i * TB + j + 1)
                    k(dve.bn_stats(st[:, 0:6], ps[:, 5 + j % 2, :]))
                    plain(dve)
                    k(dve.bn_aggr(st[:, 11:13], st[:, 0:6]))
                    dve.tensor_scalar(st[:, 7:8], st[:, 12:13], float(D) ** -1, 1e-6, ALU.mult, ALU.add).then_inc(sem("a_sim_var"), 1)

                def a_norm_vector(j):
                    n, st, sim = i * TB + j, a_st[:, j % 2, :], a_sim[:, j % 2, :]
                    dve.wait_ge(sem("a_sim_rstd"), n + 1)
                    k(dve.tensor_scalar(st[:, 13:14], st[:, 8:9], float(D) ** -0.5, None, ALU.mult))
                    dve.tensor_scalar(sim, ps[:, 5 + j % 2, :], st[:, 11:12], st[:, 13:14], ALU.subtract, ALU.mult).then_inc(sem("a_sim_used"), 1)
                    dve.wait_ge(sem("a_sim_used"), n + 1)
                    k(dve.tensor_tensor(sim, sim, a_gamma[:, :], ALU.mult))
                    k(dve.tensor_tensor(sim, sim, a_beta[:, :], ALU.add))
                    k(dve.tensor_reduce(st[:, 6:7], sim, AX.X, ALU.max))
                    dve.tensor_scalar(st[:, 9:10], st[:, 6:7], -1.0, None, ALU.mult).then_inc(sem("a_max"), 1)

                def a_add_vector(j):
                    n, st = i * TB + j, a_st[:, j % 2, :]
                    dve.wait_ge(sem("a_exp"), n + 1)
                    k(dve.reciprocal(st[:, 14:15], st[:, 10:11]))
                    k(dve.tensor_tensor(st[:, 15:16], st[:, 14:15], tg[:, 0:1], ALU.mult))
                    k(dve.scalar_tensor_tensor(X[:, n, :], a_sim[:, j % 2, :], st[:, 15:16], X[:, n, :], ALU.mult, ALU.add))

                a_stats_vector(0)
                for j in range(TB):
                    if j + 1 < TB:
                        a_stats_vector(j + 1)
                    a_norm_vector(j)
                    if j:
                        a_add_vector(j - 1)
                a_add_vector(TB - 1)
                k.leave(o, B, per)
            end_stage(dve, 0)

            if stages > 1:
                for w in range(2):
                    dve.wait_ge(sem("b_in"), 32)
                    dve.tensor_reduce(b_st[:, w:w + 1], b_raw[w], AX.X, ALU.add, apply_absolute_value=True).then_inc(sem("b_abs"), 1)
                for w, (dst, raw) in enumerate(zip(b_weights, b_raw)):
                    dve.wait_ge(sem("b_abs_ps"), w + 1)
                    k(dve.tensor_scalar(b_st[:, 2 + w:3 + w], ps[:, 2 + w, 0:1], 1.0 / (HID * D), None, ALU.mult))
                    k(dve.tensor_scalar(b_st[:, 4:5], b_st[:, 2 + w:3 + w], 1e-8, 0.5, ALU.add, ALU.mult))
                    k(dve.tensor_scalar(b_st[:, 5:6], b_st[:, 4:5], -1.0, None, ALU.mult))
                    for h in range(2):
                        half = slice(h * 2 * HID, (h + 1) * 2 * HID)
                        k(dve.tensor_scalar(b_tmp, raw[:, half], b_st[:, 5:6], None, ALU.is_lt))
                        k(dve.scalar_tensor_tensor(dst[:, half], raw[:, half], b_st[:, 4:5], b_tmp, ALU.is_gt, ALU.subtract))
                dve.wait_ge(sem("b_rows_in"), 64)
                k(dve.tensor_scalar(b_rows[:, 1:3, :], b_rows[:, 1:3, :], tg[:, 4:5], None, ALU.mult))
                dve.sem_inc(sem("weights"), 1)
                with dve.Fori(0, B) as i:
                    per = 2 * TB + TB + 3 + 3 + ROUNDS * SEARCH_STEPS + 1 + TB + TB * 7
                    o = k.enter(i, per)
                    norm_vector(dve, k, "b", i)
                    for j in range(TB):
                        for q in range(4):
                            n = (i * TB + j) * 4 + q
                            dve.wait_ge(sem("b_z_ps"), n + 1)
                            dve.scalar_tensor_tensor(b_z[:, j, q * BANK:(q + 1) * BANK], ps[:, 4 + q, :], b_st[:, 2:3],
                                                     b_bsyn[:, q * BANK:(q + 1) * BANK], ALU.mult, ALU.add).then_inc(sem("b_z_used"), 1)
                    low, step, other, cand, cnt, take = (b_tk[:, r, :] for r in range(6))
                    dve.wait_ge(sem("b_z_used"), 16 * (i + 1))
                    for j in range(TB):
                        k(dve.tensor_reduce(step[:, j:j + 1], b_z[:, j, :], AX.X, ALU.max))
                    k(dve.tensor_scalar(step, step, 0.0, 0.5, ALU.max, ALU.mult))
                    k(dve.memset(low, 0.0))
                    k(dve.tensor_copy(cand, step))
                    search_vector(dve, k, i, b_z, b_junk[:, 0, :], low, step, other, cand, cnt, take, SYN_K)
                    search_vector_end(dve, k, "b", i, low)
                    for j in range(TB):
                        k(dve.scalar_tensor_tensor(b_z[:, j, :], b_z[:, j, :], low[:, j:j + 1], b_z[:, j, :], ALU.is_ge, ALU.mult))
                        dve.sem_inc(sem("b_h"), 1)
                    def b_hT_vector(j):
                        n = i * TB + j
                        for q in range(4):
                            hi, lo = (w[:, 4 * q:4 * q + 4, :] for w in b_hT[j % 2])
                            dve.wait_ge(sem("b_hT_hi"), n * 4 + q + 1)
                            dve.tensor_tensor(lo, ps[:, q, :].rearrange("p (c t) -> p c t", c=4), hi.bitcast(F32), ALU.subtract)\
                                .then_inc(sem("b_hT"), 1)

                    b_hT_vector(0)
                    for j in range(TB):
                        n = i * TB + j
                        if j + 1 < TB:
                            b_hT_vector(j + 1)
                        dve.wait_ge(sem("b_y_ps"), n + 1)
                        dve.scalar_tensor_tensor(b_y[:, :], ps[:, 4 + j % 2, :], b_st[:, 3:4], xn[:, j, :], ALU.mult, ALU.add)\
                            .then_inc(sem("b_y_used"), 1)
                        dve.wait_ge(sem("b_y_used"), n + 1)
                        k(dve.tensor_tensor(b_y[:, :], b_y[:, :], b_rows[:, 0, :], ALU.add))
                        k(dve.bn_stats(b_st[:, 9:15], b_y[:, :]))
                        plain(dve)
                        k(dve.bn_aggr(b_st[:, 4:6], b_st[:, 9:15]))
                        dve.tensor_scalar(b_st[:, 7:8], b_st[:, 5:6], LN_EPS, None, ALU.add).then_inc(sem("b_y_var"), 1)
                        dve.wait_ge(sem("b_y_rstd"), n + 1)
                        k(dve.tensor_scalar(b_y[:, :], b_y[:, :], b_st[:, 4:5], b_st[:, 8:9], ALU.subtract, ALU.mult))
                        k(dve.tensor_tensor(b_y[:, :], b_y[:, :], b_rows[:, 1, :], ALU.mult))
                        k(dve.tensor_tensor(b_y[:, :], b_y[:, :], b_rows[:, 2, :], ALU.add))
                        k(dve.tensor_tensor(X[:, n, :], X[:, n, :], b_y[:, :], ALU.add))
                    k.leave(o, B, per)
                end_stage(dve, 1)

            if stages > 2:
                dve.wait_ge(sem("stage_in"), 48)
                dve.wait_ge(sem("weights_hi"), HI_BEFORE["c"] + 2)
                k(dve.tensor_tensor(c_ctx_lo[:, :], c_ctxT[:, :], c_ctx_hi[:, :].bitcast(F32), ALU.subtract))
                dve.tensor_tensor(c_w_lo[:, :, :], c_w[:, :, :], c_w_hi[:, :, :].bitcast(F32), ALU.subtract).then_inc(sem("weights"), 1)
                dve.wait_ge(sem("c_g"), 1)
                k(dve.tensor_scalar(c_g[:, 1:2], c_g[:, 1:2], 1.0, None, ALU.add))
                k(dve.reciprocal(c_g[:, 1:2], c_g[:, 1:2]))
                k(dve.tensor_scalar(c_g[:, 2:3], c_g[:, 1:2], -1.0, 1.0, ALU.mult, ALU.add))
                k(dve.tensor_tensor(c_g[:, 2:3], c_g[:, 2:3], tg[:, 1:2], ALU.mult))
                k(dve.tensor_scalar(c_g[:, 3:4], c_g[:, 1:2], 0.5, None, ALU.mult))
                k(dve.tensor_tensor(c_g[:, 3:4], c_g[:, 3:4], tg[:, 1:2], ALU.mult))
                with dve.Fori(0, B) as i:
                    per = 2 * TB + 2 * TB + 3 + 3 + ROUNDS * SEARCH_STEPS + 1 + TB + 2 * TB
                    o = k.enter(i, per)
                    norm_vector(dve, k, "c", i)
                    for w in range(2):
                        dve.wait_ge(sem("c_qk_hi"), i * 2 + w + 1)
                        dve.tensor_tensor(c_qk_lo[:, w, :], ps[:, 2 + w, :], c_qk_hi[:, w, :].bitcast(F32), ALU.subtract)\
                            .then_inc(sem("c_qk"), 1)
                    low, step, other, cand, cnt, take = (c_tk[:, r, :] for r in range(6))
                    dve.wait_ge(sem("c_sim"), TB * (i + 1))
                    for j in range(TB):
                        k(dve.tensor_reduce(step[:, j:j + 1], c_sim[:, j, :], AX.X, ALU.max))
                        k(dve.tensor_reduce(low[:, j:j + 1], c_sim[:, j, :], AX.X, ALU.min))
                    k(dve.tensor_tensor(step, step, low, ALU.subtract))
                    k(dve.tensor_scalar(step, step, 0.5, None, ALU.mult))
                    k(dve.tensor_tensor(cand, low, step, ALU.add))
                    search_vector(dve, k, i, c_sim, c_junk[:, 0, :], low, step, other, cand, cnt, take, SIM_K)
                    search_vector_end(dve, k, "c", i, low)
                    dve.wait_ge(sem("c_e"), TB * (i + 1))
                    for j in range(TB):
                        k(dve.scalar_tensor_tensor(c_a[:, j, :], c_sim[:, j, :], low[:, j:j + 1], c_a[:, j, :], ALU.is_ge, ALU.mult))
                    dve.sem_inc(sem("c_A"), 1)
                    for j in range(TB):
                        n = i * TB + j
                        k(dve.scalar_tensor_tensor(X[:, n, :], xn[:, j, :], c_g[:, 2:3], X[:, n, :], ALU.mult, ALU.add))
                        dve.wait_ge(sem("c_AT_ps"), n + 1)
                        dve.tensor_tensor(c_t[:, :], ps[:, 6 + j % 2, :], c_a[:, j, :], ALU.add).then_inc(sem("c_AT_used"), 1)
                        dve.wait_ge(sem("c_AT_used"), n + 1)
                        k(dve.scalar_tensor_tensor(X[:, n, :], c_t[:, :], c_g[:, 3:4], X[:, n, :], ALU.mult, ALU.add))
                    k.leave(o, B, per)
                end_stage(dve, 2)

            if stages > 3:
                dve.wait_ge(sem("stage_in"), 96)
                for c in range(C):
                    dve.tensor_tensor(d_w[:, c, :], d_w[:, c, :], d_rows[:, 0, :], ALU.mult).then_inc(sem("d_ws"), 1)
                k(dve.tensor_scalar(d_rows[:, 1, :], d_rows[:, 1, :], tg[:, 5:6], None, ALU.mult))
                dve.wait_ge(sem("weights_hi"), HI_BEFORE["d"] + 1)
                dve.tensor_tensor(d_w_lo[:, :, :], d_w[:, :, :], d_w_hi[:, :, :].bitcast(F32), ALU.subtract).then_inc(sem("weights"), 1)
                with dve.Fori(0, B) as i:
                    per = 2 * TB + TB
                    o = k.enter(i, per)
                    norm_vector(dve, k, "d", i)
                    for j in range(TB):
                        n = i * TB + j
                        k(dve.tensor_tensor(X[:, n, :], X[:, n, :], d_rows[:, 1, :], ALU.add))
                        dve.wait_ge(sem("y_ps"), n + 1)
                        dve.scalar_tensor_tensor(X[:, n, :], ps[:, 2 + j % 2, :], tg[:, 5:6], X[:, n, :], ALU.mult, ALU.add)\
                            .then_inc(sem("y_used"), 1)
                    dve.wait_ge(sem("y_used"), TB * (i + 1))
                    k.leave(o, B, per)
                end_stage(dve, 3)

            if stages > 4:
                dve.wait_ge(sem("e_tables"), 32)
                dve.memset(e_zero[:, :].bitcast(F32), 0.0).then_inc(sem("zeros"), 1)

                def e_qk_vector(turn, d):
                    u = d % 2
                    for w in range(2):
                        dve.wait_ge(sem("qk_hi"), turn * E_BODY + d * 2 + w + 1)
                        dve.tensor_tensor(e_qk_lo[:, u, w, :], ps[:, 2 + w, :], e_qk_hi[:, u, w, :].bitcast(F32), ALU.subtract)\
                            .then_inc(sem("qk"), 1)

                def e_max_vector(h, a, t):
                    dve.wait_ge(sem("scores_ps"), h * TB + t + 1)
                    dve.tensor_reduce(e_st[:, a, t:t + 1], ps[:, t % 2, :], AX.X, ALU.max, negate=True).then_inc(sem("score_max"), 1)

                def e_scale_vector(h, a):
                    dve.wait_ge(sem("exp"), TB * (h + 1))
                    k(dve.reciprocal(e_st[:, a, 8:12], e_st[:, a, 4:8]))
                    for t in range(TB):
                        dve.tensor_scalar(e_p[:, a, t, :], e_p[:, a, t, :], e_st[:, a, 8 + t:9 + t], None, ALU.mult).then_inc(sem("e_p"), 1)

                def e_head_vector(turn, hh, tail=False):
                    h = turn * E_BODY + hh
                    more = not (tail and hh == E_BODY - 1)
                    for what, t in E_VECTOR_STEPS:
                        if what == "scores" and more:
                            e_max_vector(h + 1, (hh + 1) % 2, t)
                        if what == "turned":
                            dve.wait_ge(sem("pT_hi"), h * TB + t + 1)
                            dve.tensor_tensor(e_pT_lo[:, t, :], ps[:, 2 + t % 2, :], e_pT_hi[:, t, :].bitcast(F32), ALU.subtract)\
                                .then_inc(sem("pT"), 1)
                    if more:
                        e_scale_vector(h + 1, (hh + 1) % 2)
                    if hh % 2 == 0 and not (tail and hh == E_BODY - 2):
                        e_qk_vector(turn, hh // 2 + 1)
                    dve.wait_ge(sem("head_hi"), h + 1)
                    dve.tensor_tensor(e_cT_lo[:, hh % 2, :], ps[:, 1, :], e_cT_hi[:, hh % 2, :].bitcast(F32), ALU.subtract)\
                        .then_inc(sem("head_out"), 1)

                with dve.Fori(0, E_HEADS // 4) as i:
                    for v in range(2):
                        for u in range(2):
                            n = (2 * i + v) * 2 + u
                            dve.wait_ge(sem("e_mg_hi"), 2 * (n + 1))
                            m_ = [e_qkw[:, v, q, 0:4 * P].rearrange("p (c n) -> p c n", c=C)[:, :, u * E_R:(u + 1) * E_R] for q in range(2)]
                            g_ = [e_g[:, v, q, u * D:(u + 1) * D] for q in range(2)]
                            dve.tensor_tensor(m_[1], ps[:, 1, 0:C * E_R].rearrange("p (c n) -> p c n", c=C), m_[0].bitcast(F32),
                                              ALU.subtract).then_inc(sem("e_mg"), 1)
                            dve.tensor_tensor(g_[1], ps[:, 2, :], g_[0].bitcast(F32), ALU.subtract).then_inc(sem("e_mg"), 1)
                        dve.wait_ge(sem("e_wkr_hi"), 2 * i + v + 1)
                        dve.wait_ge(sem("e_mg"), 4 * (2 * i + v + 1) + 1)
                        dve.tensor_tensor(e_qkw[:, v, 1, 4 * P:5 * P], e_wkr[:, v, :], e_qkw[:, v, 0, 4 * P:5 * P].bitcast(F32), ALU.subtract)\
                            .then_inc(sem("e_pair_made"), 1)
                        dve.wait_ge(sem("e_pair_made"), 2 * i + v + 1)
                        dve.sem_inc(sem("e_blob_used"), 1)
                with dve.Fori(0, B) as i:
                    per = 2 * TB + 4 + E_HEADS
                    o = k.enter(i, per)
                    norm_vector(dve, k, "e", i)
                    dve.wait_ge(sem("e_ctx_in"), 16 * (i + 1))
                    hd = DC // 2
                    k(dve.tensor_tensor(e_rot[:, :, 0:hd], e_ctx[:, :, hd:DC], e_sin[:, :, 0:hd], ALU.mult))
                    k(dve.tensor_tensor(e_rot[:, :, hd:DC], e_ctx[:, :, 0:hd], e_sin[:, :, hd:DC], ALU.mult))
                    k(dve.tensor_tensor(e_kvr[:, :, :], e_ctx[:, :, :], e_cos[:, :, :], ALU.mult))
                    dve.tensor_tensor(e_kvr[:, :, :], e_kvr[:, :, :], e_rot[:, :, :], ALU.add).then_inc(sem("e_kvr"), 1)
                    dve.wait_ge(sem("e_kvr"), i + 1)
                    dve.sem_inc(sem("e_ctx_used"), 1)
                    dve.wait_ge(sem("e_kvr_hi"), i + 1)
                    k(dve.tensor_tensor(e_kvr_lo[:, :, :], e_kvr[:, :, :], e_kvr_hi[:, :, :].bitcast(F32), ALU.subtract))
                    dve.wait_ge(sem("e_kT_hi"), i + 1)
                    dve.tensor_tensor(e_kT_lo[:, :], ps[:, 2, :], e_kT_hi[:, :].bitcast(F32), ALU.subtract).then_inc(sem("e_kT"), 1)
                    plain(dve)
                    e_qk_vector(i * E_TURNS, 0)
                    for t in range(TB):
                        e_max_vector(E_HEADS * i, 0, t)
                    e_scale_vector(E_HEADS * i, 0)
                    e_head_vector(i * E_TURNS, 0)
                    plain(dve)
                    with dve.Fori(0, E_TURNS - 1) as g:
                        p2 = k.enter(g, E_BODY)
                        for hh in (1, 2, 3):
                            e_head_vector(i * E_TURNS + g, hh)
                        e_head_vector(i * E_TURNS + g + 1, 0)
                        k.leave(p2, E_TURNS - 1, E_BODY)
                    for hh in (1, 2, 3):
                        e_head_vector((i + 1) * E_TURNS - 1, hh, True)
                    dve.wait_ge(sem("e_y_ps"), i + 1)
                    for j in range(TB):
                        n = i * TB + j
                        dve.scalar_tensor_tensor(X[:, n, :], ps[:, 4 + j, :], tg[:, 2:3], X[:, n, :], ALU.mult, ALU.add)\
                            .then_inc(sem("e_y_used"), 1)
                    dve.wait_ge(sem("e_y_used"), TB * (i + 1))
                    k.leave(o, B, per)
                end_stage(dve, 4)

            if stages > 5:
                dve.wait_ge(sem("weights_hi"), HI_BEFORE["f"] + 2)
                k(dve.tensor_tensor(f_w_lo[:, :, :], f_w[:, :, :], f_w_hi[:, :, :].bitcast(F32), ALU.subtract))
                k(dve.tensor_tensor(f_d_lo[:, :], f_d[:, :], f_d_hi[:, :].bitcast(F32), ALU.subtract))
                dve.tensor_tensor(f_q[:, :, :], f_q[:, :, :], f_w[:, :, :], ALU.mult).then_inc(sem("weights"), 1)
                dve.wait_ge(sem("f_const_ps"), 1)
                k(dve.tensor_copy(f_const[:, :], ps[:, 5, 0:F_N]))
                with dve.Fori(0, B) as i:
                    per = 2 * TB + 36
                    o = k.enter(i, per)
                    norm_vector(dve, k, "f", i)
                    for j in range(TB):
                        n = i * TB + j
                        dve.wait_ge(sem("f_a_ps"), n + 1)
                        k(dve.tensor_tensor(f_a[:, j, 0:P], ps[:, 2 + j % 2, 0:P], f_const[:, 0:P], ALU.subtract))
                        dve.scalar_tensor_tensor(f_a[:, j, P:F_N], ps[:, 2 + j % 2, P:F_N], -2.0, f_const[:, P:F_N], ALU.mult, ALU.add)\
                            .then_inc(sem("f_a"), 1)
                    dve.wait_ge(sem("f_a"), TB * (i + 1))
                    k(dve.tensor_tensor(f_sq[:, :, :], f_a[:, :, 0:64], f_a[:, :, 0:64], ALU.mult))
                    score, pri = f_g[:, 2, :, :], f_g[:, 3, :, :]
                    k(dve.tensor_reduce(score, f_sq[:, :, :].rearrange("p t (n s) -> p t n s", n=8), AX.X, ALU.add))
                    dve.wait_ge(sem("f_xx"), TB * (i + 1))
                    for j in range(TB):
                        k(dve.tensor_scalar(f_a[:, j, P:F_N], f_a[:, j, P:F_N], f_xx[:, j:j + 1], None, ALU.add))
                    k(dve.reciprocal(f_g[:, 4, :, :], f_a[:, :, P:F_N]))
                    k(dve.tensor_tensor(score, score, f_g[:, 4, :, :], ALU.mult))
                    for j in range(TB):
                        k(dve.tensor_tensor(f_g[:, 4, j, :], score[:, j, :], f_rows[:, 0, :], ALU.subtract))
                    for j in range(TB):
                        k(dve.tensor_tensor(f_g[:, 0, j, :], f_g[:, 4, j, :], f_rows[:, 1, :], ALU.mult))
                    dve.sem_inc(sem("f_z"), 1)
                    dve.wait_ge(sem("f_e"), i + 1)
                    gate = f_g[:, 1, :, :]
                    k(dve.tensor_scalar(gate, gate, 1.0, None, ALU.add))
                    k(dve.reciprocal(gate, gate))
                    top = f_s[:, 0, :]
                    k(dve.tensor_reduce(top, gate, AX.X, ALU.max))
                    k(dve.tensor_tensor(pri, gate, top.unsqueeze(2).broadcast_to([P, TB, 8]), ALU.is_ge))
                    for j in range(TB):
                        k(dve.tensor_tensor(pri[:, j, :], pri[:, j, :], f_rows[:, 2, :], ALU.mult))
                    k(dve.tensor_reduce(f_s[:, 1, :], pri, AX.X, ALU.max))
                    hot = f_m[:, :, 64:72]
                    k(dve.tensor_tensor(hot, pri, f_s[:, 1, :].unsqueeze(2).broadcast_to([P, TB, 8]), ALU.is_equal))
                    for j in range(TB):
                        dve.tensor_tensor(f_m[:, j, 0:64].rearrange("p (n h) -> p n h", n=8),
                                          f_a[:, j, 64:P].rearrange("p (n h) -> p n h", n=8),
                                          hot[:, j, :].unsqueeze(2).broadcast_to([P, 8, 8]), ALU.mult).then_inc(sem("f_m"), 1)
                    k(dve.tensor_scalar(f_s[:, 2, :], top, tg[:, 6:7], None, ALU.mult))
                    k(dve.tensor_scalar(f_s[:, 3, :], f_s[:, 2, :], -1.0, tg[:, 6:7], ALU.mult, ALU.add))
                    dve.wait_ge(sem("f_mT_hi"), i + 1)
                    dve.tensor_tensor(f_mT_lo[:, :], ps[0:F_K, 4, :], f_mT_hi[:, :].bitcast(F32), ALU.subtract).then_inc(sem("f_mT"), 1)
                    for j in range(TB):
                        n = i * TB + j
                        k(dve.scalar_tensor_tensor(X[:, n, :], xn[:, j, :], f_s[:, 3, j:j + 1], X[:, n, :], ALU.mult, ALU.add))
                        dve.wait_ge(sem("y_ps"), 1 * TILES + n + 1)
                        dve.scalar_tensor_tensor(X[:, n, :], ps[:, 6 + j % 2, :], f_s[:, 2, j:j + 1], X[:, n, :], ALU.mult, ALU.add)\
                            .then_inc(sem("y_used"), 1)
                    dve.wait_ge(sem("y_used"), 1 * TILES + TB * (i + 1))
                    k.leave(o, B, per)
                end_stage(dve, 5)

            if stages > 6:
                for n, (dst, hi) in enumerate(((g_wq_lo, g_wq_hi), (g_wo_lo, g_wo_hi))):
                    dve.wait_ge(sem("weights_hi"), HI_BEFORE["g"] + n + 1)
                    dve.tensor_tensor(dst[:, :, :], g_w[:, :, :], hi[:, :, :].bitcast(F32), ALU.subtract).then_inc(sem("g_raw_used"), 1)
                dve.wait_ge(sem("weights_hi"), HI_BEFORE["g"] + 5)
                dve.tensor_tensor(g_wkv_lo[:, :], g_w[:, 0:2, :].rearrange("p a n -> p (a n)"), g_wkv_hi[:, :].bitcast(F32), ALU.subtract)\
                    .then_inc(sem("weights"), 1)

                def g_qk_vector(n, g):
                    for w, src in enumerate((g_qT, g_kT)):
                        dve.wait_ge(sem("qk_hi"), G_HEADS_BEFORE + n * 2 + w + 1)
                        dve.tensor_tensor(g_qk_lo[:, w, :], src[:, g, :], g_qk_hi[:, w, :].bitcast(F32), ALU.subtract).then_inc(sem("qk"), 1)

                def g_v_vector(n):
                    dve.wait_ge(sem("g_v_hi"), n + 1)
                    dve.tensor_tensor(g_v_lo[:, :, :], ps[:, 6, :].rearrange("p (t d) -> p t d", t=TB), g_v_hi[:, :, :].bitcast(F32), ALU.subtract)\
                        .then_inc(sem("g_v"), 1)

                def g_diag_vector(h, hh):
                    dve.wait_ge(sem("exp"), (h + 1) * TB)
                    k(dve.reciprocal(g_st[:, hh % 2, 4:8], g_st[:, hh % 2, 4:8]))
                    for t in range(TB):
                        dve.tensor_scalar(g_diag[:, t, :], ident[:, :], g_st[:, hh % 2, 4 + t:5 + t], None, ALU.mult).then_inc(sem("g_diag"), 1)

                def g_max_vector(h, hh):
                    for t in range(TB):
                        dve.wait_ge(sem("scores_ps"), h * TB + t + 1)
                        dve.tensor_reduce(g_st[:, hh % 2, t:t + 1], ps[:, t, 0:(t + 1) * P], AX.X, ALU.max, negate=True).then_inc(sem("score_max"), 1)

                def g_heads_vector(n, g, tail):
                    for hh in range(4):
                        h = G_HEADS_BEFORE + n * 4 + hh
                        if hh == 3 and not tail:
                            g_qk_vector(n + 1, g + 1)
                        for c in range(TB):
                            dve.wait_ge(sem("pT_hi"), h * TB + c + 1)
                            dve.tensor_tensor(g_pT_lo[:, c, c * P:], ps[:, 4 + c % 3, c * P:], g_pT_hi[:, c, c * P:].bitcast(F32), ALU.subtract)\
                                .then_inc(sem("pT"), 1)
                        if hh < 3 or not tail:
                            g_max_vector(h + 1, hh + 1)
                            g_diag_vector(h + 1, hh + 1)
                        r = slice(hh * G_HD, (hh + 1) * G_HD)
                        dve.wait_ge(sem("g_oT_hi"), h - G_HEADS_BEFORE + 1)
                        dve.tensor_tensor(xT_lo[r, g, :], ps[r, 7, :], xT_hi[r, g, :].bitcast(F32), ALU.subtract).then_inc(sem("head_out"), 1)
                        if hh == 3 and not tail:
                            g_v_vector(n + 1)

                with dve.Fori(0, B) as i:
                    per = 2 * TB + C * 4
                    o = k.enter(i, per)
                    norm_vector(dve, k, "g", i)
                    dve.wait_ge(sem("g_ctx_hi"), i + 1)
                    dve.tensor_tensor(g_ctx_lo[:, :], g_ctxT[:, :], g_ctx_hi[:, :].bitcast(F32), ALU.subtract).then_inc(sem("g_ctx_used"), 1)
                    g_v_vector(i * C)
                    plain(dve)
                    g_qk_vector(i * C, 0)
                    g_max_vector(G_HEADS_BEFORE + i * C * 4, 0)
                    g_diag_vector(G_HEADS_BEFORE + i * C * 4, 0)
                    plain(dve)
                    with dve.Fori(0, C - 1) as g:
                        o2 = k.enter(g, 4)
                        g_heads_vector(i * C + g, g, False)
                    k.leave(o2, C - 1, 4)
                    g_heads_vector(i * C + C - 1, C - 1, True)
                    for j in range(TB):
                        n = i * TB + j
                        dve.wait_ge(sem("y_ps"), 2 * TILES + n + 1)
                        dve.scalar_tensor_tensor(X[:, n, :], ps[:, 2 + j % 2, :], tg[:, 3:4], X[:, n, :], ALU.mult, ALU.add)\
                            .then_inc(sem("y_used"), 1)
                    dve.wait_ge(sem("y_used"), 2 * TILES + TB * (i + 1))
                    k.leave(o, B, per)
                end_stage(dve, 6)

            if stages > 7:
                dve.wait_ge(sem("weights_hi"), HI_BEFORE["h"] + 1)
                dve.memset(h_zero[:, :].bitcast(F32), 0.0).then_inc(sem("zeros"), 1)
                dve.tensor_tensor(h_gw_lo[:, :, :], h_gw[:, :, :], h_gw_hi[:, :, :].bitcast(F32), ALU.subtract).then_inc(sem("weights"), 1)

                def h_gu_vector(n, u):
                    dve.wait_ge(sem("h_gu_hi"), n + 1)
                    dve.tensor_tensor(h_w_lo[:, u, 0:2 * D], h_w[:, u, 0:2 * D], h_w_hi[:, u, 0:2 * D].bitcast(F32), ALU.subtract)\
                        .then_inc(sem("h_gu_used"), 1)

                def h_d_vector(n, u):
                    dve.wait_ge(sem("h_d_hi"), n + 1)
                    dve.tensor_tensor(h_w_lo[:, u, 2 * D:], h_w[:, u, 2 * D:], h_w_hi[:, u, 2 * D:].bitcast(F32), ALU.subtract)\
                        .then_inc(sem("h_d_used"), 1)

                def h_hidden_vector(n, u, e):
                    dve.wait_ge(sem("h_sg"), n + 1)
                    k(dve.tensor_tensor(h_sg[:, u, :], ps[:, 2 + u, :], h_sg[:, u, :], ALU.mult))
                    dve.tensor_tensor(h_h[:, u, :], h_sg[:, u, :], h_gain[:, e, :], ALU.mult).then_inc(sem("h_h"), 1)
                    dve.wait_ge(sem("h_h_hi"), n + 1)
                    dve.tensor_tensor(h_h_lo[:, u, :], h_h[:, u, :], h_h_hi[:, u, :].bitcast(F32), ALU.subtract).then_inc(sem("h_h_lo"), 1)

                with dve.Fori(0, B) as i:
                    per = 2 * TB + 9 + 2 * TB - 1 + 2 * HC
                    o = k.enter(i, per)
                    first = i * 2 * HC
                    h_gu_vector(first, 0)
                    h_gu_vector(first + 1, 1)
                    h_d_vector(first, 0)
                    norm_vector(dve, k, "h", i)
                    dve.wait_ge(sem("h_l_ps"), i + 1)
                    k(dve.tensor_copy(h_l[:, 0, :, :], ps[:, 0, 0:2 * TB].rearrange("p (t e) -> p t e", t=TB)))
                    k(dve.tensor_reduce(h_s[:, 0, :], h_l[:, 0, :, :], AX.X, ALU.max))
                    dve.tensor_tensor(h_l[:, 1, :, :], h_l[:, 0, :, :], h_s[:, 0, :].unsqueeze(2).broadcast_to([P, TB, 2]), ALU.subtract)\
                        .then_inc(sem("h_logit"), 1)
                    dve.wait_ge(sem("h_le"), i + 1)
                    ee = h_l[:, 2, :, :]
                    k(dve.tensor_reduce(h_s[:, 1, :], ee, AX.X, ALU.add))
                    k(dve.reciprocal(h_s[:, 1, :], h_s[:, 1, :]))
                    k(dve.tensor_tensor(h_l[:, 3, :, :], ee, h_s[:, 1, :].unsqueeze(2).broadcast_to([P, TB, 2]), ALU.mult))
                    p0, p1 = h_l[:, 3, :, 0], h_l[:, 3, :, 1]
                    k(dve.tensor_tensor(h_l[:, 4, :, 1], p1, p0, ALU.is_gt))
                    k(dve.tensor_scalar(h_l[:, 4, :, 0], h_l[:, 4, :, 1], -1.0, 1.0, ALU.mult, ALU.add))
                    k(dve.tensor_tensor(h_l[:, 5, :, :], h_l[:, 4, :, :], h_l[:, 3, :, :], ALU.mult))
                    k(dve.tensor_scalar(h_l[:, 5, :, :], h_l[:, 5, :, :], tg[:, 7:8], None, ALU.mult))
                    for n in range(2 * TB):
                        e, j = n // TB, n % TB
                        t = dve.tensor_scalar(h_diag[:, e, j * P:(j + 1) * P], ident[:, :], h_l[:, 5, j, e:e + 1], None, ALU.mult)
                        k(t) if n < 2 * TB - 1 else t.then_inc(sem("h_diag"), 1)
                    dve.wait_ge(sem("h_gain_ps"), i + 1)
                    dve.tensor_copy(h_gain[:, :, :], ps[:, 2:4, :]).then_inc(sem("h_gain"), 1)
                    dve.wait_ge(sem("h_gain"), i + 1)
                    for e in range(2):
                        turns = HC // 2 - e
                        plain(dve)
                        with dve.Fori(0, turns) as f:
                            o2 = k.enter(f, 2)
                            n = first + e * HC + 2 * f
                            h_hidden_vector(n, 0, e)
                            h_gu_vector(n + 2, 0)
                            h_d_vector(n + 1, 1)
                            h_hidden_vector(n + 1, 1, e)
                            h_gu_vector(n + 3, 1)
                            h_d_vector(n + 2, 0)
                        k.leave(o2, turns, 2)
                    last = first + 2 * HC - 2
                    h_hidden_vector(last, 0, 1)
                    h_d_vector(last + 1, 1)
                    h_hidden_vector(last + 1, 1, 1)
                    dve.wait_ge(sem("h_y_ps"), i + 1)
                    for j in range(TB):
                        n = i * TB + j
                        dve.tensor_tensor(X[:, n, :], ps[:, 4 + j, :], X[:, n, :], ALU.add).then_inc(sem("h_y_used"), 1)
                    dve.wait_ge(sem("h_y_used"), TB * (i + 1))
                    k.leave(o, B, per)
                end_stage(dve, 7)

        @block.tensor
        def _(pe):
            pe.wait_ge(sem("consts"), 1)
            pe.wait_ge(sem("weights"), READY["a"])
            with pe.Fori(0, B) as i:
                norm_tensor(pe, "a", i)
                mm3(pe, ps[:, 2, :], a_wk_hi[:, :], a_wk_lo[:, :], a_ctx_hi[:, bass.ts(i, S)], a_ctx_lo[:, bass.ts(i, S)],
                    True, True).then_inc(sem("a_kvT_ps"), 1)
                pe.wait_ge(sem("a_kvT"), i + 1)
                for j in range(TB):
                    t = pe.transpose(ps[:, 3, j * P:(j + 1) * P], a_kvT[:, j * P:(j + 1) * P], ident[:, :])
                t.then_inc(sem("a_kv_ps"), 1)
                pe.wait_ge(sem("a_kv"), i + 1)
                for j in range(TB):
                    t = mm3(pe, ps[:, 4, :], a_kv_hi[:, j, :], a_kv_lo[:, j, :], xT_hi[:, j, :], xT_lo[:, j, :], j == 0, j == TB - 1)
                t.then_inc(sem("a_oT_ps"), 1)
                pe.wait_ge(sem("a_oT"), i + 1)
                for j in range(TB):
                    if j >= 2:
                        pe.wait_ge(sem("a_sim_used"), i * TB + j - 1)
                    q = slice(j * P, (j + 1) * P)
                    mm3(pe, ps[:, 5 + j % 2, :], a_oT_hi[:, q], a_oT_lo[:, q], a_kvT_hi[:, :], a_kvT_lo[:, :], True, True)\
                        .then_inc(sem("a_sim_ps"), 1)
            end_stage(pe, 0)
            if stages > 1:
                for w in range(2):
                    pe.wait_ge(sem("b_abs"), w + 1)
                    pe.matmul(ps[:, 2 + w, 0:1], ones[:, :], b_st[:, w:w + 1], start=True, stop=True).then_inc(sem("b_abs_ps"), 1)
                pe.wait_ge(sem("weights"), READY["b"])
                with pe.Fori(0, B) as i:
                    norm_tensor(pe, "b", i)
                    for j in range(TB):
                        for q in range(4):
                            n = (i * TB + j) * 4 + q
                            if j >= 1:
                                pe.wait_ge(sem("b_z_used"), n - 3)
                            for c in range(C):
                                for part in (xT_hi, xT_lo):
                                    t = pe.matmul(ps[:, 4 + q, :], part[:, c, j * P:(j + 1) * P], b_tsyn[:, c, q * BANK:(q + 1) * BANK],
                                                  start=(c == 0 and part is xT_hi), stop=(c == C - 1 and part is xT_lo))
                            t.then_inc(sem("b_z_ps"), 1)
                    def b_turn_tensor(j):
                        n = i * TB + j
                        pe.wait_ge(sem("b_h"), n + 1)
                        if j:
                            pe.wait_ge(sem("b_hT"), 4 * n)
                        for q in range(4):
                            for c in range(4):
                                t = pe.transpose(ps[:, q, c * P:(c + 1) * P], b_z[:, j, (4 * q + c) * P:(4 * q + c + 1) * P], ident[:, :])
                            t.then_inc(sem("b_hT_ps"), 1)

                    b_turn_tensor(0)
                    for j in range(TB):
                        n = i * TB + j
                        if j + 1 < TB:
                            b_turn_tensor(j + 1)
                        pe.wait_ge(sem("b_hT"), 4 * (n + 1))
                        if j >= 2:
                            pe.wait_ge(sem("b_y_used"), n - 1)
                        hi, lo = b_hT[j % 2]
                        for c in range(HC):
                            pe.matmul(ps[:, 4 + j % 2, :], hi[:, c, :], b_tout[:, c, :], start=c == 0, stop=False)
                            t = pe.matmul(ps[:, 4 + j % 2, :], lo[:, c, :], b_tout[:, c, :], start=False, stop=c == HC - 1)
                        t.then_inc(sem("b_y_ps"), 1)
                    pe.wait_ge(sem("b_y_used"), TB * (i + 1))
                end_stage(pe, 1)
            if stages > 2:
                pe.wait_ge(sem("weights"), READY["c"])
                with pe.Fori(0, B) as i:
                    norm_tensor(pe, "c", i)
                    for w in range(2):
                        mm3(pe, ps[:, 2 + w, :], c_w_hi[:, w, :], c_w_lo[:, w, :], c_ctx_hi[:, bass.ts(i, S)],
                            c_ctx_lo[:, bass.ts(i, S)], True, True).then_inc(sem("c_qk_ps"), 1)
                    pe.wait_ge(sem("c_qk"), 2 * (i + 1))
                    for j in range(TB):
                        if j >= 2:
                            pe.wait_ge(sem("c_sim"), i * TB + j - 1)
                        q = slice(j * P, (j + 1) * P)
                        mm3(pe, ps[:, 4 + j % 2, :], c_qk_hi[:, 0, q], c_qk_lo[:, 0, q], c_qk_hi[:, 1, :], c_qk_lo[:, 1, :],
                            True, True).then_inc(sem("c_sim_ps"), 1)
                    pe.wait_ge(sem("c_A"), i + 1)
                    for j in range(TB):
                        if j >= 2:
                            pe.wait_ge(sem("c_AT_used"), i * TB + j - 1)
                        for c in range(TB):
                            t = pe.transpose(ps[:, 6 + j % 2, c * P:(c + 1) * P], c_a[:, c, j * P:(j + 1) * P], ident[:, :])
                        t.then_inc(sem("c_AT_ps"), 1)
                    pe.wait_ge(sem("c_AT_used"), TB * (i + 1))
                end_stage(pe, 2)
            if stages > 3:
                pe.wait_ge(sem("weights"), READY["d"])
                with pe.Fori(0, B) as i:
                    norm_tensor(pe, "d", i)
                    for j in range(TB):
                        if j >= 2:
                            pe.wait_ge(sem("y_used"), i * TB + j - 1)
                        q = slice(j * P, (j + 1) * P)
                        for c in range(C):
                            t = mm3(pe, ps[:, 2 + j % 2, :], xT_hi[:, c, q], xT_lo[:, c, q], d_w_hi[:, c, :], d_w_lo[:, c, :],
                                    c == 0, c == C - 1)
                        t.then_inc(sem("y_ps"), 1)
                    pe.wait_ge(sem("y_used"), TB * (i + 1))
                end_stage(pe, 3)
            if stages > 4:
                def e_qk_tensor(turn, d, h=None):
                    u = d % 2
                    if h is not None:
                        pe.wait_ge(sem("pT"), h * TB + TB - 1)
                    pe.wait_ge(sem(f"e_qkw_in{u}"), 16 * (turn + d // 2 + 1))
                    w = [e_qkw[:, u, q, :] for q in range(2)]
                    for c in range(C):
                        t = mm3(pe, ps[:, 2, :], w[0][:, c * P:(c + 1) * P], w[1][:, c * P:(c + 1) * P], xT_hi[:, c, :], xT_lo[:, c, :],
                                c == 0, c == C - 1)
                    t.then_inc(sem("qk_ps"), 1)
                    if h is not None:
                        pe.wait_ge(sem("pT"), h * TB + TB)
                    t = mm3(pe, ps[:, 3, :], w[0][:, 4 * P:5 * P], w[1][:, 4 * P:5 * P], e_kT_hi[:, :], e_kT_lo[:, :], True, True)
                    t.then_inc(sem("qk_ps"), 1)

                def e_scores_tensor(h, a, u, t_, first=False):
                    r, q = slice(a * E_R, (a + 1) * E_R), slice(t_ * P, (t_ + 1) * P)
                    if t_ >= 2 or not first:
                        pe.wait_ge(sem("exp"), h * TB + t_ - 1)
                    mm3(pe, ps[:, t_ % 2, :], e_qk_hi[r, u, 0, q], e_qk_lo[r, u, 0, q], e_qk_hi[r, u, 1, :], e_qk_lo[r, u, 1, :], True, True)\
                        .then_inc(sem("scores_ps"), 1)

                def e_out_tensor(turn, hh, tiles):
                    u, a = hh // 2, hh % 2
                    if 0 in tiles:
                        pe.wait_ge(sem("head_out"), turn * E_BODY + hh + 1)
                        if a == 0:
                            pe.wait_ge(sem(f"e_g_in{u}"), 16 * (turn + 1))
                    gw = [e_g[:, u, q, a * D:(a + 1) * D] for q in range(2)]
                    for j in tiles:
                        q = slice(j * P, (j + 1) * P)
                        for l, r in ((e_cT_hi, 0), (e_cT_hi, 1), (e_cT_lo, 0)):
                            t = pe.matmul(ps[:, 4 + j, :], l[:, a, q], gw[r], start=False, stop=False, skip_group_check=True)
                    if a == 1 and TB - 1 in tiles:
                        t.then_inc(sem(f"e_g_used{u}"), 1)

                def e_head_tensor(turn, hh, tail=False, first=False):
                    h = turn * E_BODY + hh
                    more = not (tail and hh == E_BODY - 1)
                    if hh % 2 == 1 and more:
                        pe.wait_ge(sem("qk"), turn * E_BODY + 2 * ((hh + 1) // 2 + 1))
                    for what, c in E_STEPS:
                        if what == "scores" and more:
                            if c == 1 and not first:
                                pe.wait_ge(sem("head_out"), h)
                            e_scores_tensor(h + 1, (hh + 1) % 2, (hh + 1) // 2 % 2, c)
                        if what == "turned":
                            if c >= 2:
                                pe.wait_ge(sem("pT"), h * TB + c - 1)
                            for t_ in range(TB):
                                if c == 0:
                                    pe.wait_ge(sem("e_p"), h * TB + t_ + 1)
                                t = pe.transpose(ps[:, 2 + c % 2, t_ * P:(t_ + 1) * P], e_p[:, hh % 2, t_, c * P:(c + 1) * P], ident[:, :])
                            t.then_inc(sem("pT_ps"), 1)
                        if what == "out" and not first:
                            e_out_tensor(turn - (hh == 0), (hh - 1) % E_BODY, c)
                    if hh % 2 == 0 and not (tail and hh == E_BODY - 2):
                        e_qk_tensor(turn, hh // 2 + 1, h)
                    if more:
                        pe.wait_ge(sem("exp"), (h + 2) * TB)
                    for c in range(TB):
                        pe.wait_ge(sem("pT"), h * TB + c + 1)
                        t = mm3(pe, ps[:, 1, :], e_kvr_hi[:, c, :], e_kvr_lo[:, c, :], e_pT_hi[:, c, :], e_pT_lo[:, c, :], c == 0, c == TB - 1)
                    t.then_inc(sem("head_ps"), 1)

                with pe.Fori(0, E_HEADS // 4) as i:
                    for v in range(2):
                        for u in range(2):
                            n = (2 * i + v) * 2 + u
                            if u == 0:
                                pe.wait_ge(sem(f"e_blob_in{v}"), 32 * (i + 1))
                            raw = e_blobs[v][:, u, :]
                            kcq, wqr, wq, wkv, wo = (raw[:, a:b] for a, b in zip(E_CUTS, E_CUTS[1:]))
                            for c in range(3):
                                t = pe.matmul(ps[:, 0, 0:E_R], kcq[:, c * P:(c + 1) * P], wqr[:, c * E_R:(c + 1) * E_R], start=c == 0, stop=c == 2)
                            t.then_inc(sem("e_u_ps"), 1)
                            pe.wait_ge(sem("e_mg"), 2 * n + 1)
                            pe.matmul(ps[:, 2, :], wkv, wo, start=True, stop=True)
                            pe.wait_ge(sem("e_u"), n + 1)
                            for c in range(C):
                                t = pe.matmul(ps[:, 1, c * E_R:(c + 1) * E_R], wq[:, c * P:(c + 1) * P], e_u[:, u, :], start=True, stop=True)
                            t.then_inc(sem("e_mg_ps"), 1)
                        pe.wait_ge(sem("e_mg"), 4 * (2 * i + v + 1) + 1)
                with pe.Fori(0, B) as i:
                    norm_tensor(pe, "e", i)
                    pe.wait_ge(sem("e_kvr"), i + 1)
                    for t_ in range(TB):
                        t = pe.transpose(ps[:, 2, t_ * P:(t_ + 1) * P], e_kvr[:, t_, :], ident[:, :])
                    t.then_inc(sem("e_kT_ps"), 1)
                    pe.wait_ge(sem("e_kT"), i + 1)
                    pe.wait_ge(sem("zeros"), 1)
                    for j in range(TB):
                        pe.matmul(ps[:, 4 + j, :], e_zero[:, 0:P], e_zero[:, :], start=True, stop=False, skip_group_check=True)
                    e_qk_tensor(i * E_TURNS, 0)
                    pe.wait_ge(sem("qk"), i * E_HEADS + 2)
                    for t_ in range(TB):
                        e_scores_tensor(i * E_HEADS, 0, 0, t_, True)
                    e_head_tensor(i * E_TURNS, 0, first=True)
                    plain(pe)
                    with pe.Fori(0, E_TURNS - 1) as g:
                        for hh in (1, 2, 3):
                            e_head_tensor(i * E_TURNS + g, hh)
                        e_head_tensor(i * E_TURNS + g + 1, 0)
                    for hh in (1, 2, 3):
                        e_head_tensor((i + 1) * E_TURNS - 1, hh, True)
                    e_out_tensor((i + 1) * E_TURNS - 1, E_BODY - 1, range(TB))
                    for j in range(TB):
                        t = pe.matmul(ps[:, 4 + j, :], e_zero[:, 0:P], e_zero[:, :], start=False, stop=True, skip_group_check=True)
                    t.then_inc(sem("e_y_ps"), 1)
                    pe.wait_ge(sem("e_y_used"), TB * (i + 1))
                end_stage(pe, 4)
            if stages > 5:
                pe.wait_ge(sem("weights"), READY["f"])
                for c in range(C):
                    t = pe.matmul(ps[:, 5, 0:F_N], ones[:, :], f_q[:, c, :], start=c == 0, stop=c == C - 1)
                t.then_inc(sem("f_const_ps"), 1)
                with pe.Fori(0, B) as i:
                    norm_tensor(pe, "f", i)
                    for j in range(TB):
                        if j >= 2:
                            pe.wait_ge(sem("f_a"), i * TB + j - 1)
                        q = slice(j * P, (j + 1) * P)
                        for c in range(C):
                            t = mm3(pe, ps[:, 2 + j % 2, 0:F_N], xT_hi[:, c, q], xT_lo[:, c, q], f_w_hi[:, c, :], f_w_lo[:, c, :], c == 0, c == C - 1)
                        t.then_inc(sem("f_a_ps"), 1)
                    pe.wait_ge(sem("f_m"), TB * (i + 1))
                    for j in range(TB):
                        t = pe.transpose(ps[0:F_K, 4, j * P:(j + 1) * P], f_m[:, j, :], ident[:, :])
                    t.then_inc(sem("f_mT_ps"), 1)
                    pe.wait_ge(sem("f_mT"), i + 1)
                    for j in range(TB):
                        if j >= 2:
                            pe.wait_ge(sem("y_used"), 1 * TILES + i * TB + j - 1)
                        q = slice(j * P, (j + 1) * P)
                        mm3(pe, ps[:, 6 + j % 2, :], f_mT_hi[:, q], f_mT_lo[:, q], f_d_hi[:, :], f_d_lo[:, :], True, True).then_inc(sem("y_ps"), 1)
                    pe.wait_ge(sem("y_used"), 1 * TILES + TB * (i + 1))
                end_stage(pe, 5)
            if stages > 6:
                pe.wait_ge(sem("weights"), READY["g"])

                def g_scores_tensor(h, hh):
                    r = slice(hh * G_HD, (hh + 1) * G_HD)
                    for t_ in range(TB):
                        pe.wait_ge(sem("exp"), h * TB + t_ - TB + 1)
                        q, w = slice(t_ * P, (t_ + 1) * P), (t_ + 1) * P
                        mm3(pe, ps[:, t_, 0:w], g_qk_hi[r, 0, q], g_qk_lo[r, 0, q], g_qk_hi[r, 1, 0:w], g_qk_lo[r, 1, 0:w], True, False)
                        pe.matmul(ps[:, t_, q], g_ident_r[:, :], g_mask_r[:, :], start=False, stop=True).then_inc(sem("scores_ps"), 1)

                def g_v_tensor(n, g):
                    for t_ in range(TB):
                        q, col = slice(t_ * P, (t_ + 1) * P), bass.ds(g * P + D, P)
                        t = mm3(pe, ps[:, 6, q], g_ctx_hi[:, q], g_ctx_lo[:, q], g_wkv_hi[:, col], g_wkv_lo[:, col], True, True)
                    t.then_inc(sem("g_v_ps"), 1)

                def g_heads_tensor(n, g, tail):
                    for hh in range(4):
                        h = G_HEADS_BEFORE + n * 4 + hh
                        pe.wait_ge(sem("g_diag"), TB * (h + 1 - G_HEADS_BEFORE))
                        for c in range(TB):
                            if hh == 0 and c == 2:
                                pe.wait_ge(sem("g_v"), n + 1)
                            if c == 3:
                                pe.wait_ge(sem("pT"), h * TB + 1)
                            for t_ in range(c, TB):
                                t = pe.matmul(ps[:, 4 + c % 3, t_ * P:(t_ + 1) * P], g_p[:, t_, c * P:(c + 1) * P], g_diag[:, t_, :], start=True, stop=True)
                            t.then_inc(sem("pT_ps"), 1)
                        if hh < 3 or not tail:
                            if hh == 3:
                                pe.wait_ge(sem("qk"), G_HEADS_BEFORE + 2 * (n + 2))
                            g_scores_tensor(h + 1, (hh + 1) % 4)
                        pe.wait_ge(sem("pT"), TB * (h + 1))
                        pe.wait_ge(sem("head_out"), h)
                        if hh == 3 and not tail:
                            g_v_tensor(n + 1, g + 1)
                        for c in range(TB):
                            t = mm3(pe, ps[:, 7, c * P:], g_v_hi[:, c, :], g_v_lo[:, c, :], g_pT_hi[:, c, c * P:], g_pT_lo[:, c, c * P:], c == 0, c == TB - 1)
                        t.then_inc(sem("head_ps"), 1)

                with pe.Fori(0, B) as i:
                    norm_tensor(pe, "g", i)
                    pe.wait_ge(sem("g_ctx_used"), i + 2)
                    for m_ in range(C):
                        q = slice(m_ * P, (m_ + 1) * P)
                        if m_ >= 2:
                            pe.wait_ge(sem("g_q"), i * C + m_ - 1)
                        for c in range(C):
                            t = mm3(pe, ps[:, 2 + m_ % 2, :], g_wq_hi[:, c, q], g_wq_lo[:, c, q], xT_hi[:, c, :], xT_lo[:, c, :], c == 0, c == C - 1)
                        t.then_inc(sem("g_q_ps"), 1)
                        if m_ >= 2:
                            pe.wait_ge(sem("g_k"), i * C + m_ - 1)
                        mm3(pe, ps[:, 4 + m_ % 2, :], g_wkv_hi[:, q], g_wkv_lo[:, q], g_ctx_hi[:, :], g_ctx_lo[:, :], True, True).then_inc(sem("g_k_ps"), 1)
                    g_v_tensor(i * C, 0)
                    pe.wait_ge(sem("g_k"), C * (i + 1))
                    pe.wait_ge(sem("g_q"), C * (i + 1))
                    pe.wait_ge(sem("qk"), G_HEADS_BEFORE + 2 * (i * C + 1))
                    g_scores_tensor(G_HEADS_BEFORE + i * C * 4, 0)
                    plain(pe)
                    with pe.Fori(0, C - 1) as g:
                        g_heads_tensor(i * C + g, g, False)
                    g_heads_tensor(i * C + C - 1, C - 1, True)
                    pe.wait_ge(sem("head_out"), G_HEADS_BEFORE + (i + 1) * C * 4)
                    for j in range(TB):
                        if j >= 2:
                            pe.wait_ge(sem("y_used"), 2 * TILES + i * TB + j - 1)
                        q = slice(j * P, (j + 1) * P)
                        for c in range(C):
                            t = mm3(pe, ps[:, 2 + j % 2, :], xT_hi[:, c, q], xT_lo[:, c, q], g_wo_hi[:, c, :], g_wo_lo[:, c, :], c == 0, c == C - 1)
                        t.then_inc(sem("y_ps"), 1)
                    pe.wait_ge(sem("y_used"), 2 * TILES + TB * (i + 1))
                end_stage(pe, 6)
            if stages > 7:
                pe.wait_ge(sem("weights"), READY["h"])
                pe.wait_ge(sem("zeros"), 2)

                def h_gate_up(n, u):
                    pe.wait_ge(sem("h_gu_used"), n + 3)
                    pe.wait_ge(sem("h_h"), n + 1)
                    for w in range(2):
                        for c in range(C):
                            q = slice(w * D + c * P, w * D + (c + 1) * P)
                            t = mm3(pe, ps[:, 2 * w + u, :], h_w_hi[:, u, q], h_w_lo[:, u, q], xT_hi[:, c, :], xT_lo[:, c, :], c == 0, c == C - 1)
                    t.then_inc(sem("h_gu_ps"), 1)

                def h_down(n, u):
                    pe.wait_ge(sem("h_d_used"), n + 3)
                    pe.wait_ge(sem("h_h_lo"), n + 1)
                    for j in range(TB):
                        q = slice(j * P, (j + 1) * P)
                        for a, b in ((h_h_hi, h_w_hi), (h_h_hi, h_w_lo), (h_h_lo, h_w_hi)):
                            t = pe.matmul(ps[:, 4 + j, :], a[:, u, q], b[:, u, 2 * D:], start=False, stop=False, skip_group_check=True)
                    t.then_inc(sem("h_down"), 1)

                with pe.Fori(0, B) as i:
                    norm_tensor(pe, "h", i)
                    for j in range(TB):
                        q = slice(j * P, (j + 1) * P)
                        for c in range(C):
                            t = mm3(pe, ps[:, 0, 2 * j:2 * j + 2], xT_hi[:, c, q], xT_lo[:, c, q], h_gw_hi[:, c, :], h_gw_lo[:, c, :], c == 0, c == C - 1)
                    t.then_inc(sem("h_l_ps"), 1)
                    pe.wait_ge(sem("h_logit"), i + 1)
                    for j in range(TB):
                        pe.matmul(ps[:, 4 + j, :], h_zero[:, 0:P], h_zero[:, :], start=True, stop=False, skip_group_check=True)
                    pe.wait_ge(sem("h_diag"), i + 1)
                    for e in range(2):
                        t = pe.matmul(ps[:, 2 + e, :], ones[:, :], h_diag[:, e, :], start=True, stop=True)
                    t.then_inc(sem("h_gain_ps"), 1)
                    pe.wait_ge(sem("h_gain"), i + 1)
                    first = i * 2 * HC
                    h_gate_up(first, 0)
                    plain(pe)
                    with pe.Fori(0, HC - 1) as f:
                        n = first + 2 * f
                        h_gate_up(n + 1, 1)
                        h_down(n, 0)
                        h_gate_up(n + 2, 0)
                        h_down(n + 1, 1)
                    last = first + 2 * HC - 2
                    h_gate_up(last + 1, 1)
                    h_down(last, 0)
                    h_down(last + 1, 1)
                    for j in range(TB):
                        t = pe.matmul(ps[:, 4 + j, :], h_zero[:, 0:P], h_zero[:, :], start=False, stop=True, skip_group_check=True)
                    t.then_inc(sem("h_y_ps"), 1)
                    pe.wait_ge(sem("h_y_used"), TB * (i + 1))
                end_stage(pe, 7)


NEG = -1.0e30
HI_BEFORE = {"a": 0, "c": 2, "d": 4, "f": 5, "g": 7, "h": 12}
READY = {stage: n + 1 for n, stage in enumerate("abcdfgh")}
E_HEADS, E_R, E_CQ = 16, 64, 384
E_CUTS = np.cumsum([0, E_CQ, 3 * E_R, D, DC, D]).tolist()
E_RAW = E_CUTS[-1]
E_QKW = C * P + P
E_BODY = 4
E_VECTOR_STEPS = [('scores', 0), ('turned', 0), ('scores', 1), ('turned', 1), ('scores', 2), ('scores', 3), ('turned', 2), ('turned', 3)]
E_STEPS = (("scores", 0), ("turned", 0), ("turned", 1), ("scores", 1), ("out", (0, 1)), ("scores", 2), ("turned", 2),
           ("out", (2,)), ("scores", 3), ("turned", 3), ("out", (3,)))
QK_AHEAD = 3
E_TURNS = E_HEADS // E_BODY
F_N, F_K = 136, 72
G_HD = 32
G_HEADS_BEFORE = B * E_HEADS
G_SCALE = float(1.0 / np.sqrt(np.float32(32)))
H_BLOB = 3 * D
SYN_K = max(1, int(HID * (1.0 - 0.9)))
ROUNDS = 26
SEARCH_STEPS, SEARCH_POOL_STEPS = 6, 5
SIM_K = max(1, int(S * 0.3))
SIM1_SCALE = 1.0 / (math.sqrt(32.0) * 4)


def layout(v):
    f = np.ascontiguousarray

    def cut(a):
        return f(a.reshape(a.shape[0] // P, P, a.shape[1]).transpose(1, 0, 2))

    ctx2 = v["ctx_512"].reshape(B * S, DC)
    return {
        "x": cut(v["x"].reshape(B * S, D)),
        "g_xattn": f(v["g_xattn"]), "g_ffn": f(v["g_ffn"]),
        "ctxT": f(ctx2.T),
        "l0_wkT": f(v["L0_xattn_W_k"].T), "l0_bk": f(v["L0_xattn_b_k"].reshape(DC, 1)),
        "l0_gamma": f(v["L0_xattn_ln_gamma"]), "l0_beta": f(v["L0_xattn_ln_beta"]),
        "wsynT": cut(v["L0_ffn_W_syn"].T).reshape(P, -1), "woutT": cut(v["L0_ffn_W_out"].T).reshape(P, -1),
        "b_syn": f(v["L0_ffn_b_syn"]), "b_out": f(v["L0_ffn_b_out"]),
        "ffn_gamma": f(v["L0_ffn_gamma"]), "ffn_beta": f(v["L0_ffn_beta"]),
        "l1_wqkT": f(np.stack([v["L1_xattn_Wq"].T, v["L1_xattn_Wk"].T], 1)),
        "l1_gamma_raw": f(v["L1_xattn_gamma_raw"].reshape(1)),
        **rope(),
        "ctx": f(ctx2.reshape(B, TB, P, DC).transpose(0, 2, 1, 3)),
        "l2_heads": heads(v), "l2_wkr": f(v["L2_xattn_W_kr"].reshape(8, 2, DC, E_R).transpose(0, 2, 1, 3).reshape(8, DC, P)),
        **select_ffn(v, cut),
        "l3_wqT": cut(v["L3_xattn_Wq"].T), "l3_woT": cut(v["L3_xattn_Wout"].T), "l3_wkvT": f(v["L3_xattn_Wkv_expand"].T),
        "l3_gateT": cut(v["L3_ffn_gate_w"].T), "l3_blob": experts(v),
        "l1_wT": cut(v["L1_ffn_weight"].T), "l1_scale": f(v["L1_ffn_scale_weight"]), "l1_bias": f(v["L1_ffn_bias"]),
    }


def rope():
    inv = (1.0 / np.float32(10000.0) ** (np.arange(0, DC, 2, dtype=np.float32) / np.float32(DC))).astype(np.float32)
    freqs = np.arange(S, dtype=np.float32)[:, None] * inv[None, :]
    sin, cos = (np.repeat(t(freqs).astype(np.float32), 2, axis=-1) for t in (np.sin, np.cos))
    sin = np.concatenate([-sin[:, :DC // 2], sin[:, DC // 2:]], 1)
    return {n: np.ascontiguousarray(t.reshape(TB, P, DC).transpose(1, 0, 2)) for n, t in (("cos", cos), ("sin", sin))}


def heads(v):
    h = E_HEADS
    kcq = v["L2_xattn_w_kc_q"].transpose(0, 2, 1).reshape(h, 3, P, P).transpose(0, 2, 1, 3).reshape(h, P, -1)
    wqr = v["L2_xattn_W_qr"].reshape(h, 3, P, E_R).transpose(0, 2, 1, 3).reshape(h, P, -1)
    wq = v["L2_xattn_Wq"].reshape(h, P, D)
    wkv = v["L2_xattn_w_kc_kv"]
    wo = v["L2_xattn_Wo"].T.reshape(h, P, D)
    a = np.concatenate([kcq, wqr, wq, wkv, wo], 2)
    return np.ascontiguousarray(a.reshape(h // 2, 2, P, -1).transpose(0, 2, 1, 3))


def select_ffn(v, cut):
    sw, up = (v[n].transpose(1, 0, 2) for n in ("L2_ffn_select_weight", "L2_ffn_lora_update"))
    mean, deb = v["L2_ffn_select_mean_diff"].T, v["L2_ffn_debias_w"].T
    w = np.concatenate([sw.reshape(D, 64), up.reshape(D, 64), mean], 1)
    q = np.concatenate([np.repeat(mean, 8, 1), np.repeat(deb, 8, 1), mean], 1)
    d = np.concatenate([v["L2_ffn_lora_degen"].transpose(0, 2, 1).reshape(64, D), v["L2_ffn_bias_w"]], 0)
    return {"l2_fw": cut(w), "l2_fq": cut(q), "l2_fd": np.ascontiguousarray(d),
            "l2_center": v["L2_ffn_imp_center"], "l2_slope": v["L2_ffn_imp_slope"],
            "order": np.arange(8, 0, -1).astype(np.float32)}


def experts(v):
    g, u = (v[n].reshape(2, HC, P, C, P).transpose(0, 1, 4, 3, 2).reshape(2, HC, P, D) for n in ("L3_ffn_w_gate", "L3_ffn_w_up"))
    d = v["L3_ffn_w_down"].transpose(0, 2, 1).reshape(2, HC, P, D)
    return np.ascontiguousarray(np.concatenate([g, u, d], 3)).reshape(2 * HC, P, H_BLOB)


def kernel(**inputs):
    import concourse.bacc as _bacc
    from concourse.bass_utils import run_bass_kernel_spmd as _run

    nc = _bacc.Bacc("TRN2", target_bir_lowering=False, num_devices=1)
    arrays = {f"in_{name}": a for name, a in layout({k: np.asarray(a) for k, a in inputs.items()}).items()}
    args = {name[3:]: nc.dram_tensor(name, a.shape, mybir.dt.from_np(a.dtype), kind="ExternalInput").ap()
            for name, a in arrays.items()}
    out = nc.dram_tensor("out_0", (P, TILES, D), F32, kind="ExternalOutput").ap()
    program(nc, args, out)
    r = _run(nc, [arrays], core_ids=[0])
    return np.ascontiguousarray(r.results[0]["out_0"].transpose(1, 0, 2)).reshape(B, S, D)
```
